# Optimizing a Trainium2 kernel written in Bass

```python
import numpy as np
import jax
import jax.numpy as jnp

def _softmax(x, axis=-1):
    return jax.nn.softmax(x, axis=axis)

def _gelu(x):
    return jax.nn.gelu(x, approximate=True)

def _silu(x):
    return jax.nn.silu(x)

def _sigmoid(x):
    return jax.nn.sigmoid(x)

def _layernorm(x, axis=-1, eps=1e-05):
    m = jnp.mean(x, axis=axis, keepdims=True)
    v = jnp.var(x, axis=axis, keepdims=True)
    return (x - m) / jnp.sqrt(v + eps)

def _scatter_add(tgt, idx, src, axis=0):
    return tgt.at[idx].add(src)

def _segment_sum(src, seg, n):
    return jax.ops.segment_sum(src, seg, n)
kernel_name = 'mk_seq_postln_d1_jaxref_r8_3568e0'

def setup_inputs(seed: int=0):
    np.random.seed(seed)
    _w = jnp.asarray

    def _L0_attn_setup():
        import jax, jax.numpy as jnp
        import numpy as np
        D_MODEL = 128
        N_HEADS = 16
        D_K = D_MODEL // N_HEADS
        MAX_POS = 64
        ATT_SPAN = MAX_POS
        B, T = (4, 128)
        SCALE_FACTOR = 3

        def _heads(y):
            b, t, _ = y.shape
            return y.reshape(b, t, N_HEADS, D_K).transpose(0, 2, 1, 3)
        key = jax.random.key(seed)
        ks = jax.random.split(key, 16)
        init = lambda k, shape: jax.random.normal(k, shape, dtype=jnp.float32) * 0.02
        inp = {'x': jax.random.normal(ks[0], (B, T, D_MODEL), dtype=jnp.float32), 'Wq': init(ks[1], (D_MODEL, D_MODEL)), 'bq': jnp.zeros((D_MODEL,), jnp.float32), 'Wk': init(ks[2], (D_MODEL, D_MODEL)), 'bk': jnp.zeros((D_MODEL,), jnp.float32), 'Wv': init(ks[3], (D_MODEL, D_MODEL)), 'bv': jnp.zeros((D_MODEL,), jnp.float32), 'Wo': init(ks[4], (D_MODEL, D_MODEL)), 'bo': jnp.zeros((D_MODEL,), jnp.float32), 'Wpk': init(ks[5], (D_MODEL, D_MODEL)), 'bpk': jnp.zeros((D_MODEL,), jnp.float32), 'Wpq': init(ks[6], (D_MODEL, D_MODEL)), 'bpq': jnp.zeros((D_MODEL,), jnp.float32), 'rel_emb': init(ks[7], (2 * ATT_SPAN, D_MODEL))}
        return inp
    _L0_attn_in = _L0_attn_setup()

    def _L0_ffn_setup():
        import jax, jax.numpy as jnp
        import numpy as np
        DIM = 128
        HID = 256
        OUT = 128
        NE = 8
        TOPK = 2

        def _xavier(key, shape):
            fan_in, fan_out = (shape[-2], shape[-1])
            lim = jnp.sqrt(6.0 / (fan_in + fan_out))
            return jax.random.uniform(key, shape, jnp.float32, -lim, lim)
        key = jax.random.key(seed)
        ks = jax.random.split(key, 8)
        X = jax.random.normal(ks[0], (4, 128, DIM), jnp.float32)
        W1 = _xavier(ks[1], (NE, DIM, HID))
        W3 = _xavier(ks[2], (NE, DIM, HID))
        W2 = _xavier(ks[3], (NE, HID, OUT))
        b1 = jnp.zeros((NE, HID), jnp.float32)
        b3 = jnp.zeros((NE, HID), jnp.float32)
        b2 = jnp.zeros((NE, OUT), jnp.float32)
        Wg = _xavier(ks[4], (DIM, NE))
        bg = jnp.zeros((NE,), jnp.float32)
        Wf = _xavier(ks[5], (OUT, OUT))
        bf = jnp.zeros((OUT,), jnp.float32)
        return {'X': X, 'W1': W1, 'b1': b1, 'W3': W3, 'b3': b3, 'W2': W2, 'b2': b2, 'Wg': Wg, 'bg': bg, 'Wf': Wf, 'bf': bf}
    _L0_ffn_in = _L0_ffn_setup()
    _d = {'L0_attn_x': _L0_attn_in['x'], 'L0_attn_Wq': _L0_attn_in['Wq'], 'L0_attn_bq': _L0_attn_in['bq'], 'L0_attn_Wk': _L0_attn_in['Wk'], 'L0_attn_bk': _L0_attn_in['bk'], 'L0_attn_Wv': _L0_attn_in['Wv'], 'L0_attn_bv': _L0_attn_in['bv'], 'L0_attn_Wo': _L0_attn_in['Wo'], 'L0_attn_bo': _L0_attn_in['bo'], 'L0_attn_Wpk': _L0_attn_in['Wpk'], 'L0_attn_bpk': _L0_attn_in['bpk'], 'L0_attn_Wpq': _L0_attn_in['Wpq'], 'L0_attn_bpq': _L0_attn_in['bpq'], 'L0_attn_rel_emb': _L0_attn_in['rel_emb'], 'L0_ffn_W1': _L0_ffn_in['W1'], 'L0_ffn_b1': _L0_ffn_in['b1'], 'L0_ffn_W3': _L0_ffn_in['W3'], 'L0_ffn_b3': _L0_ffn_in['b3'], 'L0_ffn_W2': _L0_ffn_in['W2'], 'L0_ffn_b2': _L0_ffn_in['b2'], 'L0_ffn_Wg': _L0_ffn_in['Wg'], 'L0_ffn_bg': _L0_ffn_in['bg'], 'L0_ffn_Wf': _L0_ffn_in['Wf'], 'L0_ffn_bf': _L0_ffn_in['bf']}
    _x0 = _d['L0_attn_x']
    _d['L0_attn_x'] = jax.random.normal(jax.random.fold_in(jax.random.key(seed), 1), (2, 1024, 128), dtype=_x0.dtype)
    del _x0
    return _d

def reference(L0_attn_x, L0_attn_Wq, L0_attn_bq, L0_attn_Wk, L0_attn_bk, L0_attn_Wv, L0_attn_bv, L0_attn_Wo, L0_attn_bo, L0_attn_Wpk, L0_attn_bpk, L0_attn_Wpq, L0_attn_bpq, L0_attn_rel_emb, L0_ffn_W1, L0_ffn_b1, L0_ffn_W3, L0_ffn_b3, L0_ffn_W2, L0_ffn_b2, L0_ffn_Wg, L0_ffn_bg, L0_ffn_Wf, L0_ffn_bf):

    def _L0_attn_ref(x, Wq, bq, Wk, bk, Wv, bv, Wo, bo, Wpk, bpk, Wpq, bpq, rel_emb):
        import jax, jax.numpy as jnp
        import numpy as np
        D_MODEL = 128
        N_HEADS = 16
        D_K = D_MODEL // N_HEADS
        MAX_POS = 64
        ATT_SPAN = MAX_POS
        B, T = (4, 128)
        SCALE_FACTOR = 3

        def _heads(y):
            b, t, _ = y.shape
            return y.reshape(b, t, N_HEADS, D_K).transpose(0, 2, 1, 3)
        b, t, c = x.shape
        scale = 1.0 / jnp.sqrt(jnp.asarray(D_K * SCALE_FACTOR, x.dtype))
        Q = _heads(x @ Wq.T + bq)
        K = _heads(x @ Wk.T + bk)
        V = _heads(x @ Wv.T + bv)
        rel = jnp.arange(t)[None, :] - jnp.arange(t)[:, None]
        rel_pos = jnp.clip(rel + ATT_SPAN, 0, 2 * ATT_SPAN - 1)
        p2c_pos = jnp.clip(-rel + ATT_SPAN, 0, 2 * ATT_SPAN - 1)
        scores = jnp.einsum('bhqd,bhkd->bhqk', Q, K) * scale
        pos_key = (rel_emb @ Wpk.T + bpk).reshape(2 * ATT_SPAN, N_HEADS, D_K)
        c2p = jnp.einsum('bhqd,shd->bhqs', Q, pos_key) * scale
        c2p = jnp.take_along_axis(c2p, rel_pos[None, None, :, :], axis=-1)
        pos_query = (rel_emb @ Wpq.T + bpq).reshape(2 * ATT_SPAN, N_HEADS, D_K)
        p2c = jnp.einsum('bhkd,shd->bhks', K, pos_query) * scale
        p2c = jnp.take_along_axis(p2c, p2c_pos[None, None, :, :], axis=-1)
        p2c = jnp.swapaxes(p2c, -1, -2)
        scores = scores + c2p + p2c
        probs = jax.nn.softmax(scores, axis=-1)
        ctx = jnp.einsum('bhqk,bhkd->bhqd', probs, V)
        ctx = ctx.transpose(0, 2, 1, 3).reshape(b, t, c)
        return ctx @ Wo.T + bo

    def _L0_ffn_ref(X, W1, b1, W3, b3, W2, b2, Wg, bg, Wf, bf):
        import jax, jax.numpy as jnp
        import numpy as np
        DIM = 128
        HID = 256
        OUT = 128
        NE = 8
        TOPK = 2

        def _xavier(key, shape):
            fan_in, fan_out = (shape[-2], shape[-1])
            lim = jnp.sqrt(6.0 / (fan_in + fan_out))
            return jax.random.uniform(key, shape, jnp.float32, -lim, lim)
        gating = jax.nn.softmax(X @ Wg + bg, axis=-1)
        top_k_indices = jnp.argsort(gating, axis=-1)[..., -TOPK:]
        h1 = jnp.einsum('bsd,edh->bseh', X, W1) + b1
        h3 = jnp.einsum('bsd,edh->bseh', X, W3) + b3
        h = jax.nn.silu(h1 * h3)
        expert_outputs = jnp.einsum('bseh,eho->bseo', h, W2) + b2
        topk_out = jnp.take_along_axis(expert_outputs, top_k_indices[..., None], axis=2)
        topk_w = jnp.take_along_axis(gating, top_k_indices, axis=-1)
        mixed = jnp.sum(topk_w[..., None] * topk_out, axis=2)
        return mixed @ Wf + bf
    x = L0_attn_x
    x = _layernorm(x + _L0_attn_ref(x, L0_attn_Wq, L0_attn_bq, L0_attn_Wk, L0_attn_bk, L0_attn_Wv, L0_attn_bv, L0_attn_Wo, L0_attn_bo, L0_attn_Wpk, L0_attn_bpk, L0_attn_Wpq, L0_attn_bpq, L0_attn_rel_emb), axis=-1)
    x = _layernorm(x + _L0_ffn_ref(x, L0_ffn_W1, L0_ffn_b1, L0_ffn_W3, L0_ffn_b3, L0_ffn_W2, L0_ffn_b2, L0_ffn_Wg, L0_ffn_bg, L0_ffn_Wf, L0_ffn_bf), axis=-1)
    return x

_drawn_inputs = setup_inputs


def setup_inputs(seed=0):
    import zlib

    import numpy as np

    out = dict(_drawn_inputs(seed))
    spreads = {'L0_attn_bq': (0.0, 0.8),
     'L0_attn_bk': (0.0, 0.8),
     'L0_attn_bv': (0.0, 0.1),
     'L0_attn_bo': (0.0, 0.1),
     'L0_attn_bpk': (0.0, 0.8),
     'L0_attn_bpq': (0.0, 0.8),
     'L0_ffn_b1': (0.0, 0.273),
     'L0_ffn_b3': (0.0, 0.277),
     'L0_ffn_b2': (0.0, 0.1),
     'L0_ffn_bg': (0.0, 0.1),
     'L0_ffn_bf': (0.0, 0.1)}
    factors = {'L0_attn_Wq': 8.0,
     'L0_attn_Wk': 8.0,
     'L0_attn_Wv': 8.0,
     'L0_attn_Wpk': 8.0,
     'L0_attn_Wpq': 8.0,
     'L0_attn_rel_emb': 8.0}
    for name, (base, spread) in spreads.items():
        noise = np.random.default_rng([zlib.crc32(name.encode()), seed]).standard_normal(out[name].shape)
        drawn = base * np.exp(spread * noise) if base else spread * noise
        out[name] = jnp.asarray(drawn.astype(out[name].dtype))
    for name, factor in factors.items():
        out[name] = (out[name] * factor).astype(out[name].dtype)
    return out
```

```python
import concourse.bass as bass
from concourse import mybir
from contextlib import ExitStack

F32 = mybir.dt.float32
BF16 = mybir.dt.bfloat16
ALU = mybir.AluOpType
ACT = mybir.ActivationFunctionType
AX_X = mybir.AxisListType.X

B, T, D = 2, 1024, 128
H, DK = 16, 8
P = 128
NT = T // P
UNITS = B * H
S = 128
HALF = S // 2
ROWS = 48
NEAR = 3 * P
QH = 512
SCALE = 1.0 / 24.0 ** 0.5
LOW = -3.0e38
NE, HID = 8, 256
EPS = 1e-5
B_L, A_L, B_R, A_R, BASE_ROWS, M_ROW, T_ROWS = 48, 51, 54, 57, 60, 64, 66
Q_ORDER, K_ORDER = (0, 0, 0, 1, 1, 2), (0, 1, 2, 0, 1, 0)
SLOTS_BEFORE, SLOTS_AFTER = 2, 2


def head_mask(nc, pool, mask, sem, done):
    nc.gpsimd.memset(mask[:], 1.0).then_inc(sem, 1)
    pool.wait_ge(sem, done + 1)
    nc.gpsimd.affine_select(out=mask[:], in_=mask[:], compare_op=ALU.is_ge, fill=0.0, base=0,
                            pattern=[[-DK, H]], channel_multiplier=1).then_inc(sem, 1)
    pool.wait_ge(sem, done + 2)
    nc.gpsimd.affine_select(out=mask[:], in_=mask[:], compare_op=ALU.is_ge, fill=0.0, base=DK - 1,
                            pattern=[[DK, H]], channel_multiplier=-1).then_inc(sem, 1)
    pool.wait_ge(sem, done + 3)


def prologue(nc, a, scr, keep):
    ctx = ExitStack()
    with ctx:
        def sb(name, shape, dt=F32):
            return ctx.enter_context(nc.sbuf_tensor(name, shape, dt))

        def sem(name):
            return ctx.enter_context(nc.semaphore(name))

        x_sb = keep["xb"]
        w_sb = sb("w_sb", [P, 6, D])
        rel_sb = sb("rel_sb", [P, D])
        bias = sb("bias", [P, 4])
        bv_row = sb("bv_row", [P, D])
        bo_row = sb("bo_row", [P, D])
        xT = sb("xT", [P, B * T])
        wT = sb("wT", [P, 5, D])
        relT = sb("relT", [P, 2, S])
        turn = sb("turn", [P, S])
        qk = sb("qk", [P, 2, B * T])
        rest = sb("rest", [P, 2, T])
        parts = [sb(f"parts_{n}", [P, 3, B * T], BF16) for n in "qk"]
        pos = sb("pos", [P, 2, S])
        posrel = sb("posrel", [P, 2 * S])
        posrest = sb("posrest", [P, 2 * S])
        posparts = sb("posparts", [P, 3, 2 * S], BF16)
        ends = sb("ends", [P, 2, 2 * H])
        far = sb("far", [4 * H, B * T])
        farparts = sb("farparts", [4 * H, 3, B * T], BF16)
        vall = sb("vall", [P, UNITS, NT, 32])
        zeros = sb("zeros", [P, S])
        hmask = sb("hmask", [P, H])
        ps = [ctx.enter_context(nc.psum_tensor(f"pp{i}", [P, QH], F32)) for i in range(8)]

        x_in, w_in, b_in = sem("x_in"), sem("w_in"), sem("b_in")
        masks, turned = sem("masks"), sem("turned")
        ident_ready, vfill, zero_ready = sem("ident_ready"), sem("vfill"), sem("zero_ready")
        pe_bank, copied = sem("pe_bank"), sem("copied")
        first_part, split, pos_split = sem("first_part"), sem("split"), sem("pos_split")
        ends_set = sem("ends_set")
        tab_out, rows_set = sem("tab_out"), sem("rows_set")
        dve = sem("dve")
        v_done, xb_done = sem("v_done"), sem("xb_done")
        stored = sem("stored")
        block = ctx.enter_context(nc.Block())
        CHUNKS = [(0, 0), (1, 0), (2, 0), (0, 1), (1, 1), (2, 1)]
        zrow = sb("zrow", [6, T], BF16)
        STEPS = 4 + 2 + 4 + 4 + 1 + 4 + 4

        @block.sync
        def _(sp):
            xv = a["L0_attn_x"].rearrange("b (t p) d -> p (b t) d", p=P)
            for g in range(4):
                sp.dma_start(x_sb[:, 4 * g:4 * g + 4, :], xv[:, 4 * g:4 * g + 4, :]).then_inc(x_in, 16)
            for i, n in enumerate(["Wq", "Wk", "Wv", "Wpk", "Wpq", "Wo"]):
                sp.dma_start(w_sb[:, i, :], a["L0_attn_" + n]).then_inc(w_in, 16)
            sp.dma_start(rel_sb[:], a["L0_attn_rel_emb"]).then_inc(w_in, 16)
            n = 0
            sp.wait_ge(zero_ready, 1)
            sp.dma_start(bass.AP(scr["ring"], S, [[2 * S, P], [P * 2 * S, 4 * NT], [1, S]]),
                         zeros[:].unsqueeze(1).to_broadcast([P, 4 * NT, S])).then_inc(stored, 16)
            sp.wait_ge(rows_set, 9)
            for i in range(4):
                sp.dma_start(keep["kst"][i][B_R:B_R + 6, 0, :], zrow[:]).then_inc(stored, 16)
                sp.dma_start(keep["kst"][i][B_L:B_L + 6, 1, :], zrow[:]).then_inc(stored, 16)
                sp.dma_start(keep["qst"][i][BASE_ROWS:M_ROW, :], zrow[0:4, :]).then_inc(stored, 16)
            n += 13
            sp.wait_ge(pos_split, 1)
            for part in range(3):
                sp.dma_start(scr["tab"][part], posparts[:, part, :]).then_inc(tab_out, 16)
            sp.wait_ge(tab_out, 48)
            for which, order in ((0, K_ORDER), (1, Q_ORDER)):
                for r, part in enumerate(order):
                    src = bass.AP(scr["tab"], part * P * 2 * S + which * S, [[2 * S, DK], [DK * 2 * S, H], [1, S]])
                    sp.dma_start(keep["tab"][8 * r:8 * r + 8, which, :, :], src).then_inc(stored, 16)
                    n += 1
            for c, (which, b) in enumerate(CHUNKS):
                sp.wait_ge(split, c + 1)
                if which < 2:
                    for part in range(3):
                        dst = bass.AP(scr[("qparts", "kparts")[which]], (b * H * 3 + part) * DK * T,
                                      [[3 * DK * T, H], [T, DK], [1, T]])
                        sp.dma_start(dst, parts[which][:, part, b * T:(b + 1) * T]).then_inc(stored, 16)
                else:
                    for part in range(3):
                        dst = bass.AP(scr["far"], b * H * 12 * T + part * T, [[3 * T, 4], [12 * T, H], [1, T]])
                        sp.dma_start(dst, farparts[:, part, b * T:(b + 1) * T]).then_inc(stored, 16)
                n += 3
                if c == 2:
                    sp.wait_ge(v_done, 16)
                    sp.wait_ge(vfill, 2)
                    sp.dma_start(scr["v"][:].rearrange("u p n -> p u n"), vall[:].rearrange("p u t n -> p u (t n)"))\
                        .then_inc(stored, 16)
                    n += 1
            sp.wait_ge(stored, 16 * n)

        @block.gpsimd
        def _(pool):
            nc.gpsimd.memset(turn[:], 0.0).then_inc(turned, 1)
            pool.wait_ge(turned, 1)
            nc.gpsimd.affine_select(out=turn[:], in_=turn[:], compare_op=ALU.not_equal, fill=1.0,
                                    base=-S, pattern=[[1, S]], channel_multiplier=1).then_inc(turned, 1)
            pool.wait_ge(turned, 2)
            nc.gpsimd.affine_select(out=turn[:], in_=turn[:], compare_op=ALU.not_equal, fill=1.0,
                                    base=0, pattern=[[1, S]], channel_multiplier=1).then_inc(turned, 1)
            nc.gpsimd.memset(keep["ident"][:], 0.0).then_inc(masks, 1)
            pool.wait_ge(masks, 1)
            nc.gpsimd.affine_select(out=keep["ident"][:], in_=keep["ident"][:], compare_op=ALU.not_equal, fill=1.0,
                                    base=0, pattern=[[-1, P]], channel_multiplier=1).then_inc(ident_ready, 1)
            nc.gpsimd.memset(zeros[:], 0.0).then_inc(zero_ready, 1)
            for i, n in enumerate(["bq", "bk", "bpk", "bpq"]):
                pool.dma_start(bias[:, i:i + 1], a["L0_attn_" + n].unsqueeze(1)).then_inc(b_in, 16)
            pool.dma_start(bv_row[:], a["L0_attn_bv"].partition_broadcast(P)).then_inc(b_in, 16)
            pool.dma_start(bo_row[:], a["L0_attn_bo"].partition_broadcast(P)).then_inc(b_in, 16)
            head_mask(nc, pool, hmask, masks, 1)
            nc.gpsimd.memset(keep["identb"][:], 0.0).then_inc(masks, 1)
            pool.wait_ge(masks, 5)
            nc.gpsimd.affine_select(out=keep["identb"][:], in_=keep["identb"][:], compare_op=ALU.not_equal, fill=1.0,
                                    base=0, pattern=[[-1, P]], channel_multiplier=1).then_inc(masks, 1)
            nc.gpsimd.memset(keep["cmask"][:], 1.0).then_inc(masks, 1)
            pool.wait_ge(masks, 7)
            nc.gpsimd.affine_select(out=keep["cmask"][:], in_=keep["cmask"][:], compare_op=ALU.is_ge, fill=0.0,
                                    base=-S, pattern=[[1, S]], channel_multiplier=1).then_inc(masks, 1)
            nc.gpsimd.memset(keep["pmask"][:], 1.0).then_inc(masks, 1)
            pool.wait_ge(masks, 9)
            for half, bound in ((0, HALF), (1, HALF + S)):
                m = keep["pmask"][half * HALF:(half + 1) * HALF, :]
                nc.gpsimd.affine_select(out=m, in_=m, compare_op=ALU.is_ge, fill=0.0,
                                        base=bound - 1 - half * HALF, pattern=[[-1, S]],
                                        channel_multiplier=-1).then_inc(masks, 1)
                pool.wait_ge(masks, 10 + half)
            nc.gpsimd.memset(zrow[:], 0.0).then_inc(rows_set, 1)
            for i in range(4):
                nc.gpsimd.memset(keep["kst"][i][:], 1.0).then_inc(rows_set, 1)
                nc.gpsimd.memset(keep["qst"][i][:], 1.0).then_inc(rows_set, 1)
            pool.wait_ge(masks, 11)
            pool.wait_ge(b_in, 96)
            pool.wait_ge(x_in, 64)
            pool.wait_ge(copied, 4)
            nc.gpsimd.tensor_tensor(keep["xb"][:], x_sb[:], bo_row[:].unsqueeze(1).to_broadcast([P, B * NT, D]),
                                    ALU.add).then_inc(xb_done, 1)

        @block.tensor
        def _(pe):
            pe.wait_ge(ident_ready, 1)
            step = 0

            def bank():
                if step >= 8:
                    pe.wait_ge(copied, step - 7)
                return ps[step % 8]

            for g in range(4):
                pe.wait_ge(x_in, 64)
                o = bank()
                for i in range(4):
                    last = nc.tensor.transpose(o[:, i * P:(i + 1) * P], x_sb[:, 4 * g + i, :], keep["ident"][:])
                last.then_inc(pe_bank, 1)
                step += 1
            pe.wait_ge(w_in, 7 * 16)
            pe.wait_ge(turned, 3)
            for g in range(2):
                o = bank()
                for i in range(4):
                    src = rel_sb[:] if g == 1 and i >= 2 else w_sb[:, 4 * g + i, :]
                    perm = turn[:] if g == 1 and i == 3 else keep["ident"][:]
                    last = nc.tensor.transpose(o[:, i * P:(i + 1) * P], src, perm)
                last.then_inc(pe_bank, 1)
                step += 1
            for which in range(2):
                for g in range(4):
                    o = bank()
                    if which == 0:
                        pe.wait_ge(copied, 6)
                    nc.tensor.matmul(o[:], wT[:, which, :], xT[:, g * QH:(g + 1) * QH], start=True, stop=True)\
                        .then_inc(pe_bank, 1)
                    step += 1
            o = bank()
            nc.tensor.matmul(o[:, 0:S], wT[:, 3, :], relT[:, 0, :], start=True, stop=True)
            nc.tensor.matmul(o[:, S:2 * S], wT[:, 4, :], relT[:, 1, :], start=True, stop=True).then_inc(pe_bank, 1)
            step += 1
            for g in range(4):
                o = bank()
                for i in range(4):
                    last = nc.tensor.matmul(o[:, i * P:(i + 1) * P], xT[:, (4 * g + i) * P:(4 * g + i + 1) * P],
                                            wT[:, 2, :], start=True, stop=True)
                last.then_inc(pe_bank, 1)
                step += 1
            pe.wait_ge(ends_set, 1)
            for g in range(4):
                o = bank()
                nc.tensor.matmul(o[0:32, :], ends[:, 0, :], qk[:, 0, g * QH:(g + 1) * QH], start=True, stop=True)
                nc.tensor.matmul(o[32:64, :], ends[:, 1, :], qk[:, 1, g * QH:(g + 1) * QH], start=True, stop=True)\
                    .then_inc(pe_bank, 1)
                step += 1
            assert step == STEPS

        def chunk_src(which, b):
            return far[:, b * T:(b + 1) * T] if which == 2 else qk[:, which, b * T:(b + 1) * T]

        def chunk_part(which, b, part):
            return (farparts if which == 2 else parts[which])[:, part, b * T:(b + 1) * T]

        @block.scalar
        def _(act):
            copies = [0]

            def evacuate(step):
                act.wait_ge(pe_bank, step + 1)
                o = ps[step % 8]
                if step < 4:
                    nc.scalar.activation(xT[:, step * QH:(step + 1) * QH], o[:], ACT.Copy).then_inc(copied, 1)
                elif step == 4:
                    nc.scalar.activation(wT[:, 0:4, :].rearrange("p a b -> p (a b)"), o[:], ACT.Copy).then_inc(copied, 1)
                elif step == 5:
                    nc.scalar.activation(wT[:, 4, :], o[:, 0:P], ACT.Copy)
                    nc.scalar.activation(keep["woT"][:], o[:, P:2 * P], ACT.Copy)
                    nc.scalar.activation(relT[:].rearrange("p a s -> p (a s)"), o[:, 2 * P:4 * P], ACT.Copy)\
                        .then_inc(copied, 1)
                elif step < 14:
                    which, g = (step - 6) // 4, (step - 6) % 4
                    nc.scalar.activation(qk[:, which, g * QH:(g + 1) * QH], o[:], ACT.Identity,
                                         bias=bias[:, which:which + 1]).then_inc(copied, 1)
                elif step == 14:
                    nc.scalar.activation(pos[:, 0, :], o[:, 0:S], ACT.Identity, bias=bias[:, 2:3])
                    nc.scalar.activation(pos[:, 1, :], o[:, S:2 * S], ACT.Identity, bias=bias[:, 3:4]).then_inc(copied, 1)
                else:
                    g = step - 19
                    nc.scalar.activation(far[:, g * QH:(g + 1) * QH], o[0:4 * H, :], ACT.Copy).then_inc(copied, 1)
                copies[0] += 1

            def first(which, b):
                act.wait_ge(copied, copies[0])
                nc.scalar.activation(chunk_part(which, b, 0), chunk_src(which, b), ACT.Copy).then_inc(first_part, 1)

            act.wait_ge(b_in, 96)
            for step in range(15):
                evacuate(step)
            first(0, 0)
            first(1, 0)
            for step in range(19, STEPS):
                evacuate(step)
            for which, b in CHUNKS[2:]:
                first(which, b)

        @block.vector
        def _(v):
            count = [0]

            def step(ins):
                count[0] += 1
                ins.then_inc(dve, 1)
                v.wait_ge(dve, count[0])

            def rest_parts(src, rem, out, done):
                step(nc.vector.tensor_tensor(rem, src, out[0], ALU.subtract))
                step(nc.vector.tensor_copy(out[1], rem))
                nc.vector.tensor_tensor(out[2], rem, out[1], ALU.subtract).then_inc(done, 1)

            step(nc.vector.memset(vall[:, :, :, DK:], 0.0))
            nc.vector.memset(vall[:, :, :, DK:DK + 1], 1.0).then_inc(vfill, 2)
            v.wait_ge(copied, 15)
            v.wait_ge(masks, 4)
            nc.vector.tensor_scalar(posrel[:, 0:S], pos[:, 0, :], pos[:, 0, 0:1], None, ALU.subtract)
            nc.vector.tensor_scalar(posrel[:, S:S + 1], pos[:, 1, 1:2], pos[:, 1, 0:1], None, ALU.subtract)
            step(nc.vector.tensor_scalar(posrel[:, S + 1:2 * S], pos[:, 1, 1:S], pos[:, 1, 0:1], None, ALU.subtract))
            for which, col, at in ((0, 0, 0), (0, S - 1, H), (1, 0, 0), (1, 1, H)):
                last = nc.vector.tensor_scalar(ends[:, which, at:at + H], hmask[:], pos[:, which, col:col + 1],
                                               None, ALU.mult)
            last.then_inc(ends_set, 1)
            step(nc.vector.tensor_copy(posparts[:, 0, :], posrel[:]))
            rest_parts(posrel[:], posrest[:], [posparts[:, i, :] for i in range(3)], pos_split)
            for c, (which, b) in enumerate(CHUNKS):
                v.wait_ge(first_part, c + 1)
                if c >= 2:
                    v.wait_ge(split, c - 1)
                src, rem = chunk_src(which, b), rest[:, c % 2, :]
                if which == 2:
                    rem = rest[0:4 * H, c % 2, :]
                rest_parts(src, rem, [chunk_part(which, b, i) for i in range(3)], split)
                if c == 1:
                    v.wait_ge(vfill, 2)
                    for t16 in range(B * NT):
                        g, i = t16 // 4, t16 % 4
                        v.wait_ge(pe_bank, 16 + g)
                        bb, t = t16 // NT, t16 % NT
                        nc.vector.tensor_tensor(vall[:, bb * H:(bb + 1) * H, t, 0:DK],
                                                ps[(15 + g) % 8][:, i * P:(i + 1) * P].rearrange("p (h d) -> p h d", d=DK),
                                                bv_row[:].rearrange("p (h d) -> p h d", d=DK), ALU.add).then_inc(v_done, 1)


def attention(nc, a, scr, keep):
    ctx = ExitStack()
    with ctx:
        def sb(name, shape, dt=F32):
            return ctx.enter_context(nc.sbuf_tensor(name, shape, dt))

        def sem(name):
            return ctx.enter_context(nc.semaphore(name))

        ident, identb = keep["ident"], keep["identb"]
        tab, qst, kst = keep["tab"], keep["qst"], keep["kst"]
        rawq = [sb(f"rawq{i}", [ROWS, T], BF16) for i in range(2)]
        rawk = [sb(f"rawk{i}", [ROWS, T], BF16) for i in range(2)]
        vst = [sb(f"vst{i}", [P, NT, 32]) for i in range(4)]
        raw = [sb(f"raw{i}", [P, 2, NT, S]) for i in range(2)]
        fix = sb("fix", [P, NT, S])
        skew = [sb(f"skew{i}", [P, 2, NT, NEAR]) for i in range(2)]
        near = [sb(f"near{i}", [P, NT, NEAR]) for i in range(2)]
        probs = sb("probs", [P, 16, QH])
        st = sb("st", [P, NT, 3])
        mx = sb("mx", [P, NT])
        mparts = sb("mparts", [P, NT, 2], BF16)
        pvs = [sb(f"pvs{i}", [P, QH]) for i in range(2)]
        m_hat = sb("m_hat", [P, NT])
        csum = sb("csum", [P, NT, DK + 1])
        crec = sb("crec", [P, NT])

        nat = [ctx.enter_context(nc.psum_tensor(f"nat{i}", [P, T], F32)) for i in range(2)]
        tps = [ctx.enter_context(nc.psum_tensor(f"tps{i}", [P, QH], F32)) for i in range(2)]
        pv = ctx.enter_context(nc.psum_tensor("pv", [P, QH], F32))
        misc = ctx.enter_context(nc.psum_tensor("misc", [P, QH], F32))
        misc_b = misc[:].bitcast(BF16)

        zeroed = sem("zeroed")
        raw_in = [sem(f"raw_in{i}") for i in range(2)]
        unit_in = [sem(f"unit_in{i}") for i in range(4)]
        v_in = [sem(f"v_in{i}") for i in range(4)]
        raw_done, raw_copied = sem("raw_done"), sem("raw_copied")
        fix_done, rel_done = sem("fix_done"), sem("rel_done")
        skew_out = [sem(f"skew_out{i}") for i in range(2)]
        skew_in = [sem(f"skew_in{i}") for i in range(2)]
        nat_done, near_done, far_done = sem("nat_done"), sem("near_done"), sem("far_done")
        m_step, m_done, mT_done, m_rows = sem("m_step"), sem("m_done"), sem("mT_done"), sem("m_rows")
        m_hat_done, sub_done = sem("m_hat_done"), sem("sub_done")
        t_done, exp_done = sem("t_done"), sem("exp_done")
        pv_done, pv_copied = sem("pv_done"), sem("pv_copied")
        finT_done, fin_step, fin_done = sem("finT_done"), sem("fin_step"), sem("fin_done")
        LOADS = 3 + 3 + 2 + 2
        RAW_LOADS = 6

        def near_cols(t):
            return max(0, (t - 1) * P), min(T, (t + 2) * P)

        def far_pieces(t):
            lo, hi = near_cols(t)
            return [(i + 1, c0, c1) for i, (c0, c1) in enumerate(((0, lo), (hi, T))) if c1 > c0]

        FAR = [sum(len(far_pieces(t)) for t in range(n)) for n in range(NT + 1)]

        def slots():
            return range(-SLOTS_BEFORE, UNITS + SLOTS_AFTER)

        def unit(u):
            return 0 <= u < UNITS

        def t_tiles(s, t):
            u, i = (s - 1, t - 3) if t >= 3 else (s - 2, t + 5)
            return (u, (2 * i, 2 * i + 1)) if unit(u) else (u, ())

        PV_AT = {5: (1, 0), 7: (1, 1), 1: (2, 2), 3: (2, 3)}
        FIN_AT = 4
        MT_AT = 1
        RAW_AT = {2: 0, 3: 1, 5: 2, 6: 3}
        SUB_AT = {0: (0, 1), 1: (2, 3), 2: (4, 5), 3: (6, 7)}

        block = ctx.enter_context(nc.Block())

        @block.sync
        def _(sp):
            def load_parts(name, u, order, dsts, done):
                if order is Q_ORDER:
                    for r0, reps, part in ((0, 3, 0), (24, 2, 1), (40, 1, 2)):
                        for dst in dsts:
                            sp.dma_start(dst[r0:r0 + 8 * reps], bass.AP(scr[name], (u * 3 + part) * DK * T,
                                                                       [[0, reps], [T, DK], [1, T]])).then_inc(done, 16)
                else:
                    for r0, parts in ((0, 3), (24, 2), (40, 1)):
                        src = [[T, parts * DK], [1, T]]
                        if len(dsts[0].shape) == 3:
                            src = [[T, parts * DK], [0, 2], [1, T]]
                        sp.dma_start(dsts[0][r0:r0 + 8 * parts], bass.AP(scr[name], u * 3 * DK * T, src)).then_inc(done, 16)

            for s in slots():
                u = s + 2
                if unit(u):
                    i = u % 2
                    if u >= 2:
                        sp.wait_ge(raw_done, 4 * (u - 1))
                    load_parts("qparts", u, Q_ORDER, [rawq[i]], raw_in[i])
                    load_parts("kparts", u, K_ORDER, [rawk[i]], raw_in[i])
                u = s + 1
                if unit(u):
                    i = u % 4
                    if u >= 4:
                        sp.wait_ge(t_done, 16 * (u - 3))
                    done = unit_in[i]
                    load_parts("qparts", u, Q_ORDER, [qst[i]], done)
                    load_parts("kparts", u, K_ORDER, [kst[i]], done)
                    for kind, dst in enumerate((qst[i][A_L:A_L + 3], qst[i][A_R:A_R + 3], kst[i][B_L:B_L + 3, 0],
                                                kst[i][B_R:B_R + 3, 1])):
                        sp.dma_start(dst, bass.AP(scr["far"], (u * 4 + kind) * 3 * T, [[T, 3], [1, T]])).then_inc(done, 16)
                u = s + 1
                if unit(u):
                    if u >= 4:
                        sp.wait_ge(pv_done, 4 * (u - 3))
                    sp.dma_start(vst[u % 4][:].rearrange("p t n -> p (t n)"), scr["v"][u]).then_inc(v_in[u % 4], 16)
                    i = u % 2
                    ring = i * 2 * NT * P * 2 * S
                    if u >= 2:
                        sp.wait_ge(skew_in[i], 32 * (u // 2))
                    for kind in range(2):
                        sp.wait_ge(rel_done, 2 * u + kind + 1)
                        dst = bass.AP(scr["ring"], ring + kind * NT * P * 2 * S, [[2 * S, P], [P * 2 * S, NT], [1, S]])
                        sp.dma_start(dst, raw[i][:, kind, :, :]).then_inc(skew_out[kind], 16)
                    if u >= 2:
                        sp.wait_ge(near_done, NT * (u - 1))
                        sp.wait_ge(nat_done, NT * (u - 1))
                    for kind in range(2):
                        sp.wait_ge(skew_out[kind], 16 * (u + 1))
                        src = bass.AP(scr["ring"], ring + kind * NT * P * 2 * S, [[2 * S - 1, P], [P * 2 * S, NT], [1, 2 * S]])
                        sp.dma_start(skew[i][:, kind, :, HALF:HALF + 2 * S], src).then_inc(skew_in[i], 16)

        @block.gpsimd
        def _(pool):
            for i in range(2):
                for c in (0, NEAR - HALF):
                    nc.gpsimd.memset(skew[i][:, :, :, c:c + HALF].rearrange("p a t c -> p (a t) c"), 0.0)\
                        .then_inc(zeroed, 1)
            for s in slots():
                u = s + 2
                if not unit(u):
                    continue
                r = raw[u % 2]
                for kind in range(2):
                    pool.wait_ge(raw_copied, 4 * u + 2 * kind + 2)
                    if 2 * u + kind >= 1:
                        pool.wait_ge(rel_done, 2 * u + kind)
                    mask, col = ((keep["cmask"], S - 1), (keep["pmask"], 0))[kind]
                    for t in range(NT):
                        last = nc.gpsimd.tensor_scalar(fix[:, t, :], mask[:], r[:, kind, t, col:col + 1], 0.0,
                                                       ALU.mult, ALU.add)
                    last.then_inc(fix_done, 1)
                    pool.wait_ge(fix_done, 2 * u + kind + 1)
                    nc.gpsimd.tensor_tensor(r[:, kind], r[:, kind], fix[:], ALU.subtract).then_inc(rel_done, 1)

        @block.tensor
        def _(pe):
            pe.wait_ge(zeroed, 4)

            def natural(u, t):
                n = NT * u + t
                if t == 0:
                    pe.wait_ge(unit_in[u % 4], 16 * LOADS * (u // 4 + 1))
                    pe.wait_ge(skew_in[u % 2], 32 * (u // 2 + 1))
                if n >= 2:
                    pe.wait_ge(near_done, n - 1)
                    pe.wait_ge(far_done, FAR[NT] * ((n - 2) // NT) + FAR[(n - 2) % NT + 1])
                o, q, k = nat[t % 2], qst[u % 4], kst[u % 4]
                pk = skew[u % 2][:, 1]
                edge = min(t * P + HALF, T)
                jobs = []
                for side, c0, c1 in ((0, 0, edge), (1, edge, T)):
                    for b0 in (0, QH):
                        l, r = max(c0, b0), min(c1, b0 + QH)
                        if r > l:
                            jobs.append((b0, l, lambda st_, l=l, r=r, side=side: nc.tensor.matmul(
                                o[:, l:r], q[0:BASE_ROWS, t * P:(t + 1) * P], k[0:BASE_ROWS, side, l:r],
                                start=st_, stop=False, skip_group_check=True)))
                for kt, p1, x0 in ((t - 1, P, 2 * P), (t, P, P), (t + 1, HALF, 0)):
                    if 0 <= kt < NT:
                        c = kt * P
                        jobs.append((c // QH * QH, c, lambda st_, kt=kt, p1=p1, x0=x0, c=c: nc.tensor.matmul(
                            o[:, c:c + p1], pk[0:p1, kt, x0:x0 + P], ident[0:p1, 0:p1],
                            start=False, stop=True, is_transpose=True, skip_group_check=True)))
                seen = set()
                for b0, _, job in jobs:
                    last = job(b0 not in seen)
                    seen.add(b0)
                last.then_inc(nat_done, 1)

            def transposed(u, n):
                kt, half = n // 2, n % 2
                g = 16 * u + n
                if g >= 2:
                    pe.wait_ge(exp_done, g - 1)
                pe.wait_ge(sub_done, NT * u + min(NT, kt + 2))
                o, q, k = tps[n % 2], qst[u % 4], kst[u % 4]
                G = near[u % 2]
                h0, h1 = half * QH, (half + 1) * QH
                first, last = True, None
                n0, n1 = max(h0, (kt - 1) * P), min(h1, kt * P + P + HALF)
                for side, c0, c1 in ((1, h0, min(h1, (kt - 1) * P)), (0, max(h0, kt * P + P + HALF), h1)):
                    if c1 > c0:
                        last = nc.tensor.matmul(o[:, c0 - h0:c1 - h0], k[0:T_ROWS, side, kt * P:(kt + 1) * P],
                                                q[0:T_ROWS, c0:c1], start=first, stop=False, skip_group_check=True)
                        first = False
                if n1 > n0:
                    for qt, p1, x0 in ((kt - 1, P, 2 * P), (kt, P, P), (kt + 1, HALF, 0)):
                        c = qt * P
                        if h0 <= c < h1 and 0 <= qt < NT:
                            last = nc.tensor.matmul(o[:, c - h0:c - h0 + p1], G[0:p1, qt, x0:x0 + P],
                                                    ident[0:p1, 0:p1], start=first, stop=True,
                                                    is_transpose=True, skip_group_check=True)
                            first = False
                last.then_inc(t_done, 1)

            for s in slots():
                for t in range(NT):
                    if unit(s):
                        natural(s, t)
                    if t == MT_AT and unit(s - 1):
                        u = s - 1
                        pe.wait_ge(m_done, u + 1)
                        if unit(s + 1):
                            pe.wait_ge(raw_copied, 4 * (s + 2))
                        elif unit(s - 3):
                            pe.wait_ge(fin_done, s - 2)
                        for i in range(NT):
                            last = nc.tensor.transpose(misc_b[0:2, i * P:(i + 1) * P], mparts[:, i, :], identb[:])
                        last.then_inc(mT_done, 1)
                    u, tiles = t_tiles(s, t)
                    if tiles and tiles[0] == 0:
                        pe.wait_ge(m_rows, u + 1)
                    for n in tiles:
                        transposed(u, n)
                    if t in PV_AT:
                        lag, g = PV_AT[t]
                        u = s - lag
                        if unit(u):
                            pe.wait_ge(exp_done, 16 * u + 4 * g + 4)
                            if g == 0:
                                pe.wait_ge(v_in[u % 4], 16 * (u // 4 + 1))
                            if g == 0 and u >= 1:
                                pe.wait_ge(pv_copied, u)
                            for j in range(4):
                                last = nc.tensor.matmul(pv[32 * j:32 * j + 32, :], vst[u % 4][:, 2 * g + j // 2, :],
                                                        probs[:, 4 * g + j, :], start=g == 0, stop=g == 3)
                            last.then_inc(pv_done, 1)
                    if t == FIN_AT and unit(s - 2):
                        u = s - 2
                        pe.wait_ge(pv_copied, u + 1)
                        if unit(s + 2):
                            pe.wait_ge(raw_copied, 4 * (s + 2) + 2)
                        elif unit(s - 1):
                            pe.wait_ge(m_rows, s)
                        else:
                            pe.wait_ge(fin_done, u)
                        for i in range(4):
                            last = nc.tensor.transpose(misc[:, i * P:(i + 1) * P], pvs[u % 2][:, i * P:(i + 1) * P], ident[:])
                        last.then_inc(finT_done, 1)
                    if t in RAW_AT and unit(s + 2):
                        u, r = s + 2, RAW_AT[t]
                        kind, half = r // 2, r % 2
                        if r == 0:
                            pe.wait_ge(raw_in[u % 2], 16 * RAW_LOADS * (u // 2 + 1))
                        if r == 0 and unit(s - 1):
                            pe.wait_ge(m_rows, s)
                        elif r == 2 and unit(s - 2):
                            pe.wait_ge(fin_done, s - 1)
                        elif 4 * u + r >= 1:
                            pe.wait_ge(raw_copied, 4 * u + r)
                        for i in range(4):
                            tt = 4 * half + i
                            lhs = (rawq, rawk)[kind][u % 2][:, tt * P:(tt + 1) * P]
                            last = nc.tensor.matmul(misc[:, i * P:(i + 1) * P], lhs, tab[:, kind, u % H, :],
                                                    start=True, stop=True)
                        last.then_inc(raw_done, 1)

        @block.scalar
        def _(act):
            for s in slots():
                for t in range(NT):
                    u, tiles = t_tiles(s, t)
                    for n in tiles:
                        g = 16 * u + n
                        act.wait_ge(t_done, g + 1)
                        if u >= 1:
                            act.wait_ge(pv_done, 4 * (u - 1) + n // 4 + 1)
                        nc.scalar.activation(probs[:, n, :], tps[n % 2][:], ACT.Exp, scale=SCALE).then_inc(exp_done, 1)
                    if t == MT_AT and unit(s - 1):
                        u = s - 1
                        act.wait_ge(mT_done, u + 1)
                        nc.scalar.activation(qst[u % 4][M_ROW:T_ROWS, :], misc_b[0:2, :], ACT.Copy).then_inc(m_rows, 1)
                    if t == 3 and unit(s - 2):
                        u = s - 2
                        act.wait_ge(pv_done, 4 * u + 4)
                        if u >= 2:
                            act.wait_ge(finT_done, u - 1)
                        nc.scalar.activation(pvs[u % 2][:], pv[:], ACT.Copy).then_inc(pv_copied, 1)
                    if t in RAW_AT and unit(s + 2):
                        u, r = s + 2, RAW_AT[t]
                        kind, half = r // 2, r % 2
                        act.wait_ge(raw_done, 4 * u + r + 1)
                        if u >= 2:
                            act.wait_ge(skew_out[kind], 16 * (u - 1))
                        nc.scalar.activation(raw[u % 2][:, kind, 4 * half:4 * half + 4, :].rearrange("p t s -> p (t s)"),
                                             misc[:], ACT.Copy).then_inc(raw_copied, 1)

        @block.vector
        def _(v):
            v.wait_ge(zeroed, 4)
            nc.vector.memset(st[:], LOW).then_inc(m_step, 1)
            v.wait_ge(m_step, 1)
            steps = [1]

            def m_wait(ins):
                steps[0] += 1
                ins.then_inc(m_step, 1)
                v.wait_ge(m_step, steps[0])

            def finish(u):
                v.wait_ge(finT_done, u + 1)
                nc.vector.tensor_reduce(csum[:].rearrange("p (h t) n -> p h t n", h=2),
                                        misc[:].rearrange("p (t r h n) -> p h t n r", t=4, r=2, h=2)[:, :, :, 0:DK + 1, :],
                                        AX_X, ALU.add).then_inc(fin_step, 1)
                v.wait_ge(fin_step, 2 * u + 1)
                nc.vector.reciprocal(crec[:], csum[:, :, DK]).then_inc(fin_step, 1)
                v.wait_ge(fin_step, 2 * u + 2)
                b, h = u // H, u % H
                nc.vector.tensor_tensor(keep["ctx"][:, b * NT:(b + 1) * NT, h * DK:(h + 1) * DK],
                                        csum[:, :, 0:DK], crec[:].unsqueeze(2).to_broadcast([P, NT, DK]),
                                        ALU.mult).then_inc(fin_done, 1)

            for s in slots():
                for t in range(NT):
                    if unit(s):
                        u = s
                        v.wait_ge(nat_done, NT * u + t + 1)
                        if t in (0, NT // 2) and u >= 2:
                            v.wait_ge(t_done, 16 * (u - 2) + (10 if t == 0 else 16))
                        if t == 0 and u >= 1:
                            v.wait_ge(m_step, steps[0])
                        lo, hi = near_cols(t)
                        x0 = lo - (t - 1) * P
                        x1 = x0 + hi - lo
                        nc.vector.tensor_tensor_reduce(out=near[u % 2][:, t, x0:x1], in0=nat[t % 2][:, lo:hi],
                                                       in1=skew[u % 2][:, 0, t, x0:x1], scale=1.0, scalar=LOW,
                                                       op0=ALU.add, op1=ALU.max,
                                                       accum_out=st[:, t, 0:1]).then_inc(near_done, 1)
                        for piece, c0, c1 in far_pieces(t):
                            nc.vector.reduce_max(st[:, t, piece:piece + 1], nat[t % 2][:, c0:c1], AX_X)\
                                .then_inc(far_done, 1)
                    if t == FIN_AT and unit(s - 2):
                        finish(s - 2)
                    if t in SUB_AT and unit(s - 1):
                        u = s - 1
                        if t == 0:
                            v.wait_ge(m_hat_done, u + 1)
                        for i in SUB_AT[t]:
                            lo, hi = near_cols(i)
                            g = near[u % 2][:, i, lo - (i - 1) * P:hi - (i - 1) * P]
                            nc.vector.tensor_scalar(g, g, m_hat[:, i:i + 1], None, ALU.add).then_inc(sub_done, 1)
                if unit(s):
                    v.wait_ge(near_done, NT * (s + 1))
                    v.wait_ge(far_done, FAR[NT] * (s + 1))
                    m_wait(nc.vector.tensor_reduce(mx[:], st[:], AX_X, ALU.max))
                    if s >= 1:
                        v.wait_ge(mT_done, s)
                        v.wait_ge(m_done, s)
                    m_wait(nc.vector.tensor_scalar(mparts[:, :, 0], mx[:], -1.0, None, ALU.mult))
                    nc.vector.scalar_tensor_tensor(out=mparts[:, :, 1], in0=mx[:], scalar=-1.0, in1=mparts[:, :, 0],
                                                   op0=ALU.mult, op1=ALU.subtract).then_inc(m_done, 1)
                    v.wait_ge(m_done, s + 1)
                    nc.vector.tensor_tensor(m_hat[:], mparts[:, :, 0], mparts[:, :, 1], ALU.add).then_inc(m_hat_done, 1)


def ffn(nc, a, keep, out):
    ctx = ExitStack()
    NTOK = B * NT
    with ctx:
        def sb(name, shape, dt=F32):
            return ctx.enter_context(nc.sbuf_tensor(name, shape, dt))

        def sem(name):
            return ctx.enter_context(nc.semaphore(name))

        ident = keep["ident"]
        w1 = sb("w1", [P, NE, HID])
        w3 = sb("w3", [P, NE, HID])
        w2 = sb("w2", [P, NE, 2, D])
        b1 = sb("b1", [P, NE, 2])
        b3 = sb("b3", [P, NE, 2])
        wg = sb("wg", [P, NE])
        bg = sb("bg", [P, NE])
        wf = sb("wf", [P, D])
        bf = sb("bf", [P, D])
        b2rep = sb("b2rep", [P, D])
        hmask = sb("hmask2", [P, H])
        later = sb("later", [P, NE, NE])
        b2diag = sb("b2diag", [P, NTOK, D])
        xT = sb("xT2", [P, NTOK, P])
        y = sb("y", [P, NTOK, D])
        x1 = sb("x1", [P, NTOK, D])
        stats = sb("stats", [P, NTOK, 6])
        mv = sb("mv", [P, NTOK, 2])
        rstd = sb("rstd", [P, NTOK])
        logit = sb("logit", [P, NTOK, NE])
        gmax = sb("gmax", [P, NTOK])
        gate = sb("gate", [P, NTOK, NE])
        beats = sb("beats", [P, NTOK, NE, NE])
        ties = sb("ties", [P, NTOK, NE, NE])
        rank = sb("rank", [P, NTOK, NE])
        gw = sb("gw", [P, NTOK, NE])
        gwT = sb("gwT", [P, P])
        acc = sb("acc", [P, NTOK, D])
        h3b = [sb(f"h3b{i}", [P, QH]) for i in range(2)]
        hg = [sb(f"hg{i}", [P, QH]) for i in range(2)]
        hs = [sb(f"hs{i}", [P, QH]) for i in range(4)]
        epsc = sb("epsc", [P, 1])
        ps = [ctx.enter_context(nc.psum_tensor(f"pf{i}", [P, QH], F32)) for i in range(8)]

        wa_in, wb_in, mk = sem("wa_in"), sem("wb_in"), sem("mk")
        ctxT, ctxT_c, proj, yadd = sem("ctxT"), sem("ctxT_c"), sem("proj"), sem("yadd")
        dv, rs, rt, x1_done = sem("dv"), sem("rs"), sem("rt"), sem("x1_done")
        x1T, x1T_c, lg, lgc = sem("x1T"), sem("x1T_c"), sem("lg"), sem("lgc")
        glog, gexp, gwd, gwTd, gwTc, b2d, b2c, bd = (sem(n) for n in ("glog", "gexp", "gwd", "gwTd", "gwTc", "b2d", "b2c", "bd"))
        up, h3c, hgd, hsd, down, mixed = (sem(n) for n in ("up", "h3c", "hgd", "hsd", "down", "mixed"))
        mixT, mixT_c, fin, fy, rs2, rt2, od, stored = (sem(n) for n in ("mixT", "mixT_c", "fin", "fy", "rs2", "rt2", "od", "stored"))
        block = ctx.enter_context(nc.Block())
        units = [(g, e, c) for g in range(4) for e in range(NE) for c in range(2)]

        @block.sync
        def _(sp):
            sp.dma_start(wg[:], a["L0_ffn_Wg"]).then_inc(wa_in, 16)
            sp.dma_start(bg[:], a["L0_ffn_bg"].partition_broadcast(P)).then_inc(wa_in, 16)
            with nc.allow_non_contiguous_dma(reason="bias columns"):
                sp.dma_start(b1[:], a["L0_ffn_b1"].rearrange("e (c p) -> p e c", p=P)).then_inc(wa_in, 16)
                sp.dma_start(b3[:], a["L0_ffn_b3"].rearrange("e (c p) -> p e c", p=P)).then_inc(wa_in, 16)
            for i in range(NTOK):
                sp.dma_start(b2rep[i * NE:(i + 1) * NE, :], a["L0_ffn_b2"]).then_inc(wa_in, 16)
            sp.dma_start(w1[:], a["L0_ffn_W1"].rearrange("e d h -> d e h")).then_inc(wb_in, 16)
            sp.dma_start(w3[:], a["L0_ffn_W3"].rearrange("e d h -> d e h")).then_inc(wb_in, 16)
            sp.dma_start(w2[:], a["L0_ffn_W2"].rearrange("e (c p) o -> p e c o", p=P)).then_inc(wb_in, 16)
            sp.dma_start(wf[:], a["L0_ffn_Wf"]).then_inc(wb_in, 16)
            sp.dma_start(bf[:], a["L0_ffn_bf"].partition_broadcast(P)).then_inc(wb_in, 16)
            ov = out.rearrange("b (t p) d -> p (b t) d", p=P)
            for g in range(4):
                sp.wait_ge(od, 4 * g + 4)
                sp.dma_start(ov[:, 4 * g:4 * g + 4, :], y[:, 4 * g:4 * g + 4, :]).then_inc(stored, 16)
            sp.wait_ge(stored, 64)

        @block.gpsimd
        def _(pool):
            head_mask(nc, pool, hmask, mk, 0)
            nc.gpsimd.memset(later[:], 1.0).then_inc(mk, 1)
            pool.wait_ge(mk, 4)
            nc.gpsimd.affine_select(out=later[:], in_=later[:], compare_op=ALU.is_ge, fill=0.0, base=-1,
                                    pattern=[[-1, NE], [1, NE]], channel_multiplier=0).then_inc(mk, 1)
            nc.gpsimd.memset(epsc[:], EPS).then_inc(mk, 1)
            pool.wait_ge(wa_in, 16 * 20)
            for i in range(NTOK):
                nc.gpsimd.tensor_scalar(b2diag[:, i, :], b2rep[:], hmask[:, i:i + 1], 0.0, ALU.mult, ALU.add)\
                    .then_inc(bd, 1)

        @block.tensor
        def _(pe):
            for g in range(4):
                if g >= 2:
                    pe.wait_ge(ctxT_c, g - 1)
                for i in range(4):
                    last = nc.tensor.transpose(ps[g % 2][:, i * P:(i + 1) * P], keep["ctx"][:, 4 * g + i, :], ident[:])
                last.then_inc(ctxT, 1)
            for g in range(4):
                pe.wait_ge(ctxT_c, g + 1)
                if g >= 2:
                    pe.wait_ge(yadd, 4 * (g - 1))
                for i in range(4):
                    last = nc.tensor.matmul(ps[2 + g % 2][:, i * P:(i + 1) * P], xT[:, 4 * g + i, :], keep["woT"][:],
                                            start=True, stop=True)
                last.then_inc(proj, 1)
            for g in range(4):
                pe.wait_ge(x1_done, 4 * g + 4)
                if g >= 2:
                    pe.wait_ge(x1T_c, g - 1)
                for i in range(4):
                    last = nc.tensor.transpose(ps[g % 2][:, i * P:(i + 1) * P], x1[:, 4 * g + i, :], ident[:])
                last.then_inc(x1T, 1)
            pe.wait_ge(x1T_c, 4)
            pe.wait_ge(wa_in, 16 * 20)
            for i in range(NTOK):
                last = nc.tensor.matmul(ps[4][:, i * NE:(i + 1) * NE], xT[:, i, :], wg[:], start=True, stop=True)
            last.then_inc(lg, 1)
            pe.wait_ge(wb_in, 16 * 5)

            def down_proj(n):
                g, e, _ = units[n]
                pe.wait_ge(hsd, n + 1)
                k = n // 2
                if k < 2:
                    pe.wait_ge(b2c, 4)
                else:
                    pe.wait_ge(mixed, 4 * (k - 1))
                for i in range(4):
                    for c in range(2):
                        last = nc.tensor.matmul(ps[6 + k % 2][:, i * P:(i + 1) * P], hs[(n - 1 + c) % 4][:, i * P:(i + 1) * P],
                                                w2[:, e, c, :], start=c == 0, stop=c == 1)
                last.then_inc(down, 1)

            for n, (g, e, c) in enumerate(units):
                pair = (n % 3) * 2
                if n == 2:
                    pe.wait_ge(lgc, 1)
                if n >= 3:
                    pe.wait_ge(hgd, n - 2)
                for w, bank in ((w3, pair), (w1, pair + 1)):
                    last = nc.tensor.matmul(ps[bank][:], w[:, e, c * P:(c + 1) * P],
                                            xT[:, 4 * g:4 * g + 4, :], start=True, stop=True)
                last.then_inc(up, 1)
                if n == 1:
                    pe.wait_ge(gwd, 1)
                    nc.tensor.transpose(ps[6][:, 0:P], gw[:].rearrange("p t e -> p (t e)"), ident[:]).then_inc(gwTd, 1)
                    pe.wait_ge(gwTc, 1)
                    pe.wait_ge(bd, NTOK)
                    for j in range(4):
                        if j >= 1:
                            pe.wait_ge(b2c, j)
                        nc.tensor.matmul(ps[7][:], gwT[:], b2diag[:, 4 * j:4 * j + 4, :], start=True, stop=True)\
                            .then_inc(b2d, 1)
                if n >= 3 and n % 2 == 1:
                    down_proj(n - 2)
            down_proj(len(units) - 1)
            for g in range(4):
                pe.wait_ge(mixed, 4 * NE * 4)
                if g >= 2:
                    pe.wait_ge(mixT_c, g - 1)
                for i in range(4):
                    last = nc.tensor.transpose(ps[g % 2][:, i * P:(i + 1) * P], acc[:, 4 * g + i, :], ident[:])
                last.then_inc(mixT, 1)
            for g in range(4):
                pe.wait_ge(mixT_c, g + 1)
                if g >= 2:
                    pe.wait_ge(fy, 4 * (g - 1))
                for i in range(4):
                    last = nc.tensor.matmul(ps[2 + g % 2][:, i * P:(i + 1) * P], b2diag[:, 4 * g + i, :], wf[:],
                                            start=True, stop=True)
                last.then_inc(fin, 1)

        @block.scalar
        def _(act):
            for g in range(4):
                act.wait_ge(ctxT, g + 1)
                nc.scalar.activation(xT[:, 4 * g:4 * g + 4, :].rearrange("p t d -> p (t d)"), ps[g % 2][:], ACT.Copy)\
                    .then_inc(ctxT_c, 1)
            act.wait_ge(mk, 6)
            for g in range(4):
                act.wait_ge(rs, g + 1)
                nc.scalar.activation(rstd[:, 4 * g:4 * g + 4], mv[:, 4 * g:4 * g + 4, 1], ACT.Sqrt, bias=epsc[:])\
                    .then_inc(rt, 1)
            act.wait_ge(proj, 4)
            for g in range(4):
                act.wait_ge(x1T, g + 1)
                nc.scalar.activation(xT[:, 4 * g:4 * g + 4, :].rearrange("p t d -> p (t d)"), ps[g % 2][:], ACT.Copy)\
                    .then_inc(x1T_c, 1)
            act.wait_ge(glog, 1)
            nc.scalar.activation(gate[:], logit[:], ACT.Exp).then_inc(gexp, 1)
            act.wait_ge(gwTd, 1)
            nc.scalar.activation(gwT[:], ps[6][:, 0:P], ACT.Copy).then_inc(gwTc, 1)
            for n, (g, e, c) in enumerate(units):
                act.wait_ge(up, n + 1)
                if n >= 2:
                    act.wait_ge(hgd, n - 1)
                nc.scalar.activation(h3b[n % 2][:], ps[(n % 3) * 2][:], ACT.Identity, bias=b3[:, e, c:c + 1])\
                    .then_inc(h3c, 1)
                if n >= 1:
                    m = n - 1
                    act.wait_ge(hgd, m + 1)
                    if m >= 4:
                        act.wait_ge(down, (m - 4) // 2 + 1)
                    nc.scalar.activation(hs[m % 4][:], hg[m % 2][:], ACT.Silu).then_inc(hsd, 1)
            m = len(units) - 1
            act.wait_ge(hgd, m + 1)
            nc.scalar.activation(hs[m % 4][:], hg[m % 2][:], ACT.Silu).then_inc(hsd, 1)
            for g in range(4):
                act.wait_ge(mixT, g + 1)
                nc.scalar.activation(b2diag[:, 4 * g:4 * g + 4, :].rearrange("p t d -> p (t d)"), ps[g % 2][:], ACT.Copy)\
                    .then_inc(mixT_c, 1)
            for g in range(4):
                act.wait_ge(rs2, g + 1)
                nc.scalar.activation(rstd[:, 4 * g:4 * g + 4], mv[:, 4 * g:4 * g + 4, 1], ACT.Sqrt, bias=epsc[:])\
                    .then_inc(rt2, 1)

        @block.vector
        def _(v):
            count = [0]

            def step(ins):
                count[0] += 1
                ins.then_inc(dv, 1)
                v.wait_ge(dv, count[0])

            def norm_stats(g, src, done):
                for i in range(4 * g, 4 * g + 4):
                    last = nc.vector.bn_stats(stats[:, i, :], src[:, i, :])
                step(last)
                for i in range(4 * g, 4 * g + 4):
                    last = nc.vector.bn_aggr(mv[:, i, :], stats[:, i, :])
                last.then_inc(done, 1)

            def norm_apply(g, src, dst, roots, done):
                v.wait_ge(roots, g + 1)
                step(nc.vector.reciprocal(rstd[:, 4 * g:4 * g + 4], rstd[:, 4 * g:4 * g + 4]))
                for i in range(4 * g, 4 * g + 4):
                    nc.vector.tensor_scalar(dst[:, i, :], src[:, i, :], mv[:, i, 0:1], rstd[:, i:i + 1],
                                            ALU.subtract, ALU.mult).then_inc(done, 1)

            for g in range(4):
                v.wait_ge(proj, g + 1)
                for i in range(4):
                    nc.vector.tensor_tensor(y[:, 4 * g + i, :], ps[2 + g % 2][:, i * P:(i + 1) * P],
                                            keep["xb"][:, 4 * g + i, :], ALU.add).then_inc(yadd, 1)
                v.wait_ge(yadd, 4 * g + 4)
                norm_stats(g, y, rs)
                if g >= 1:
                    norm_apply(g - 1, y, x1, rt, x1_done)
            norm_apply(3, y, x1, rt, x1_done)
            v.wait_ge(lg, 1)
            bgb = bg[:].unsqueeze(1).to_broadcast([P, NTOK, NE])
            nc.vector.tensor_tensor(logit[:], ps[4][:, 0:NTOK * NE].rearrange("p (t e) -> p t e", e=NE), bgb, ALU.add)\
                .then_inc(lgc, 1)
            v.wait_ge(lgc, 1)
            step(nc.vector.tensor_reduce(gmax[:], logit[:], AX_X, ALU.max))
            nc.vector.tensor_tensor(logit[:], logit[:], gmax[:].unsqueeze(2).to_broadcast([P, NTOK, NE]),
                                    ALU.subtract).then_inc(glog, 1)
            v.wait_ge(gexp, 1)
            step(nc.vector.tensor_reduce(gmax[:], gate[:], AX_X, ALU.add))
            step(nc.vector.reciprocal(gmax[:], gmax[:]))
            step(nc.vector.tensor_tensor(gate[:], gate[:], gmax[:].unsqueeze(2).to_broadcast([P, NTOK, NE]), ALU.mult))
            v.wait_ge(mk, 6)
            for t0 in range(NTOK):
                mine = gate[:, t0, :].unsqueeze(2).to_broadcast([P, NE, NE])
                other = gate[:, t0, :].unsqueeze(1).to_broadcast([P, NE, NE])
                nc.vector.tensor_tensor(beats[:, t0], other, mine, ALU.is_gt)
                last = nc.vector.tensor_tensor(ties[:, t0], other, mine, ALU.is_equal)
            step(last)
            fl = lambda x: x[:].rearrange("p t e f -> p t (e f)")
            lat = later[:].rearrange("p e f -> p (e f)").unsqueeze(1).to_broadcast([P, NTOK, NE * NE])
            step(nc.vector.tensor_tensor(fl(ties), fl(ties), lat, ALU.mult))
            step(nc.vector.tensor_tensor(fl(beats), fl(beats), fl(ties), ALU.add))
            step(nc.vector.tensor_reduce(rank[:], beats[:], AX_X, ALU.add))
            step(nc.vector.tensor_scalar(rank[:], rank[:], 1.5, None, ALU.is_lt))
            nc.vector.tensor_tensor(gw[:], gate[:], rank[:], ALU.mult).then_inc(gwd, 1)

            def bias_of_experts():
                for j in range(4):
                    v.wait_ge(b2d, j + 1)
                    nc.vector.tensor_copy(acc[:, 4 * j:4 * j + 4, :].rearrange("p t d -> p (t d)"), ps[7][:]).then_inc(b2c, 1)

            def mix(k):
                g, e = k // NE, k % NE
                v.wait_ge(down, k + 1)
                v.wait_ge(mixed, 4 * k) if k else v.wait_ge(b2c, 4)
                for i in range(4):
                    tt = 4 * g + i
                    nc.vector.scalar_tensor_tensor(out=acc[:, tt, :], in0=ps[6 + k % 2][:, i * P:(i + 1) * P],
                                                   scalar=gw[:, tt, e:e + 1], in1=acc[:, tt, :],
                                                   op0=ALU.mult, op1=ALU.add).then_inc(mixed, 1)

            for n, (g, e, c) in enumerate(units):
                if n == 2:
                    bias_of_experts()
                v.wait_ge(h3c, n + 1)
                v.wait_ge(up, n + 1)
                if n >= 2:
                    v.wait_ge(hsd, n - 1)
                nc.vector.scalar_tensor_tensor(out=hg[n % 2][:], in0=ps[(n % 3) * 2 + 1][:], scalar=b1[:, e, c:c + 1],
                                               in1=h3b[n % 2][:], op0=ALU.add, op1=ALU.mult).then_inc(hgd, 1)
                if n >= 5 and n % 2 == 1:
                    mix((n - 5) // 2)
            mix(len(units) // 2 - 2)
            mix(len(units) // 2 - 1)
            v.wait_ge(mixed, 4 * NE * 4)
            for i in range(NTOK):
                last = nc.vector.tensor_tensor(x1[:, i, :], x1[:, i, :], bf[:], ALU.add)
            step(last)
            for g in range(4):
                v.wait_ge(fin, g + 1)
                for i in range(4):
                    nc.vector.tensor_tensor(acc[:, 4 * g + i, :], ps[2 + g % 2][:, i * P:(i + 1) * P],
                                            x1[:, 4 * g + i, :], ALU.add).then_inc(fy, 1)
                v.wait_ge(fy, 4 * g + 4)
                norm_stats(g, acc, rs2)
                if g >= 1:
                    norm_apply(g - 1, acc, y, rt2, od)
            norm_apply(3, acc, y, rt2, od)


NAMES = ["L0_attn_x", "L0_attn_Wq", "L0_attn_bq", "L0_attn_Wk", "L0_attn_bk", "L0_attn_Wv", "L0_attn_bv",
         "L0_attn_Wo", "L0_attn_bo", "L0_attn_Wpk", "L0_attn_bpk", "L0_attn_Wpq", "L0_attn_bpq", "L0_attn_rel_emb",
         "L0_ffn_W1", "L0_ffn_b1", "L0_ffn_W3", "L0_ffn_b3", "L0_ffn_W2", "L0_ffn_b2", "L0_ffn_Wg", "L0_ffn_bg",
         "L0_ffn_Wf", "L0_ffn_bf"]


def build(nc, a, out):
    scr = {
        "qparts": nc.dram_tensor("qparts", [UNITS, 3, DK, T], BF16, kind="Internal"),
        "kparts": nc.dram_tensor("kparts", [UNITS, 3, DK, T], BF16, kind="Internal"),
        "far": nc.dram_tensor("far_rows", [UNITS, 4, 3, T], BF16, kind="Internal"),
        "v": nc.dram_tensor("v_units", [UNITS, P, NT * 32], F32, kind="Internal"),
        "tab": nc.dram_tensor("pos_parts", [3, P, 2 * S], BF16, kind="Internal"),
        "ring": nc.dram_tensor("skew_ring", [2, 2, NT * P, 2 * S], F32, kind="Internal"),
    }
    ctx = ExitStack()
    with ctx:
        keep = {}
        for name, shape, dt in (("ident", [P, P], F32), ("identb", [P, P], BF16), ("cmask", [P, S], F32),
                                ("pmask", [P, S], F32), ("woT", [P, P], F32), ("xb", [P, B * NT, D], F32),
                                ("ctx", [P, B * NT, D], F32)):
            keep[name] = ctx.enter_context(nc.sbuf_tensor(name, shape, dt))
        keep["tab"] = ctx.enter_context(nc.sbuf_tensor("tab", [ROWS, 2, H, S], BF16))
        keep["qst"] = [ctx.enter_context(nc.sbuf_tensor(f"qst{i}", [T_ROWS, T], BF16)) for i in range(4)]
        keep["kst"] = [ctx.enter_context(nc.sbuf_tensor(f"kst{i}", [T_ROWS, 2, T], BF16)) for i in range(4)]
        prologue(nc, a, scr, keep)
        attention(nc, a, scr, keep)
        ffn(nc, a, keep, out)


def kernel(**inputs):
    import numpy as np
    import concourse.bacc as bacc
    from concourse.bass_utils import run_bass_kernel_spmd

    nc = bacc.Bacc("TRN2", target_bir_lowering=False, num_devices=1)
    arrays, args = {}, {}
    for name in NAMES:
        x = np.ascontiguousarray(inputs[name])
        arrays[f"in_{name}"] = x
        args[name] = nc.dram_tensor(f"in_{name}", x.shape, mybir.dt.from_np(x.dtype), kind="ExternalInput").ap()
    out = nc.dram_tensor("out_0_dram", (B, T, D), F32, kind="ExternalOutput").ap()
    build(nc, args, out)
    return run_bass_kernel_spmd(nc, [arrays], core_ids=[0]).results[0]["out_0_dram"]
```

```python
import concourse.bass as bass
from concourse import mybir
from contextlib import ExitStack

F32 = mybir.dt.float32
BF16 = mybir.dt.bfloat16
ALU = mybir.AluOpType
ACT = mybir.ActivationFunctionType
AX_X = mybir.AxisListType.X

B, T, D = 2, 1024, 128
H, DK = 16, 8
P = 128
NT = T // P
UNITS = B * H
S = 128
HALF = S // 2
ROWS = 48
NEAR = 3 * P
QH = 512
SCALE = 1.0 / 24.0 ** 0.5
LOW = -3.0e38
NE, HID = 8, 256
EPS = 1e-5
B_L, A_L, B_R, A_R, BASE_ROWS, M_ROW, T_ROWS = 48, 51, 54, 57, 60, 64, 66
Q_ORDER, K_ORDER = (0, 0, 0, 1, 1, 2), (0, 1, 2, 0, 1, 0)
SLOTS_BEFORE, SLOTS_AFTER = 2, 2


def head_mask(nc, pool, mask, sem, done):
    nc.gpsimd.memset(mask[:], 1.0).then_inc(sem, 1)
    pool.wait_ge(sem, done + 1)
    nc.gpsimd.affine_select(out=mask[:], in_=mask[:], compare_op=ALU.is_ge, fill=0.0, base=0,
                            pattern=[[-DK, H]], channel_multiplier=1).then_inc(sem, 1)
    pool.wait_ge(sem, done + 2)
    nc.gpsimd.affine_select(out=mask[:], in_=mask[:], compare_op=ALU.is_ge, fill=0.0, base=DK - 1,
                            pattern=[[DK, H]], channel_multiplier=-1).then_inc(sem, 1)
    pool.wait_ge(sem, done + 3)


def prologue(nc, a, scr, keep):
    ctx = ExitStack()
    with ctx:
        def sb(name, shape, dt=F32):
            return ctx.enter_context(nc.sbuf_tensor(name, shape, dt))

        def sem(name):
            return ctx.enter_context(nc.semaphore(name))

        x_sb = keep["xb"]
        w_sb = sb("w_sb", [P, 6, D])
        rel_sb = sb("rel_sb", [P, D])
        bias = sb("bias", [P, 4])
        bv_row = sb("bv_row", [P, D])
        bo_row = sb("bo_row", [P, D])
        xT = sb("xT", [P, B * T])
        wT = sb("wT", [P, 5, D])
        relT = sb("relT", [P, 2, S])
        turn = sb("turn", [P, S])
        qk = sb("qk", [P, 2, B * T])
        rest = sb("rest", [P, 2, T])
        parts = [sb(f"parts_{n}", [P, 3, B * T], BF16) for n in "qk"]
        pos = sb("pos", [P, 2, S])
        posrel = sb("posrel", [P, 2 * S])
        posrest = sb("posrest", [P, 2 * S])
        posparts = sb("posparts", [P, 3, 2 * S], BF16)
        ends = sb("ends", [P, 2, 2 * H])
        far = sb("far", [4 * H, B * T])
        farparts = sb("farparts", [4 * H, 3, B * T], BF16)
        vall = sb("vall", [P, UNITS, NT, 32])
        zeros = sb("zeros", [P, S])
        hmask = sb("hmask", [P, H])
        ps = [ctx.enter_context(nc.psum_tensor(f"pp{i}", [P, QH], F32)) for i in range(8)]

        x_in, w_in, b_in = sem("x_in"), sem("w_in"), sem("b_in")
        masks, turned = sem("masks"), sem("turned")
        ident_ready, vfill, zero_ready = sem("ident_ready"), sem("vfill"), sem("zero_ready")
        pe_bank, copied = sem("pe_bank"), sem("copied")
        first_part, split, pos_split = sem("first_part"), sem("split"), sem("pos_split")
        ends_set = sem("ends_set")
        tab_out, rows_set = sem("tab_out"), sem("rows_set")
        dve = sem("dve")
        v_done, xb_done = sem("v_done"), sem("xb_done")
        stored = sem("stored")
        block = ctx.enter_context(nc.Block())
        CHUNKS = [(0, 0), (1, 0), (2, 0), (0, 1), (1, 1), (2, 1)]
        zrow = sb("zrow", [6, T], BF16)
        STEPS = 4 + 2 + 4 + 4 + 1 + 4 + 4

        @block.sync
        def _(sp):
            xv = a["L0_attn_x"].rearrange("b (t p) d -> p (b t) d", p=P)
            for g in range(4):
                sp.dma_start(x_sb[:, 4 * g:4 * g + 4, :], xv[:, 4 * g:4 * g + 4, :]).then_inc(x_in, 16)
            for i, n in enumerate(["Wq", "Wk", "Wv", "Wpk", "Wpq", "Wo"]):
                sp.dma_start(w_sb[:, i, :], a["L0_attn_" + n]).then_inc(w_in, 16)
            sp.dma_start(rel_sb[:], a["L0_attn_rel_emb"]).then_inc(w_in, 16)
            n = 0
            sp.wait_ge(zero_ready, 1)
            sp.dma_start(bass.AP(scr["ring"], S, [[2 * S, P], [P * 2 * S, 4 * NT], [1, S]]),
                         zeros[:].unsqueeze(1).to_broadcast([P, 4 * NT, S])).then_inc(stored, 16)
            sp.wait_ge(rows_set, 9)
            for i in range(4):
                sp.dma_start(keep["kst"][i][B_R:B_R + 6, 0, :], zrow[:]).then_inc(stored, 16)
                sp.dma_start(keep["kst"][i][B_L:B_L + 6, 1, :], zrow[:]).then_inc(stored, 16)
                sp.dma_start(keep["qst"][i][BASE_ROWS:M_ROW, :], zrow[0:4, :]).then_inc(stored, 16)
            n += 13
            sp.wait_ge(pos_split, 1)
            for part in range(3):
                sp.dma_start(scr["tab"][part], posparts[:, part, :]).then_inc(tab_out, 16)
            sp.wait_ge(tab_out, 48)
            for which, order in ((0, K_ORDER), (1, Q_ORDER)):
                for r, part in enumerate(order):
                    src = bass.AP(scr["tab"], part * P * 2 * S + which * S, [[2 * S, DK], [DK * 2 * S, H], [1, S]])
                    sp.dma_start(keep["tab"][8 * r:8 * r + 8, which, :, :], src).then_inc(stored, 16)
                    n += 1
            for c, (which, b) in enumerate(CHUNKS):
                sp.wait_ge(split, c + 1)
                if which < 2:
                    for part in range(3):
                        dst = bass.AP(scr[("qparts", "kparts")[which]], (b * H * 3 + part) * DK * T,
                                      [[3 * DK * T, H], [T, DK], [1, T]])
                        sp.dma_start(dst, parts[which][:, part, b * T:(b + 1) * T]).then_inc(stored, 16)
                else:
                    for part in range(3):
                        dst = bass.AP(scr["far"], b * H * 12 * T + part * T, [[3 * T, 4], [12 * T, H], [1, T]])
                        sp.dma_start(dst, farparts[:, part, b * T:(b + 1) * T]).then_inc(stored, 16)
                n += 3
                if c == 2:
                    sp.wait_ge(v_done, 16)
                    sp.wait_ge(vfill, 2)
                    sp.dma_start(scr["v"][:].rearrange("u p n -> p u n"), vall[:].rearrange("p u t n -> p u (t n)"))\
                        .then_inc(stored, 16)
                    n += 1
            sp.wait_ge(stored, 16 * n)

        @block.gpsimd
        def _(pool):
            nc.gpsimd.memset(turn[:], 0.0).then_inc(turned, 1)
            pool.wait_ge(turned, 1)
            nc.gpsimd.affine_select(out=turn[:], in_=turn[:], compare_op=ALU.not_equal, fill=1.0,
                                    base=-S, pattern=[[1, S]], channel_multiplier=1).then_inc(turned, 1)
            pool.wait_ge(turned, 2)
            nc.gpsimd.affine_select(out=turn[:], in_=turn[:], compare_op=ALU.not_equal, fill=1.0,
                                    base=0, pattern=[[1, S]], channel_multiplier=1).then_inc(turned, 1)
            nc.gpsimd.memset(keep["ident"][:], 0.0).then_inc(masks, 1)
            pool.wait_ge(masks, 1)
            nc.gpsimd.affine_select(out=keep["ident"][:], in_=keep["ident"][:], compare_op=ALU.not_equal, fill=1.0,
                                    base=0, pattern=[[-1, P]], channel_multiplier=1).then_inc(ident_ready, 1)
            nc.gpsimd.memset(zeros[:], 0.0).then_inc(zero_ready, 1)
            for i, n in enumerate(["bq", "bk", "bpk", "bpq"]):
                pool.dma_start(bias[:, i:i + 1], a["L0_attn_" + n].unsqueeze(1)).then_inc(b_in, 16)
            pool.dma_start(bv_row[:], a["L0_attn_bv"].partition_broadcast(P)).then_inc(b_in, 16)
            pool.dma_start(bo_row[:], a["L0_attn_bo"].partition_broadcast(P)).then_inc(b_in, 16)
            head_mask(nc, pool, hmask, masks, 1)
            nc.gpsimd.memset(keep["identb"][:], 0.0).then_inc(masks, 1)
            pool.wait_ge(masks, 5)
            nc.gpsimd.affine_select(out=keep["identb"][:], in_=keep["identb"][:], compare_op=ALU.not_equal, fill=1.0,
                                    base=0, pattern=[[-1, P]], channel_multiplier=1).then_inc(masks, 1)
            nc.gpsimd.memset(keep["cmask"][:], 1.0).then_inc(masks, 1)
            pool.wait_ge(masks, 7)
            nc.gpsimd.affine_select(out=keep["cmask"][:], in_=keep["cmask"][:], compare_op=ALU.is_ge, fill=0.0,
                                    base=-S, pattern=[[1, S]], channel_multiplier=1).then_inc(masks, 1)
            nc.gpsimd.memset(keep["pmask"][:], 1.0).then_inc(masks, 1)
            pool.wait_ge(masks, 9)
            for half, bound in ((0, HALF), (1, HALF + S)):
                m = keep["pmask"][half * HALF:(half + 1) * HALF, :]
                nc.gpsimd.affine_select(out=m, in_=m, compare_op=ALU.is_ge, fill=0.0,
                                        base=bound - 1 - half * HALF, pattern=[[-1, S]],
                                        channel_multiplier=-1).then_inc(masks, 1)
                pool.wait_ge(masks, 10 + half)
            nc.gpsimd.memset(zrow[:], 0.0).then_inc(rows_set, 1)
            for i in range(4):
                nc.gpsimd.memset(keep["kst"][i][:], 1.0).then_inc(rows_set, 1)
                nc.gpsimd.memset(keep["qst"][i][:], 1.0).then_inc(rows_set, 1)
            pool.wait_ge(masks, 11)
            pool.wait_ge(b_in, 96)
            pool.wait_ge(x_in, 64)
            pool.wait_ge(copied, 4)
            nc.gpsimd.tensor_tensor(keep["xb"][:], x_sb[:], bo_row[:].unsqueeze(1).to_broadcast([P, B * NT, D]),
                                    ALU.add).then_inc(xb_done, 1)

        @block.tensor
        def _(pe):
            pe.wait_ge(ident_ready, 1)
            step = 0

            def bank():
                if step >= 8:
                    pe.wait_ge(copied, step - 7)
                return ps[step % 8]

            for g in range(4):
                pe.wait_ge(x_in, 64)
                o = bank()
                for i in range(4):
                    last = nc.tensor.transpose(o[:, i * P:(i + 1) * P], x_sb[:, 4 * g + i, :], keep["ident"][:])
                last.then_inc(pe_bank, 1)
                step += 1
            pe.wait_ge(w_in, 7 * 16)
            pe.wait_ge(turned, 3)
            for g in range(2):
                o = bank()
                for i in range(4):
                    src = rel_sb[:] if g == 1 and i >= 2 else w_sb[:, 4 * g + i, :]
                    perm = turn[:] if g == 1 and i == 3 else keep["ident"][:]
                    last = nc.tensor.transpose(o[:, i * P:(i + 1) * P], src, perm)
                last.then_inc(pe_bank, 1)
                step += 1
            for which in range(2):
                for g in range(4):
                    o = bank()
                    if which == 0:
                        pe.wait_ge(copied, 6)
                    nc.tensor.matmul(o[:], wT[:, which, :], xT[:, g * QH:(g + 1) * QH], start=True, stop=True)\
                        .then_inc(pe_bank, 1)
                    step += 1
            o = bank()
            nc.tensor.matmul(o[:, 0:S], wT[:, 3, :], relT[:, 0, :], start=True, stop=True)
            nc.tensor.matmul(o[:, S:2 * S], wT[:, 4, :], relT[:, 1, :], start=True, stop=True).then_inc(pe_bank, 1)
            step += 1
            for g in range(4):
                o = bank()
                for i in range(4):
                    last = nc.tensor.matmul(o[:, i * P:(i + 1) * P], xT[:, (4 * g + i) * P:(4 * g + i + 1) * P],
                                            wT[:, 2, :], start=True, stop=True)
                last.then_inc(pe_bank, 1)
                step += 1
            pe.wait_ge(ends_set, 1)
            for g in range(4):
                o = bank()
                nc.tensor.matmul(o[0:32, :], ends[:, 0, :], qk[:, 0, g * QH:(g + 1) * QH], start=True, stop=True)
                nc.tensor.matmul(o[32:64, :], ends[:, 1, :], qk[:, 1, g * QH:(g + 1) * QH], start=True, stop=True)\
                    .then_inc(pe_bank, 1)
                step += 1
            assert step == STEPS

        def chunk_src(which, b):
            return far[:, b * T:(b + 1) * T] if which == 2 else qk[:, which, b * T:(b + 1) * T]

        def chunk_part(which, b, part):
            return (farparts if which == 2 else parts[which])[:, part, b * T:(b + 1) * T]

        @block.scalar
        def _(act):
            copies = [0]

            def evacuate(step):
                act.wait_ge(pe_bank, step + 1)
                o = ps[step % 8]
                if step < 4:
                    nc.scalar.activation(xT[:, step * QH:(step + 1) * QH], o[:], ACT.Copy).then_inc(copied, 1)
                elif step == 4:
                    nc.scalar.activation(wT[:, 0:4, :].rearrange("p a b -> p (a b)"), o[:], ACT.Copy).then_inc(copied, 1)
                elif step == 5:
                    nc.scalar.activation(wT[:, 4, :], o[:, 0:P], ACT.Copy)
                    nc.scalar.activation(keep["woT"][:], o[:, P:2 * P], ACT.Copy)
                    nc.scalar.activation(relT[:].rearrange("p a s -> p (a s)"), o[:, 2 * P:4 * P], ACT.Copy)\
                        .then_inc(copied, 1)
                elif step < 14:
                    which, g = (step - 6) // 4, (step - 6) % 4
                    nc.scalar.activation(qk[:, which, g * QH:(g + 1) * QH], o[:], ACT.Identity,
                                         bias=bias[:, which:which + 1]).then_inc(copied, 1)
                elif step == 14:
                    nc.scalar.activation(pos[:, 0, :], o[:, 0:S], ACT.Identity, bias=bias[:, 2:3])
                    nc.scalar.activation(pos[:, 1, :], o[:, S:2 * S], ACT.Identity, bias=bias[:, 3:4]).then_inc(copied, 1)
                else:
                    g = step - 19
                    nc.scalar.activation(far[:, g * QH:(g + 1) * QH], o[0:4 * H, :], ACT.Copy).then_inc(copied, 1)
                copies[0] += 1

            def first(which, b):
                act.wait_ge(copied, copies[0])
                nc.scalar.activation(chunk_part(which, b, 0), chunk_src(which, b), ACT.Copy).then_inc(first_part, 1)

            act.wait_ge(b_in, 96)
            for step in range(15):
                evacuate(step)
            first(0, 0)
            first(1, 0)
            for step in range(19, STEPS):
                evacuate(step)
            for which, b in CHUNKS[2:]:
                first(which, b)

        @block.vector
        def _(v):
            count = [0]

            def step(ins):
                count[0] += 1
                ins.then_inc(dve, 1)
                v.wait_ge(dve, count[0])

            def rest_parts(src, rem, out, done):
                step(nc.vector.tensor_tensor(rem, src, out[0], ALU.subtract))
                step(nc.vector.tensor_copy(out[1], rem))
                nc.vector.tensor_tensor(out[2], rem, out[1], ALU.subtract).then_inc(done, 1)

            step(nc.vector.memset(vall[:, :, :, DK:], 0.0))
            nc.vector.memset(vall[:, :, :, DK:DK + 1], 1.0).then_inc(vfill, 2)
            v.wait_ge(copied, 15)
            v.wait_ge(masks, 4)
            nc.vector.tensor_scalar(posrel[:, 0:S], pos[:, 0, :], pos[:, 0, 0:1], None, ALU.subtract)
            nc.vector.tensor_scalar(posrel[:, S:S + 1], pos[:, 1, 1:2], pos[:, 1, 0:1], None, ALU.subtract)
            step(nc.vector.tensor_scalar(posrel[:, S + 1:2 * S], pos[:, 1, 1:S], pos[:, 1, 0:1], None, ALU.subtract))
            for which, col, at in ((0, 0, 0), (0, S - 1, H), (1, 0, 0), (1, 1, H)):
                last = nc.vector.tensor_scalar(ends[:, which, at:at + H], hmask[:], pos[:, which, col:col + 1],
                                               None, ALU.mult)
            last.then_inc(ends_set, 1)
            step(nc.vector.tensor_copy(posparts[:, 0, :], posrel[:]))
            rest_parts(posrel[:], posrest[:], [posparts[:, i, :] for i in range(3)], pos_split)
            for c, (which, b) in enumerate(CHUNKS):
                v.wait_ge(first_part, c + 1)
                if c >= 2:
                    v.wait_ge(split, c - 1)
                src, rem = chunk_src(which, b), rest[:, c % 2, :]
                if which == 2:
                    rem = rest[0:4 * H, c % 2, :]
                rest_parts(src, rem, [chunk_part(which, b, i) for i in range(3)], split)
                if c == 1:
                    v.wait_ge(vfill, 2)
                    for t16 in range(B * NT):
                        g, i = t16 // 4, t16 % 4
                        v.wait_ge(pe_bank, 16 + g)
                        bb, t = t16 // NT, t16 % NT
                        nc.vector.tensor_tensor(vall[:, bb * H:(bb + 1) * H, t, 0:DK],
                                                ps[(15 + g) % 8][:, i * P:(i + 1) * P].rearrange("p (h d) -> p h d", d=DK),
                                                bv_row[:].rearrange("p (h d) -> p h d", d=DK), ALU.add).then_inc(v_done, 1)


def attention(nc, a, scr, keep):
    ctx = ExitStack()
    with ctx:
        def sb(name, shape, dt=F32):
            return ctx.enter_context(nc.sbuf_tensor(name, shape, dt))

        def sem(name):
            return ctx.enter_context(nc.semaphore(name))

        ident, identb = keep["ident"], keep["identb"]
        tab, qst, kst = keep["tab"], keep["qst"], keep["kst"]
        rawq = [sb(f"rawq{i}", [ROWS, T], BF16) for i in range(2)]
        rawk = [sb(f"rawk{i}", [ROWS, T], BF16) for i in range(2)]
        vst = [sb(f"vst{i}", [P, NT, 32]) for i in range(4)]
        raw = [sb(f"raw{i}", [P, 2, NT, S]) for i in range(2)]
        fix = sb("fix", [P, NT, S])
        skew = [sb(f"skew{i}", [P, 2, NT, NEAR]) for i in range(2)]
        near = [sb(f"near{i}", [P, NT, NEAR]) for i in range(2)]
        probs = sb("probs", [P, 16, QH])
        st = sb("st", [P, NT, 3])
        mx = sb("mx", [P, NT])
        mparts = sb("mparts", [P, NT, 2], BF16)
        pvs = [sb(f"pvs{i}", [P, QH]) for i in range(2)]
        m_hat = sb("m_hat", [P, NT])
        csum = sb("csum", [P, NT, DK + 1])
        crec = sb("crec", [P, NT])

        nat = [ctx.enter_context(nc.psum_tensor(f"nat{i}", [P, T], F32)) for i in range(2)]
        tps = [ctx.enter_context(nc.psum_tensor(f"tps{i}", [P, QH], F32)) for i in range(2)]
        pv = ctx.enter_context(nc.psum_tensor("pv", [P, QH], F32))
        misc = ctx.enter_context(nc.psum_tensor("misc", [P, QH], F32))
        misc_b = misc[:].bitcast(BF16)

        zeroed = sem("zeroed")
        raw_in = [sem(f"raw_in{i}") for i in range(2)]
        unit_in = [sem(f"unit_in{i}") for i in range(4)]
        v_in = [sem(f"v_in{i}") for i in range(4)]
        raw_done, raw_copied = sem("raw_done"), sem("raw_copied")
        fix_done, rel_done = sem("fix_done"), sem("rel_done")
        skew_out = [sem(f"skew_out{i}") for i in range(2)]
        skew_in = [sem(f"skew_in{i}") for i in range(2)]
        nat_done, near_done, far_done = sem("nat_done"), sem("near_done"), sem("far_done")
        m_step, m_done, mT_done, m_rows = sem("m_step"), sem("m_done"), sem("mT_done"), sem("m_rows")
        m_hat_done, sub_done = sem("m_hat_done"), sem("sub_done")
        t_done, exp_done = sem("t_done"), sem("exp_done")
        pv_done, pv_copied = sem("pv_done"), sem("pv_copied")
        finT_done, fin_step, fin_done = sem("finT_done"), sem("fin_step"), sem("fin_done")
        LOADS = 3 + 3 + 2 + 2
        RAW_LOADS = 6

        def near_cols(t):
            return max(0, (t - 1) * P), min(T, (t + 2) * P)

        def far_pieces(t):
            lo, hi = near_cols(t)
            return [(i + 1, c0, c1) for i, (c0, c1) in enumerate(((0, lo), (hi, T))) if c1 > c0]

        FAR = [sum(len(far_pieces(t)) for t in range(n)) for n in range(NT + 1)]

        def slots():
            return range(-SLOTS_BEFORE, UNITS + SLOTS_AFTER)

        def unit(u):
            return 0 <= u < UNITS

        def t_tiles(s, t):
            u, i = (s - 1, t - 3) if t >= 3 else (s - 2, t + 5)
            return (u, (2 * i, 2 * i + 1)) if unit(u) else (u, ())

        PV_AT = {5: (1, 0), 7: (1, 1), 1: (2, 2), 3: (2, 3)}
        FIN_AT = 4
        MT_AT = 1
        RAW_AT = {2: 0, 3: 1, 5: 2, 6: 3}
        SUB_AT = {0: (0, 1), 1: (2, 3), 2: (4, 5), 3: (6, 7)}

        block = ctx.enter_context(nc.Block())

        @block.sync
        def _(sp):
            def load_parts(name, u, order, dsts, done):
                if order is Q_ORDER:
                    for r0, reps, part in ((0, 3, 0), (24, 2, 1), (40, 1, 2)):
                        for dst in dsts:
                            sp.dma_start(dst[r0:r0 + 8 * reps], bass.AP(scr[name], (u * 3 + part) * DK * T,
                                                                       [[0, reps], [T, DK], [1, T]])).then_inc(done, 16)
                else:
                    for r0, parts in ((0, 3), (24, 2), (40, 1)):
                        src = [[T, parts * DK], [1, T]]
                        if len(dsts[0].shape) == 3:
                            src = [[T, parts * DK], [0, 2], [1, T]]
                        sp.dma_start(dsts[0][r0:r0 + 8 * parts], bass.AP(scr[name], u * 3 * DK * T, src)).then_inc(done, 16)

            for s in slots():
                u = s + 2
                if unit(u):
                    i = u % 2
                    if u >= 2:
                        sp.wait_ge(raw_done, 4 * (u - 1))
                    load_parts("qparts", u, Q_ORDER, [rawq[i]], raw_in[i])
                    load_parts("kparts", u, K_ORDER, [rawk[i]], raw_in[i])
                u = s + 1
                if unit(u):
                    i = u % 4
                    if u >= 4:
                        sp.wait_ge(t_done, 16 * (u - 3))
                    done = unit_in[i]
                    load_parts("qparts", u, Q_ORDER, [qst[i]], done)
                    load_parts("kparts", u, K_ORDER, [kst[i]], done)
                    for kind, dst in enumerate((qst[i][A_L:A_L + 3], qst[i][A_R:A_R + 3], kst[i][B_L:B_L + 3, 0],
                                                kst[i][B_R:B_R + 3, 1])):
                        sp.dma_start(dst, bass.AP(scr["far"], (u * 4 + kind) * 3 * T, [[T, 3], [1, T]])).then_inc(done, 16)
                u = s + 1
                if unit(u):
                    if u >= 4:
                        sp.wait_ge(pv_done, 4 * (u - 3))
                    sp.dma_start(vst[u % 4][:].rearrange("p t n -> p (t n)"), scr["v"][u]).then_inc(v_in[u % 4], 16)
                    i = u % 2
                    ring = i * 2 * NT * P * 2 * S
                    if u >= 2:
                        sp.wait_ge(skew_in[i], 32 * (u // 2))
                    for kind in range(2):
                        sp.wait_ge(rel_done, 2 * u + kind + 1)
                        dst = bass.AP(scr["ring"], ring + kind * NT * P * 2 * S, [[2 * S, P], [P * 2 * S, NT], [1, S]])
                        sp.dma_start(dst, raw[i][:, kind, :, :]).then_inc(skew_out[kind], 16)
                    if u >= 2:
                        sp.wait_ge(near_done, NT * (u - 1))
                        sp.wait_ge(nat_done, NT * (u - 1))
                    for kind in range(2):
                        sp.wait_ge(skew_out[kind], 16 * (u + 1))
                        src = bass.AP(scr["ring"], ring + kind * NT * P * 2 * S, [[2 * S - 1, P], [P * 2 * S, NT], [1, 2 * S]])
                        sp.dma_start(skew[i][:, kind, :, HALF:HALF + 2 * S], src).then_inc(skew_in[i], 16)

        @block.gpsimd
        def _(pool):
            for i in range(2):
                for c in (0, NEAR - HALF):
                    nc.gpsimd.memset(skew[i][:, :, :, c:c + HALF].rearrange("p a t c -> p (a t) c"), 0.0)\
                        .then_inc(zeroed, 1)
            for s in slots():
                u = s + 2
                if not unit(u):
                    continue
                r = raw[u % 2]
                for kind in range(2):
                    pool.wait_ge(raw_copied, 4 * u + 2 * kind + 2)
                    if 2 * u + kind >= 1:
                        pool.wait_ge(rel_done, 2 * u + kind)
                    mask, col = ((keep["cmask"], S - 1), (keep["pmask"], 0))[kind]
                    for t in range(NT):
                        last = nc.gpsimd.tensor_scalar(fix[:, t, :], mask[:], r[:, kind, t, col:col + 1], 0.0,
                                                       ALU.mult, ALU.add)
                    last.then_inc(fix_done, 1)
                    pool.wait_ge(fix_done, 2 * u + kind + 1)
                    nc.gpsimd.tensor_tensor(r[:, kind], r[:, kind], fix[:], ALU.subtract).then_inc(rel_done, 1)

        @block.tensor
        def _(pe):
            pe.wait_ge(zeroed, 4)

            def natural(u, t):
                n = NT * u + t
                if t == 0:
                    pe.wait_ge(unit_in[u % 4], 16 * LOADS * (u // 4 + 1))
                    pe.wait_ge(skew_in[u % 2], 32 * (u // 2 + 1))
                if n >= 2:
                    pe.wait_ge(near_done, n - 1)
                    pe.wait_ge(far_done, FAR[NT] * ((n - 2) // NT) + FAR[(n - 2) % NT + 1])
                o, q, k = nat[t % 2], qst[u % 4], kst[u % 4]
                pk = skew[u % 2][:, 1]
                edge = min(t * P + HALF, T)
                jobs = []
                for side, c0, c1 in ((0, 0, edge), (1, edge, T)):
                    for b0 in (0, QH):
                        l, r = max(c0, b0), min(c1, b0 + QH)
                        if r > l:
                            jobs.append((b0, l, lambda st_, l=l, r=r, side=side: nc.tensor.matmul(
                                o[:, l:r], q[0:BASE_ROWS, t * P:(t + 1) * P], k[0:BASE_ROWS, side, l:r],
                                start=st_, stop=False, skip_group_check=True)))
                for kt, p1, x0 in ((t - 1, P, 2 * P), (t, P, P), (t + 1, HALF, 0)):
                    if 0 <= kt < NT:
                        c = kt * P
                        jobs.append((c // QH * QH, c, lambda st_, kt=kt, p1=p1, x0=x0, c=c: nc.tensor.matmul(
                            o[:, c:c + p1], pk[0:p1, kt, x0:x0 + P], ident[0:p1, 0:p1],
                            start=False, stop=True, is_transpose=True, skip_group_check=True)))
                seen = set()
                for b0, _, job in jobs:
                    last = job(b0 not in seen)
                    seen.add(b0)
                last.then_inc(nat_done, 1)

            def transposed(u, n):
                kt, half = n // 2, n % 2
                g = 16 * u + n
                if g >= 2:
                    pe.wait_ge(exp_done, g - 1)
                pe.wait_ge(sub_done, NT * u + min(NT, kt + 2))
                o, q, k = tps[n % 2], qst[u % 4], kst[u % 4]
                G = near[u % 2]
                h0, h1 = half * QH, (half + 1) * QH
                first, last = True, None
                n0, n1 = max(h0, (kt - 1) * P), min(h1, kt * P + P + HALF)
                for side, c0, c1 in ((1, h0, min(h1, (kt - 1) * P)), (0, max(h0, kt * P + P + HALF), h1)):
                    if c1 > c0:
                        last = nc.tensor.matmul(o[:, c0 - h0:c1 - h0], k[0:T_ROWS, side, kt * P:(kt + 1) * P],
                                                q[0:T_ROWS, c0:c1], start=first, stop=False, skip_group_check=True)
                        first = False
                if n1 > n0:
                    for qt, p1, x0 in ((kt - 1, P, 2 * P), (kt, P, P), (kt + 1, HALF, 0)):
                        c = qt * P
                        if h0 <= c < h1 and 0 <= qt < NT:
                            last = nc.tensor.matmul(o[:, c - h0:c - h0 + p1], G[0:p1, qt, x0:x0 + P],
                                                    ident[0:p1, 0:p1], start=first, stop=True,
                                                    is_transpose=True, skip_group_check=True)
                            first = False
                last.then_inc(t_done, 1)

            for s in slots():
                for t in range(NT):
                    if unit(s):
                        natural(s, t)
                    if t == MT_AT and unit(s - 1):
                        u = s - 1
                        pe.wait_ge(m_done, u + 1)
                        if unit(s + 1):
                            pe.wait_ge(raw_copied, 4 * (s + 2))
                        elif unit(s - 3):
                            pe.wait_ge(fin_done, s - 2)
                        for i in range(NT):
                            last = nc.tensor.transpose(misc_b[0:2, i * P:(i + 1) * P], mparts[:, i, :], identb[:])
                        last.then_inc(mT_done, 1)
                    u, tiles = t_tiles(s, t)
                    if tiles and tiles[0] == 0:
                        pe.wait_ge(m_rows, u + 1)
                    for n in tiles:
                        transposed(u, n)
                    if t in PV_AT:
                        lag, g = PV_AT[t]
                        u = s - lag
                        if unit(u):
                            pe.wait_ge(exp_done, 16 * u + 4 * g + 4)
                            if g == 0:
                                pe.wait_ge(v_in[u % 4], 16 * (u // 4 + 1))
                            if g == 0 and u >= 1:
                                pe.wait_ge(pv_copied, u)
                            for j in range(4):
                                last = nc.tensor.matmul(pv[32 * j:32 * j + 32, :], vst[u % 4][:, 2 * g + j // 2, :],
                                                        probs[:, 4 * g + j, :], start=g == 0, stop=g == 3)
                            last.then_inc(pv_done, 1)
                    if t == FIN_AT and unit(s - 2):
                        u = s - 2
                        pe.wait_ge(pv_copied, u + 1)
                        if unit(s + 2):
                            pe.wait_ge(raw_copied, 4 * (s + 2) + 2)
                        elif unit(s - 1):
                            pe.wait_ge(m_rows, s)
                        else:
                            pe.wait_ge(fin_done, u)
                        for i in range(4):
                            last = nc.tensor.transpose(misc[:, i * P:(i + 1) * P], pvs[u % 2][:, i * P:(i + 1) * P], ident[:])
                        last.then_inc(finT_done, 1)
                    if t in RAW_AT and unit(s + 2):
                        u, r = s + 2, RAW_AT[t]
                        kind, half = r // 2, r % 2
                        if r == 0:
                            pe.wait_ge(raw_in[u % 2], 16 * RAW_LOADS * (u // 2 + 1))
                        if r == 0 and unit(s - 1):
                            pe.wait_ge(m_rows, s)
                        elif r == 2 and unit(s - 2):
                            pe.wait_ge(fin_done, s - 1)
                        elif 4 * u + r >= 1:
                            pe.wait_ge(raw_copied, 4 * u + r)
                        for i in range(4):
                            tt = 4 * half + i
                            lhs = (rawq, rawk)[kind][u % 2][:, tt * P:(tt + 1) * P]
                            last = nc.tensor.matmul(misc[:, i * P:(i + 1) * P], lhs, tab[:, kind, u % H, :],
                                                    start=True, stop=True)
                        last.then_inc(raw_done, 1)

        @block.scalar
        def _(act):
            for s in slots():
                for t in range(NT):
                    u, tiles = t_tiles(s, t)
                    for n in tiles:
                        g = 16 * u + n
                        act.wait_ge(t_done, g + 1)
                        if u >= 1:
                            act.wait_ge(pv_done, 4 * (u - 1) + n // 4 + 1)
                        nc.scalar.activation(probs[:, n, :], tps[n % 2][:], ACT.Exp, scale=SCALE).then_inc(exp_done, 1)
                    if t == MT_AT and unit(s - 1):
                        u = s - 1
                        act.wait_ge(mT_done, u + 1)
                        nc.scalar.activation(qst[u % 4][M_ROW:T_ROWS, :], misc_b[0:2, :], ACT.Copy).then_inc(m_rows, 1)
                    if t == 3 and unit(s - 2):
                        u = s - 2
                        act.wait_ge(pv_done, 4 * u + 4)
                        if u >= 2:
                            act.wait_ge(finT_done, u - 1)
                        nc.scalar.activation(pvs[u % 2][:], pv[:], ACT.Copy).then_inc(pv_copied, 1)
                    if t in RAW_AT and unit(s + 2):
                        u, r = s + 2, RAW_AT[t]
                        kind, half = r // 2, r % 2
                        act.wait_ge(raw_done, 4 * u + r + 1)
                        if u >= 2:
                            act.wait_ge(skew_out[kind], 16 * (u - 1))
                        nc.scalar.activation(raw[u % 2][:, kind, 4 * half:4 * half + 4, :].rearrange("p t s -> p (t s)"),
                                             misc[:], ACT.Copy).then_inc(raw_copied, 1)

        @block.vector
        def _(v):
            v.wait_ge(zeroed, 4)
            nc.vector.memset(st[:], LOW).then_inc(m_step, 1)
            v.wait_ge(m_step, 1)
            steps = [1]

            def m_wait(ins):
                steps[0] += 1
                ins.then_inc(m_step, 1)
                v.wait_ge(m_step, steps[0])

            def finish(u):
                v.wait_ge(finT_done, u + 1)
                nc.vector.tensor_reduce(csum[:].rearrange("p (h t) n -> p h t n", h=2),
                                        misc[:].rearrange("p (t r h n) -> p h t n r", t=4, r=2, h=2)[:, :, :, 0:DK + 1, :],
                                        AX_X, ALU.add).then_inc(fin_step, 1)
                v.wait_ge(fin_step, 2 * u + 1)
                nc.vector.reciprocal(crec[:], csum[:, :, DK]).then_inc(fin_step, 1)
                v.wait_ge(fin_step, 2 * u + 2)
                b, h = u // H, u % H
                nc.vector.tensor_tensor(keep["ctx"][:, b * NT:(b + 1) * NT, h * DK:(h + 1) * DK],
                                        csum[:, :, 0:DK], crec[:].unsqueeze(2).to_broadcast([P, NT, DK]),
                                        ALU.mult).then_inc(fin_done, 1)

            for s in slots():
                for t in range(NT):
                    if unit(s):
                        u = s
                        v.wait_ge(nat_done, NT * u + t + 1)
                        if t in (0, NT // 2) and u >= 2:
                            v.wait_ge(t_done, 16 * (u - 2) + (10 if t == 0 else 16))
                        if t == 0 and u >= 1:
                            v.wait_ge(m_step, steps[0])
                        lo, hi = near_cols(t)
                        x0 = lo - (t - 1) * P
                        x1 = x0 + hi - lo
                        nc.vector.tensor_tensor_reduce(out=near[u % 2][:, t, x0:x1], in0=nat[t % 2][:, lo:hi],
                                                       in1=skew[u % 2][:, 0, t, x0:x1], scale=1.0, scalar=LOW,
                                                       op0=ALU.add, op1=ALU.max,
                                                       accum_out=st[:, t, 0:1]).then_inc(near_done, 1)
                        for piece, c0, c1 in far_pieces(t):
                            nc.vector.reduce_max(st[:, t, piece:piece + 1], nat[t % 2][:, c0:c1], AX_X)\
                                .then_inc(far_done, 1)
                    if t == FIN_AT and unit(s - 2):
                        finish(s - 2)
                    if t in SUB_AT and unit(s - 1):
                        u = s - 1
                        if t == 0:
                            v.wait_ge(m_hat_done, u + 1)
                        for i in SUB_AT[t]:
                            lo, hi = near_cols(i)
                            g = near[u % 2][:, i, lo - (i - 1) * P:hi - (i - 1) * P]
                            nc.vector.tensor_scalar(g, g, m_hat[:, i:i + 1], None, ALU.add).then_inc(sub_done, 1)
                if unit(s):
                    v.wait_ge(near_done, NT * (s + 1))
                    v.wait_ge(far_done, FAR[NT] * (s + 1))
                    m_wait(nc.vector.tensor_reduce(mx[:], st[:], AX_X, ALU.max))
                    if s >= 1:
                        v.wait_ge(mT_done, s)
                        v.wait_ge(m_done, s)
                    m_wait(nc.vector.tensor_scalar(mparts[:, :, 0], mx[:], -1.0, None, ALU.mult))
                    nc.vector.scalar_tensor_tensor(out=mparts[:, :, 1], in0=mx[:], scalar=-1.0, in1=mparts[:, :, 0],
                                                   op0=ALU.mult, op1=ALU.subtract).then_inc(m_done, 1)
                    v.wait_ge(m_done, s + 1)
                    nc.vector.tensor_tensor(m_hat[:], mparts[:, :, 0], mparts[:, :, 1], ALU.add).then_inc(m_hat_done, 1)


def ffn(nc, a, keep, out):
    ctx = ExitStack()
    NTOK = B * NT
    GROUPS = NTOK // 4
    GATE = 5
    HS = GATE + 7
    with ctx:
        def sb(name, shape, dt=F32):
            return ctx.enter_context(nc.sbuf_tensor(name, shape, dt))

        def sem(name):
            return ctx.enter_context(nc.semaphore(name))

        ident = keep["ident"]
        w1 = sb("w1", [P, NE, HID])
        w3 = sb("w3", [P, NE, HID])
        w2 = sb("w2", [P, NE, 2, D])
        b1 = sb("b1", [P, NE, 2])
        b3 = sb("b3", [P, NE, 2])
        wg = sb("wg", [P, NE])
        bg = sb("bg", [P, NE])
        wf = sb("wf", [P, D])
        bf = sb("bf", [P, D])
        b2rep = sb("b2rep", [P, D])
        tile_mask = sb("tile_mask", [P, NTOK])
        later = sb("later", [P, NE, NE])
        b2diag = sb("b2diag", [P, NTOK, D])
        xT = sb("xT2", [P, NTOK, P])
        y = sb("y", [P, NTOK, D])
        x1 = sb("x1", [P, NTOK, D])
        stats = sb("stats", [P, NTOK, 6])
        mv = sb("mv", [P, NTOK, 2])
        rstd = sb("rstd", [P, NTOK])
        logit = sb("logit", [P, NTOK, NE])
        gmax = sb("gmax", [P, NTOK])
        gate = sb("gate", [P, NTOK, NE])
        beats = sb("beats", [P, NTOK, NE, NE])
        ties = sb("ties", [P, NTOK, NE, NE])
        rank = sb("rank", [P, NTOK, NE])
        gw = sb("gw", [P, NTOK, NE])
        gwT = sb("gwT", [P, P])
        acc = sb("acc", [P, NTOK, D])
        h3b = [sb(f"h3b{i}", [P, QH]) for i in range(2)]
        hg = [sb(f"hg{i}", [P, QH]) for i in range(2)]
        hs = [sb(f"hs{i}", [P, QH]) for i in range(HS)]
        epsc = sb("epsc", [P, 1])
        warm = sb("warm", [P, 1])
        ps = [ctx.enter_context(nc.psum_tensor(f"pf{i}", [P, QH], F32)) for i in range(8)]
        UP = 5
        DOWN, SIDE = (5, 6), 7

        w_first, w_rest, w_gate, b_up = sem("w_first"), sem("w_rest"), sem("w_gate"), sem("b_up")
        w2_in, b2_in, wf_in, mk = sem("w2_in"), sem("b2_in"), sem("wf_in"), sem("mk")
        ctxT, ctxT_c, proj, yadd = sem("ctxT"), sem("ctxT_c"), sem("proj"), sem("yadd")
        dv, rs, rt, rr, x1_first, x1_rest, x1_bf = (sem(n) for n in ("dv", "rs", "rt", "rr", "x1_first", "x1_rest", "x1_bf"))
        x1T, x1T_c, lg, lgc = sem("x1T"), sem("x1T_c"), sem("lg"), sem("lgc")
        glog, gexp, gwd, gwTd, gwTc, bd = (sem(n) for n in ("glog", "gexp", "gwd", "gwTd", "gwTc", "bd"))
        up, h3c, hgd, hsd, down, mixed = (sem(n) for n in ("up", "h3c", "hgd", "hsd", "down", "mixed"))
        mixT, mixT_c, fin, fy, rs2, rt2, rr2 = (sem(n) for n in ("mixT", "mixT_c", "fin", "fy", "rs2", "rt2", "rr2"))
        od_first, od_last, stored = sem("od_first"), sem("od_last"), sem("stored")
        block = ctx.enter_context(nc.Block())

        units = [(g, e, c) for g in range(GROUPS) for e in range(NE) for c in range(2)]
        PER_GROUP = 2 * NE
        LAST = len(units) - 1
        entries = []
        for g in range(GROUPS):
            for e in (0, 1, 2, 3, 4, NE, 5, 6, 7):
                n = PER_GROUP * g + (12 if e == NE else 2 * e + 3)
                entries.append((g, e, max(n, GATE + 5 + len(entries))))
        ENTRY = {(g, e): k for k, (g, e, _) in enumerate(entries)}
        NEXT_X1 = {0: 1, 1: 2, 3: 3}
        MIXT_AT, FINAL_AT, OUT_AT = PER_GROUP + 4, PER_GROUP + 6, PER_GROUP + 7
        ROOTS_AT = LAST - 7 + 1

        @block.sync
        def _(sp):
            w1v, w3v = (a["L0_ffn_" + n].rearrange("e d h -> d e h") for n in ("W1", "W3"))
            sp.dma_start(w3[:, 0:2], w3v[:, 0:2]).then_inc(w_first, 16)
            sp.dma_start(w1[:, 0:2], w1v[:, 0:2]).then_inc(w_first, 16)
            with nc.allow_non_contiguous_dma(reason="bias columns"):
                sp.dma_start(b3[:], a["L0_ffn_b3"].rearrange("e (c p) -> p e c", p=P)).then_inc(b_up, 16)
                sp.dma_start(b1[:], a["L0_ffn_b1"].rearrange("e (c p) -> p e c", p=P)).then_inc(b_up, 16)
            sp.dma_start(wg[:], a["L0_ffn_Wg"]).then_inc(w_gate, 16)
            sp.dma_start(bg[:], a["L0_ffn_bg"].partition_broadcast(P)).then_inc(w_gate, 16)
            sp.dma_start(w3[:, 2:NE], w3v[:, 2:NE]).then_inc(w_rest, 16)
            sp.dma_start(w1[:, 2:NE], w1v[:, 2:NE]).then_inc(w_rest, 16)
            sp.dma_start(w2[:], a["L0_ffn_W2"].rearrange("e (c p) o -> p e c o", p=P)).then_inc(w2_in, 16)
            for i in range(NTOK):
                sp.dma_start(b2rep[i * NE:(i + 1) * NE, :], a["L0_ffn_b2"]).then_inc(b2_in, 16)
            sp.dma_start(wf[:], a["L0_ffn_Wf"]).then_inc(wf_in, 16)
            sp.dma_start(bf[:], a["L0_ffn_bf"].partition_broadcast(P)).then_inc(wf_in, 16)
            ov = out.rearrange("b (t p) d -> p (b t) d", p=P)
            for g in range(GROUPS):
                if g < GROUPS - 1:
                    sp.wait_ge(od_first, 4 * g + 4)
                else:
                    sp.wait_ge(od_last, 4)
                sp.dma_start(ov[:, 4 * g:4 * g + 4, :], y[:, 4 * g:4 * g + 4, :]).then_inc(stored, 16)
            sp.wait_ge(stored, 16 * GROUPS)

        @block.gpsimd
        def _(pool):
            nc.gpsimd.memset(epsc[:], EPS).then_inc(mk, 1)
            head_mask(nc, pool, tile_mask, mk, 1)
            nc.gpsimd.memset(later[:], 1.0).then_inc(mk, 1)
            pool.wait_ge(mk, 5)
            nc.gpsimd.affine_select(out=later[:], in_=later[:], compare_op=ALU.is_ge, fill=0.0, base=-1,
                                    pattern=[[-1, NE], [1, NE]], channel_multiplier=0).then_inc(mk, 1)
            for g in range(2, GROUPS):
                pool.wait_ge(rr, g + 1)
                for i in range(4 * g, 4 * g + 4):
                    nc.gpsimd.tensor_scalar(x1[:, i, :], y[:, i, :], mv[:, i, 0:1], rstd[:, i:i + 1],
                                            ALU.subtract, ALU.mult).then_inc(x1_rest, 1)
            pool.wait_ge(b2_in, 16 * NTOK)
            for i in range(NTOK):
                nc.gpsimd.tensor_scalar(b2diag[:, i, :], b2rep[:], tile_mask[:, i:i + 1], 0.0, ALU.mult, ALU.add)\
                    .then_inc(bd, 1)
            pool.wait_ge(wf_in, 32)
            pool.wait_ge(x1_first, 8)
            pool.wait_ge(x1T, GROUPS)
            pool.wait_ge(x1_rest, 4 * (GROUPS - 2))
            nc.gpsimd.tensor_tensor(x1[:], x1[:], bf[:].unsqueeze(1).to_broadcast([P, NTOK, D]), ALU.add)\
                .then_inc(x1_bf, 1)
            for g in range(GROUPS - 1):
                pool.wait_ge(rr2, g + 1)
                for i in range(4 * g, 4 * g + 4):
                    nc.gpsimd.tensor_scalar(y[:, i, :], y[:, i, :], mv[:, i, 0:1], rstd[:, i:i + 1],
                                            ALU.subtract, ALU.mult).then_inc(od_first, 1)

        @block.tensor
        def _(pe):
            def transposes(g, src, bank, done):
                for i in range(4):
                    last = nc.tensor.transpose(ps[bank][:, i * P:(i + 1) * P], src[:, 4 * g + i, :], ident[:])
                last.then_inc(done, 1)

            def project(g):
                pe.wait_ge(ctxT_c, g + 1)
                for i in range(4):
                    last = nc.tensor.matmul(ps[4 + g][:, i * P:(i + 1) * P], xT[:, 4 * g + i, :], keep["woT"][:],
                                            start=True, stop=True)
                last.then_inc(proj, 1)

            def down_entry(k):
                g, e, _ = entries[k]
                if k >= 2:
                    pe.wait_ge(mixed, 4 * (k - 1))
                o = ps[DOWN[k % 2]]
                if e == NE:
                    last = nc.tensor.matmul(o[:], gwT[:], b2diag[:, 4 * g:4 * g + 4, :], start=True, stop=True)
                else:
                    m = PER_GROUP * g + 2 * e
                    pe.wait_ge(hsd, m + 2)
                    for i in range(4):
                        for c in range(2):
                            last = nc.tensor.matmul(o[:, i * P:(i + 1) * P], hs[(m + c) % HS][:, i * P:(i + 1) * P],
                                                    w2[:, e, c, :], start=c == 0, stop=c == 1)
                last.then_inc(down, 1)

            def mixed_back(g, bank):
                pe.wait_ge(mixed, 4 * (ENTRY[g, NE - 1] + 1))
                transposes(g, acc, bank, mixT)

            def final(g, bank):
                pe.wait_ge(mixT_c, g + 1)
                for i in range(4):
                    last = nc.tensor.matmul(ps[bank][:, i * P:(i + 1) * P], xT[:, 4 * g + i, :], wf[:],
                                            start=True, stop=True)
                last.then_inc(fin, 1)

            transposes(0, keep["ctx"], 0, ctxT)
            transposes(1, keep["ctx"], 1, ctxT)
            project(0)
            transposes(2, keep["ctx"], 2, ctxT)
            project(1)
            transposes(3, keep["ctx"], 3, ctxT)
            project(2)
            project(3)
            pe.wait_ge(x1_first, 4)
            transposes(0, x1, 3, x1T)
            pe.wait_ge(x1T_c, 1)
            pe.wait_ge(w_first, 32)
            k = 0
            for n, (g, e, c) in enumerate(units):
                if n == 4:
                    pe.wait_ge(w_rest, 32)
                if n % PER_GROUP == 0 and 0 < g:
                    pe.wait_ge(x1T_c, g + 1)
                for j, w in ((2 * n, w3), (2 * n + 1, w1)):
                    if j >= UP:
                        if (j - UP) % 2 == 0:
                            pe.wait_ge(h3c, (j - UP) // 2 + 1)
                        else:
                            pe.wait_ge(hgd, (j - UP) // 2 + 1)
                    nc.tensor.matmul(ps[j % UP][:], w[:, e, c * P:(c + 1) * P], xT[:, 4 * g:4 * g + 4, :],
                                     start=True, stop=True).then_inc(up, 1)
                if n in NEXT_X1:
                    m = NEXT_X1[n]
                    if m == 1:
                        pe.wait_ge(x1_first, 8)
                        pe.wait_ge(yadd, 4)
                    else:
                        pe.wait_ge(x1_rest, 4 * (m - 1))
                        pe.wait_ge(x1T_c, m)
                    transposes(m, x1, SIDE, x1T)
                if n == GATE - 1:
                    pe.wait_ge(w_gate, 32)
                    pe.wait_ge(x1T_c, GROUPS)
                    for i in range(NTOK):
                        last = nc.tensor.matmul(ps[SIDE][:, i * NE:(i + 1) * NE], xT[:, i, :], wg[:], start=True, stop=True)
                    last.then_inc(lg, 1)
                    pe.wait_ge(w2_in, 16)
                if n == GATE + 5:
                    pe.wait_ge(gwd, 1)
                    nc.tensor.transpose(ps[SIDE][:, 0:P], gw[:].rearrange("p t e -> p (t e)"), ident[:]).then_inc(gwTd, 1)
                if n == entries[ENTRY[0, NE]][2]:
                    pe.wait_ge(gwTc, 1)
                    pe.wait_ge(bd, NTOK)
                while k < len(entries) and entries[k][2] == n:
                    down_entry(k)
                    k += 1
                if n > MIXT_AT - 1 and n % PER_GROUP == MIXT_AT % PER_GROUP:
                    mg = n // PER_GROUP - 1
                    if mg >= 1:
                        pe.wait_ge(fy, mg)
                    else:
                        pe.wait_ge(wf_in, 32)
                    mixed_back(mg, SIDE)
                if n > FINAL_AT - 1 and n % PER_GROUP == FINAL_AT % PER_GROUP:
                    final(n // PER_GROUP - 1, SIDE)
            down_entry(len(entries) - 1)
            mixed_back(GROUPS - 1, 0)
            final(GROUPS - 1, 1)

        @block.scalar
        def _(act):
            def copy_group(g, bank, done):
                nc.scalar.activation(xT[:, 4 * g:4 * g + 4, :].rearrange("p t d -> p (t d)"), ps[bank][:], ACT.Copy)\
                    .then_inc(done, 1)

            def root(g, ready, done):
                act.wait_ge(ready, g + 1)
                nc.scalar.activation(rstd[:, 4 * g:4 * g + 4], mv[:, 4 * g:4 * g + 4, 1], ACT.Sqrt, bias=epsc[:])\
                    .then_inc(done, 1)

            def silu(m):
                act.wait_ge(hgd, m + 1)
                if m >= HS:
                    g, e, _ = units[m - HS]
                    act.wait_ge(down, ENTRY[g, e] + 1)
                nc.scalar.activation(hs[m % HS][:], hg[m % 2][:], ACT.Silu).then_inc(hsd, 1)

            act.wait_ge(mk, 1)
            nc.scalar.activation(warm[:], epsc[:], ACT.Sqrt)
            for g in range(GROUPS):
                act.wait_ge(ctxT, g + 1)
                copy_group(g, g, ctxT_c)
            root(0, rs, rt)
            root(1, rs, rt)
            act.wait_ge(proj, 1)
            act.wait_ge(x1T, 1)
            copy_group(0, 3, x1T_c)
            root(2, rs, rt)
            root(3, rs, rt)
            act.wait_ge(proj, GROUPS)
            act.wait_ge(b_up, 32)
            for n, (g, e, c) in enumerate(units):
                act.wait_ge(up, 2 * n + 1)
                if n >= 2:
                    act.wait_ge(hgd, n - 1)
                nc.scalar.activation(h3b[n % 2][:], ps[2 * n % UP][:], ACT.Identity, bias=b3[:, e, c:c + 1])\
                    .then_inc(h3c, 1)
                if n in NEXT_X1:
                    act.wait_ge(x1T, NEXT_X1[n] + 1)
                    copy_group(NEXT_X1[n], SIDE, x1T_c)
                if n >= 1:
                    silu(n - 1)
                if n == GATE + 1:
                    act.wait_ge(glog, 1)
                    nc.scalar.activation(gate[:], logit[:], ACT.Exp).then_inc(gexp, 1)
                if n == GATE + 5:
                    act.wait_ge(gwTd, 1)
                    nc.scalar.activation(gwT[:], ps[SIDE][:, 0:P], ACT.Copy).then_inc(gwTc, 1)
                if n > MIXT_AT - 1 and n % PER_GROUP == MIXT_AT % PER_GROUP:
                    mg = n // PER_GROUP - 1
                    act.wait_ge(mixT, mg + 1)
                    copy_group(mg, SIDE, mixT_c)
                if n == ROOTS_AT:
                    for g in range(GROUPS - 1):
                        root(g, rs2, rt2)
            silu(LAST)
            nc.scalar.activation(warm[:], epsc[:], ACT.Sqrt)
            act.wait_ge(mixT, GROUPS)
            copy_group(GROUPS - 1, 0, mixT_c)
            root(GROUPS - 1, rs2, rt2)

        @block.vector
        def _(v):
            count = [0]

            def step(ins):
                count[0] += 1
                ins.then_inc(dv, 1)
                v.wait_ge(dv, count[0])

            def norm_stats(g, done):
                for i in range(4 * g, 4 * g + 4):
                    last = nc.vector.bn_stats(stats[:, i, :], y[:, i, :])
                step(last)
                for i in range(4 * g, 4 * g + 4):
                    last = nc.vector.bn_aggr(mv[:, i, :], stats[:, i, :])
                last.then_inc(done, 1)

            def one_over(g, roots, done):
                v.wait_ge(roots, g + 1)
                nc.vector.reciprocal(rstd[:, 4 * g:4 * g + 4], rstd[:, 4 * g:4 * g + 4]).then_inc(done, 1)

            def residual(g):
                v.wait_ge(proj, g + 1)
                nc.vector.tensor_tensor(y[:, 4 * g:4 * g + 4, :].rearrange("p t d -> p (t d)"), ps[4 + g][:],
                                        keep["xb"][:, 4 * g:4 * g + 4, :].rearrange("p t d -> p (t d)"),
                                        ALU.add).then_inc(yadd, 1)
                v.wait_ge(yadd, g + 1)
                norm_stats(g, rs)

            def mix(k):
                g, e, _ = entries[k]
                v.wait_ge(down, k + 1)
                if e > 0:
                    v.wait_ge(mixed, 4 * k)
                o = ps[DOWN[k % 2]]
                if e == NE:
                    whole = acc[:, 4 * g:4 * g + 4, :].rearrange("p t d -> p (t d)")
                    nc.vector.tensor_tensor(whole, o[:], whole, ALU.add).then_inc(mixed, 4)
                    return
                for i in range(4):
                    tt = 4 * g + i
                    if e == 0:
                        nc.vector.tensor_scalar(acc[:, tt, :], o[:, i * P:(i + 1) * P], gw[:, tt, e:e + 1], None,
                                                ALU.mult).then_inc(mixed, 1)
                    else:
                        nc.vector.scalar_tensor_tensor(out=acc[:, tt, :], in0=o[:, i * P:(i + 1) * P],
                                                       scalar=gw[:, tt, e:e + 1], in1=acc[:, tt, :],
                                                       op0=ALU.mult, op1=ALU.add).then_inc(mixed, 1)

            def output_stats(g, bank):
                v.wait_ge(fin, g + 1)
                if g == 0:
                    v.wait_ge(x1_bf, 1)
                nc.vector.tensor_tensor(y[:, 4 * g:4 * g + 4, :].rearrange("p t d -> p (t d)"), ps[bank][:],
                                        x1[:, 4 * g:4 * g + 4, :].rearrange("p t d -> p (t d)"), ALU.add).then_inc(fy, 1)
                v.wait_ge(fy, g + 1)
                norm_stats(g, rs2)

            residual(0)
            residual(1)
            one_over(0, rt, rr)
            v.wait_ge(rr, 1)
            for i in range(4):
                nc.vector.tensor_scalar(x1[:, i, :], y[:, i, :], mv[:, i, 0:1], rstd[:, i:i + 1],
                                        ALU.subtract, ALU.mult).then_inc(x1_first, 1)
            one_over(1, rt, rr)
            v.wait_ge(rr, 2)
            for i in range(4, 8):
                nc.vector.tensor_scalar(x1[:, i, :], y[:, i, :], mv[:, i, 0:1], rstd[:, i:i + 1],
                                        ALU.subtract, ALU.mult).then_inc(x1_first, 1)
            residual(2)
            one_over(2, rt, rr)
            residual(3)
            one_over(3, rt, rr)
            fl = lambda x: x[:].rearrange("p t e f -> p t (e f)")
            k = 0
            for n, (g, e, c) in enumerate(units):
                v.wait_ge(h3c, n + 1)
                v.wait_ge(up, 2 * n + 2)
                if n >= 2:
                    v.wait_ge(hsd, n - 1)
                nc.vector.scalar_tensor_tensor(out=hg[n % 2][:], in0=ps[(2 * n + 1) % UP][:], scalar=b1[:, e, c:c + 1],
                                               in1=h3b[n % 2][:], op0=ALU.add, op1=ALU.mult).then_inc(hgd, 1)
                if n == GATE:
                    v.wait_ge(lg, 1)
                    nc.vector.tensor_tensor(logit[:], ps[SIDE][:, 0:NTOK * NE].rearrange("p (t e) -> p t e", e=NE),
                                            bg[:].unsqueeze(1).to_broadcast([P, NTOK, NE]), ALU.add).then_inc(lgc, 1)
                    v.wait_ge(lgc, 1)
                    step(nc.vector.tensor_reduce(gmax[:], logit[:], AX_X, ALU.max))
                    nc.vector.tensor_tensor(logit[:], logit[:], gmax[:].unsqueeze(2).to_broadcast([P, NTOK, NE]),
                                            ALU.subtract).then_inc(glog, 1)
                if n == GATE + 1:
                    v.wait_ge(gexp, 1)
                    step(nc.vector.tensor_reduce(gmax[:], gate[:], AX_X, ALU.add))
                    step(nc.vector.reciprocal(gmax[:], gmax[:]))
                    step(nc.vector.tensor_tensor(gate[:], gate[:], gmax[:].unsqueeze(2).to_broadcast([P, NTOK, NE]),
                                                 ALU.mult))
                    v.wait_ge(mk, 6)
                    mine = gate[:].unsqueeze(3).to_broadcast([P, NTOK, NE, NE])
                    other = gate[:].unsqueeze(2).to_broadcast([P, NTOK, NE, NE])
                    nc.vector.tensor_tensor(beats[:], other, mine, ALU.is_gt)
                if n == GATE + 2:
                    step(nc.vector.tensor_tensor(ties[:], other, mine, ALU.is_equal))
                    lat = later[:].rearrange("p e f -> p (e f)").unsqueeze(1).to_broadcast([P, NTOK, NE * NE])
                    step(nc.vector.tensor_tensor(fl(ties), fl(ties), lat, ALU.mult))
                if n == GATE + 3:
                    step(nc.vector.tensor_tensor(fl(beats), fl(beats), fl(ties), ALU.add))
                if n == GATE + 4:
                    step(nc.vector.tensor_reduce(rank[:], beats[:], AX_X, ALU.add))
                    step(nc.vector.tensor_scalar(rank[:], rank[:], 1.5, None, ALU.is_lt))
                    nc.vector.tensor_tensor(gw[:], gate[:], rank[:], ALU.mult).then_inc(gwd, 1)
                    v.wait_ge(gwd, 1)
                while k < len(entries) and entries[k][2] + 1 == n:
                    mix(k)
                    k += 1
                if n > OUT_AT - 1 and n % PER_GROUP == OUT_AT % PER_GROUP:
                    output_stats(n // PER_GROUP - 1, SIDE)
                if n == ROOTS_AT + 1:
                    for og in range(GROUPS - 1):
                        one_over(og, rt2, rr2)
            for rest in range(k, len(entries)):
                mix(rest)
            output_stats(GROUPS - 1, 1)
            one_over(GROUPS - 1, rt2, rr2)
            v.wait_ge(rr2, GROUPS)
            for i in range(4 * GROUPS - 4, 4 * GROUPS):
                nc.vector.tensor_scalar(y[:, i, :], y[:, i, :], mv[:, i, 0:1], rstd[:, i:i + 1],
                                        ALU.subtract, ALU.mult).then_inc(od_last, 1)


NAMES = ["L0_attn_x", "L0_attn_Wq", "L0_attn_bq", "L0_attn_Wk", "L0_attn_bk", "L0_attn_Wv", "L0_attn_bv",
         "L0_attn_Wo", "L0_attn_bo", "L0_attn_Wpk", "L0_attn_bpk", "L0_attn_Wpq", "L0_attn_bpq", "L0_attn_rel_emb",
         "L0_ffn_W1", "L0_ffn_b1", "L0_ffn_W3", "L0_ffn_b3", "L0_ffn_W2", "L0_ffn_b2", "L0_ffn_Wg", "L0_ffn_bg",
         "L0_ffn_Wf", "L0_ffn_bf"]


def build(nc, a, out):
    scr = {
        "qparts": nc.dram_tensor("qparts", [UNITS, 3, DK, T], BF16, kind="Internal"),
        "kparts": nc.dram_tensor("kparts", [UNITS, 3, DK, T], BF16, kind="Internal"),
        "far": nc.dram_tensor("far_rows", [UNITS, 4, 3, T], BF16, kind="Internal"),
        "v": nc.dram_tensor("v_units", [UNITS, P, NT * 32], F32, kind="Internal"),
        "tab": nc.dram_tensor("pos_parts", [3, P, 2 * S], BF16, kind="Internal"),
        "ring": nc.dram_tensor("skew_ring", [2, 2, NT * P, 2 * S], F32, kind="Internal"),
    }
    ctx = ExitStack()
    with ctx:
        keep = {}
        for name, shape, dt in (("ident", [P, P], F32), ("identb", [P, P], BF16), ("cmask", [P, S], F32),
                                ("pmask", [P, S], F32), ("woT", [P, P], F32), ("xb", [P, B * NT, D], F32),
                                ("ctx", [P, B * NT, D], F32)):
            keep[name] = ctx.enter_context(nc.sbuf_tensor(name, shape, dt))
        keep["tab"] = ctx.enter_context(nc.sbuf_tensor("tab", [ROWS, 2, H, S], BF16))
        keep["qst"] = [ctx.enter_context(nc.sbuf_tensor(f"qst{i}", [T_ROWS, T], BF16)) for i in range(4)]
        keep["kst"] = [ctx.enter_context(nc.sbuf_tensor(f"kst{i}", [T_ROWS, 2, T], BF16)) for i in range(4)]
        prologue(nc, a, scr, keep)
        attention(nc, a, scr, keep)
        ffn(nc, a, keep, out)


def kernel(**inputs):
    import numpy as np
    import concourse.bacc as bacc
    from concourse.bass_utils import run_bass_kernel_spmd

    nc = bacc.Bacc("TRN2", target_bir_lowering=False, num_devices=1)
    arrays, args = {}, {}
    for name in NAMES:
        x = np.ascontiguousarray(inputs[name])
        arrays[f"in_{name}"] = x
        args[name] = nc.dram_tensor(f"in_{name}", x.shape, mybir.dt.from_np(x.dtype), kind="ExternalInput").ap()
    out = nc.dram_tensor("out_0_dram", (B, T, D), F32, kind="ExternalOutput").ap()
    build(nc, args, out)
    return run_bass_kernel_spmd(nc, [arrays], core_ids=[0]).results[0]["out_0_dram"]
```

```python
import concourse.bass as bass
from concourse import mybir
from contextlib import ExitStack

F32 = mybir.dt.float32
BF16 = mybir.dt.bfloat16
F32R = mybir.dt.float32r
ALU = mybir.AluOpType
ACT = mybir.ActivationFunctionType
AX_X = mybir.AxisListType.X

B, T, D = 2, 1024, 128
H, DK = 16, 8
P = 128
NT = T // P
UNITS = B * H
S = 128
HALF = S // 2
ROWS = 48
NEAR = 3 * P
QH = 512
SCALE = 1.0 / 24.0 ** 0.5
LOW = -3.0e38
NE, HID = 8, 256
EPS = 1e-5
B_L, A_L, B_R, A_R, BASE_ROWS, M_ROW, T_ROWS = 48, 51, 54, 57, 60, 64, 66
Q_ORDER, K_ORDER = (0, 0, 0, 1, 1, 2), (0, 1, 2, 0, 1, 0)
SLOTS_BEFORE, SLOTS_AFTER = 2, 2
WARM_UP = 80


def head_mask(nc, pool, mask, sem, done):
    nc.gpsimd.memset(mask[:], 1.0).then_inc(sem, 1)
    pool.wait_ge(sem, done + 1)
    nc.gpsimd.affine_select(out=mask[:], in_=mask[:], compare_op=ALU.is_ge, fill=0.0, base=0,
                            pattern=[[-DK, H]], channel_multiplier=1).then_inc(sem, 1)
    pool.wait_ge(sem, done + 2)
    nc.gpsimd.affine_select(out=mask[:], in_=mask[:], compare_op=ALU.is_ge, fill=0.0, base=DK - 1,
                            pattern=[[DK, H]], channel_multiplier=-1).then_inc(sem, 1)
    pool.wait_ge(sem, done + 3)


def load_parts(sp, scratch, u, order, dst, done):
    if order is Q_ORDER:
        for r0, reps, part in ((0, 3, 0), (24, 2, 1), (40, 1, 2)):
            sp.dma_start(dst[r0:r0 + 8 * reps], bass.AP(scratch, (u * 3 + part) * DK * T,
                                                        [[0, reps], [T, DK], [1, T]])).then_inc(done, 16)
    else:
        for r0, parts in ((0, 3), (24, 2), (40, 1)):
            sides = [[0, 2]] if len(dst.shape) == 3 else []
            sp.dma_start(dst[r0:r0 + 8 * parts], bass.AP(scratch, u * 3 * DK * T,
                                                         [[T, parts * DK]] + sides + [[1, T]])).then_inc(done, 16)


def prologue(nc, a, scr, keep):
    ctx = ExitStack()
    with ctx:
        def sb(name, shape, dt=F32):
            return ctx.enter_context(nc.sbuf_tensor(name, shape, dt))

        def sem(name):
            return ctx.enter_context(nc.semaphore(name))

        x_sb = keep["xb"]
        w_sb = sb("w_sb", [P, 6, D])
        rel_sb = sb("rel_sb", [P, D])
        bias = sb("bias", [P, 4])
        bv_row = sb("bv_row", [P, D])
        xT = sb("xT", [P, B * T])
        wT = sb("wT", [P, 5, D])
        relT = sb("relT", [P, 2, S])
        turn = sb("turn", [P, S])
        qk = sb("qk", [P, 2, B * T])
        rest = sb("rest", [P, 3, T])
        room = keep["probs"][:].rearrange("p n q -> p (n q)").bitcast(BF16)
        parts = [room[:, w * 3 * B * T:(w + 1) * 3 * B * T].rearrange("p (k t) -> p k t", k=3) for w in range(2)]
        pos = sb("pos", [P, 2, S])
        posrel = sb("posrel", [P, 2 * S])
        posrest = sb("posrest", [P, 2 * S])
        posparts = sb("posparts", [P, 3, 2 * S], BF16)
        ends = sb("ends", [P, 2, 2 * H])
        far = sb("far", [P, T])
        farparts = room[:, 6 * B * T:6 * B * T + 3 * T].rearrange("p (k t) -> p k t", k=3)
        zrow = room[0:6, 6 * B * T + 3 * T:6 * B * T + 4 * T]
        zeros = sb("zeros", [P, S])
        hmask = sb("hmask", [P, H])
        ps = [ctx.enter_context(nc.psum_tensor(f"pp{i}", [P, QH], F32)) for i in range(8)]

        x_in, w_in, b_in, brow_in = sem("x_in"), sem("w_in"), sem("b_in"), sem("brow_in")
        masks, turned = sem("masks"), sem("turned")
        ident_ready, zero_ready = sem("ident_ready"), sem("zero_ready")
        pe_bank, copied = sem("pe_bank"), sem("copied")
        first_part, rest_done, second_part = sem("first_part"), sem("rest_done"), sem("second_part")
        split, pos_split = sem("split"), sem("pos_split")
        ends_set = sem("ends_set")
        tab_out, tab_in, rows_set = sem("tab_out"), sem("tab_in"), sem("rows_set")
        dve = sem("dve")
        v_done = sem("v_done")
        stored = sem("stored")
        block = ctx.enter_context(nc.Block())
        CHUNKS = [(0, 0), (1, 0), (0, 1), (2, 0), (1, 1)]
        W_T, QK0, POS, QK1, FAR_AT, V_AT, STEPS = 4, 6, 10, 11, 15, 17, 21

        def table_rows(queue, which, order, done):
            for r, part in enumerate(order):
                src = bass.AP(scr["tab"], part * P * 2 * S + which * S, [[2 * S, DK], [DK * 2 * S, H], [1, S]])
                queue.dma_start(keep["tab"][8 * r:8 * r + 8, which, :, :], src).then_inc(done, 16)

        @block.sync
        def _(sp):
            xv = a["L0_attn_x"].rearrange("b (t p) d -> p (b t) d", p=P)
            for g in range(4):
                sp.dma_start(x_sb[:, 4 * g:4 * g + 4, :], xv[:, 4 * g:4 * g + 4, :]).then_inc(x_in, 16)
            for i, n in enumerate(["Wq", "Wk", "Wv", "Wpk", "Wpq", "Wo"]):
                sp.dma_start(w_sb[:, i, :], a["L0_attn_" + n]).then_inc(w_in, 16)
            sp.dma_start(rel_sb[:], a["L0_attn_rel_emb"]).then_inc(w_in, 16)
            for i, n in enumerate(["bq", "bk", "bpk", "bpq"]):
                sp.dma_start(bias[:, i:i + 1], a["L0_attn_" + n].unsqueeze(1)).then_inc(b_in, 16)
            sp.wait_ge(zero_ready, 1)
            sp.dma_start(bass.AP(scr["ring"], S, [[2 * S, P], [P * 2 * S, 4 * NT], [1, S]]),
                         zeros[:].unsqueeze(1).to_broadcast([P, 4 * NT, S])).then_inc(stored, 16)

            def store_chunk(c):
                which, b = CHUNKS[c]
                sp.wait_ge(split, c + 1)
                if which == 2:
                    sp.dma_start(scr["far"][:], farparts).then_inc(keep["far_stored"], 16)
                    return
                for part in range(3):
                    dst = bass.AP(scr[("qparts", "kparts")[which]], (b * H * 3 + part) * DK * T,
                                  [[3 * DK * T, H], [T, DK], [1, T]])
                    sp.dma_start(dst, parts[which][:, part, b * T:(b + 1) * T])\
                        .then_inc(keep["parts_stored"][b], 16)

            store_chunk(0)
            sp.wait_ge(pos_split, 1)
            for part in range(3):
                sp.dma_start(scr["tab"][part], posparts[:, part, :]).then_inc(tab_out, 16)
            store_chunk(1)
            sp.wait_ge(tab_out, 48)
            table_rows(sp, 0, K_ORDER, stored)
            sp.wait_ge(keep["parts_stored"][0], 16 * 6)
            load_parts(sp, scr["qparts"], 0, Q_ORDER, keep["rawq"][0], keep["raw_in"][0])
            load_parts(sp, scr["kparts"], 0, K_ORDER, keep["rawk"][0], keep["raw_in"][0])
            store_chunk(2)
            store_chunk(3)
            store_chunk(4)
            sp.wait_ge(rows_set, 3)
            for dst in (keep["kst"][B_R:B_R + 6, :, 0, :], keep["kst"][B_L:B_L + 6, :, 1, :],
                        keep["qst"][BASE_ROWS:M_ROW, :, :]):
                rows = dst.shape[0]
                sp.dma_start(dst, zrow[0:rows, :].unsqueeze(1).to_broadcast([rows, 4, T])).then_inc(keep["rows_in"], 16)
            sp.wait_ge(stored, 16 * (1 + 6))

        @block.gpsimd
        def _(pool):
            nc.gpsimd.memset(turn[:], 0.0).then_inc(turned, 1)
            pool.wait_ge(turned, 1)
            nc.gpsimd.affine_select(out=turn[:], in_=turn[:], compare_op=ALU.not_equal, fill=1.0,
                                    base=-S, pattern=[[1, S]], channel_multiplier=1).then_inc(turned, 1)
            pool.wait_ge(turned, 2)
            nc.gpsimd.affine_select(out=turn[:], in_=turn[:], compare_op=ALU.not_equal, fill=1.0,
                                    base=0, pattern=[[1, S]], channel_multiplier=1).then_inc(turned, 1)
            nc.gpsimd.memset(keep["ident"][:], 0.0).then_inc(masks, 1)
            pool.wait_ge(masks, 1)
            nc.gpsimd.affine_select(out=keep["ident"][:], in_=keep["ident"][:], compare_op=ALU.not_equal, fill=1.0,
                                    base=0, pattern=[[-1, P]], channel_multiplier=1).then_inc(ident_ready, 1)
            nc.gpsimd.memset(zeros[:], 0.0).then_inc(zero_ready, 1)
            pool.dma_start(bv_row[:], a["L0_attn_bv"].partition_broadcast(P)).then_inc(brow_in, 16)
            pool.dma_start(keep["bo_row"][:], a["L0_attn_bo"].partition_broadcast(P)).then_inc(brow_in, 16)
            head_mask(nc, pool, hmask, masks, 1)
            nc.gpsimd.memset(keep["identb"][:], 0.0).then_inc(masks, 1)
            pool.wait_ge(masks, 5)
            nc.gpsimd.affine_select(out=keep["identb"][:], in_=keep["identb"][:], compare_op=ALU.not_equal, fill=1.0,
                                    base=0, pattern=[[-1, P]], channel_multiplier=1).then_inc(masks, 1)
            nc.gpsimd.memset(keep["cmask"][:], 1.0).then_inc(masks, 1)
            pool.wait_ge(masks, 7)
            nc.gpsimd.affine_select(out=keep["cmask"][:], in_=keep["cmask"][:], compare_op=ALU.is_ge, fill=0.0,
                                    base=-S, pattern=[[1, S]], channel_multiplier=1).then_inc(masks, 1)
            nc.gpsimd.memset(keep["pmask"][:], 1.0).then_inc(masks, 1)
            pool.wait_ge(masks, 9)
            for half, bound in ((0, HALF), (1, HALF + S)):
                m = keep["pmask"][half * HALF:(half + 1) * HALF, :]
                nc.gpsimd.affine_select(out=m, in_=m, compare_op=ALU.is_ge, fill=0.0,
                                        base=bound - 1 - half * HALF, pattern=[[-1, S]],
                                        channel_multiplier=-1).then_inc(masks, 1)
                pool.wait_ge(masks, 10 + half)
            nc.gpsimd.memset(zrow, 0.0).then_inc(rows_set, 1)
            nc.gpsimd.memset(keep["kst"][:], 1.0).then_inc(rows_set, 1)
            nc.gpsimd.memset(keep["qst"][:], 1.0).then_inc(rows_set, 1)
            pool.wait_ge(tab_out, 48)
            table_rows(pool, 1, Q_ORDER, tab_in)
            pool.wait_ge(tab_in, 16 * 6)

        @block.tensor
        def _(pe):
            pe.wait_ge(ident_ready, 1)
            step = 0

            def bank():
                if step >= 8:
                    pe.wait_ge(copied, step - 7)
                return ps[step % 8]

            for g in range(4):
                pe.wait_ge(x_in, 64)
                o = bank()
                for i in range(4):
                    last = nc.tensor.transpose(o[:, i * P:(i + 1) * P], x_sb[:, 4 * g + i, :], keep["ident"][:])
                last.then_inc(pe_bank, 1)
                step += 1
            pe.wait_ge(w_in, 7 * 16)
            pe.wait_ge(turned, 3)
            for g in range(2):
                o = bank()
                for i in range(4):
                    src = rel_sb[:] if g == 1 and i >= 2 else w_sb[:, 4 * g + i, :]
                    perm = turn[:] if g == 1 and i == 3 else keep["ident"][:]
                    last = nc.tensor.transpose(o[:, i * P:(i + 1) * P], src, perm)
                last.then_inc(pe_bank, 1)
                step += 1

            def project(bb):
                nonlocal step
                for which in range(2):
                    for g in (2 * bb, 2 * bb + 1):
                        o = bank()
                        nc.tensor.matmul(o[:], wT[:, which, :], xT[:, g * QH:(g + 1) * QH], start=True, stop=True)\
                            .then_inc(pe_bank, 1)
                        step += 1

            pe.wait_ge(copied, QK0)
            project(0)
            o = bank()
            nc.tensor.matmul(o[:, 0:S], wT[:, 3, :], relT[:, 0, :], start=True, stop=True)
            nc.tensor.matmul(o[:, S:2 * S], wT[:, 4, :], relT[:, 1, :], start=True, stop=True).then_inc(pe_bank, 1)
            step += 1
            project(1)
            pe.wait_ge(ends_set, 1)
            pe.wait_ge(copied, FAR_AT)
            for g in range(2):
                o = bank()
                for bb in range(B):
                    for which in range(2):
                        r0 = 4 * H * bb + 2 * H * which
                        last = nc.tensor.matmul(o[r0:r0 + 2 * H, :], ends[:, which, :],
                                                qk[:, which, bb * T + g * QH:bb * T + (g + 1) * QH],
                                                start=True, stop=True)
                last.then_inc(pe_bank, 1)
                step += 1
            for g in range(4):
                o = bank()
                for i in range(4):
                    last = nc.tensor.matmul(o[:, i * P:(i + 1) * P], xT[:, (4 * g + i) * P:(4 * g + i + 1) * P],
                                            wT[:, 2, :], start=True, stop=True)
                last.then_inc(pe_bank, 1)
                step += 1
            assert step == STEPS

        def chunk_src(which, b):
            return far[:] if which == 2 else qk[:, which, b * T:(b + 1) * T]

        def chunk_part(which, b, part):
            return (farparts if which == 2 else parts[which])[:, part, b * T:(b + 1) * T]

        @block.scalar
        def _(act):
            copies = [0]

            def evacuate(step):
                act.wait_ge(pe_bank, step + 1)
                o = ps[step % 8]
                if step < 4:
                    nc.scalar.activation(xT[:, step * QH:(step + 1) * QH], o[:], ACT.Copy).then_inc(copied, 1)
                elif step == 4:
                    nc.scalar.activation(wT[:, 0:4, :].rearrange("p a b -> p (a b)"), o[:], ACT.Copy).then_inc(copied, 1)
                elif step == 5:
                    nc.scalar.activation(wT[:, 4, :], o[:, 0:P], ACT.Copy)
                    nc.scalar.activation(keep["woT"][:], o[:, P:2 * P], ACT.Copy)
                    nc.scalar.activation(relT[:].rearrange("p a s -> p (a s)"), o[:, 2 * P:4 * P], ACT.Copy)\
                        .then_inc(copied, 1)
                elif step == POS:
                    nc.scalar.activation(pos[:, 0, :], o[:, 0:S], ACT.Identity, bias=bias[:, 2:3])
                    nc.scalar.activation(pos[:, 1, :], o[:, S:2 * S], ACT.Identity, bias=bias[:, 3:4]).then_inc(copied, 1)
                elif step < FAR_AT:
                    bb, i = (0, step - QK0) if step < POS else (1, step - QK1)
                    which, g = i // 2, 2 * bb + i % 2
                    nc.scalar.activation(qk[:, which, g * QH:(g + 1) * QH], o[:], ACT.Identity,
                                         bias=bias[:, which:which + 1]).then_inc(copied, 1)
                else:
                    g = step - FAR_AT
                    nc.scalar.activation(far[:, g * QH:(g + 1) * QH], o[:], ACT.Copy).then_inc(copied, 1)
                copies[0] += 1

            def first(c):
                act.wait_ge(copied, copies[0])
                nc.scalar.activation(chunk_part(*CHUNKS[c], 0), chunk_src(*CHUNKS[c]), ACT.Copy).then_inc(first_part, 1)

            def second(c):
                act.wait_ge(rest_done, c + 1)
                nc.scalar.activation(chunk_part(*CHUNKS[c], 1), rest[:, c % 3, :], ACT.Copy).then_inc(second_part, 1)

            for step in range(QK0):
                evacuate(step)
            act.wait_ge(b_in, 64)
            evacuate(6)
            evacuate(7)
            first(0)
            evacuate(8)
            evacuate(9)
            first(1)
            evacuate(POS)
            second(0)
            evacuate(11)
            evacuate(12)
            first(2)
            second(1)
            evacuate(13)
            evacuate(14)
            second(2)
            evacuate(15)
            evacuate(16)
            first(3)
            first(4)
            second(3)
            second(4)

        @block.vector
        def _(v):
            count = [0]

            def step(ins):
                count[0] += 1
                ins.then_inc(dve, 1)
                v.wait_ge(dve, count[0])

            def rest_parts(src, rem, out, done):
                step(nc.vector.tensor_tensor(rem, src, out[0], ALU.subtract))
                step(nc.vector.tensor_copy(out[1], rem))
                nc.vector.tensor_tensor(out[2], rem, out[1], ALU.subtract).then_inc(done, 1)

            def rest_of(c):
                v.wait_ge(first_part, c + 1)
                if c >= 3:
                    v.wait_ge(split, c - 2)
                nc.vector.tensor_tensor(rest[:, c % 3, :], chunk_src(*CHUNKS[c]), chunk_part(*CHUNKS[c], 0),
                                        ALU.subtract).then_inc(rest_done, 1)

            def third(c):
                v.wait_ge(rest_done, c + 1)
                v.wait_ge(second_part, c + 1)
                nc.vector.tensor_tensor(chunk_part(*CHUNKS[c], 2), rest[:, c % 3, :], chunk_part(*CHUNKS[c], 1),
                                        ALU.subtract).then_inc(split, 1)

            rest_of(0)
            rest_of(1)
            v.wait_ge(copied, POS + 1)
            v.wait_ge(masks, 4)
            nc.vector.tensor_scalar(posrel[:, 0:S], pos[:, 0, :], pos[:, 0, 0:1], None, ALU.subtract)
            nc.vector.tensor_scalar(posrel[:, S:S + 1], pos[:, 1, 1:2], pos[:, 1, 0:1], None, ALU.subtract)
            step(nc.vector.tensor_scalar(posrel[:, S + 1:2 * S], pos[:, 1, 1:S], pos[:, 1, 0:1], None, ALU.subtract))
            for which, col, at in ((0, 0, 0), (0, S - 1, H), (1, 0, 0), (1, 1, H)):
                last = nc.vector.tensor_scalar(ends[:, which, at:at + H], hmask[:], pos[:, which, col:col + 1],
                                               None, ALU.mult)
            last.then_inc(ends_set, 1)
            third(0)
            step(nc.vector.tensor_copy(posparts[:, 0, :], posrel[:]))
            rest_parts(posrel[:], posrest[:], [posparts[:, i, :] for i in range(3)], pos_split)
            third(1)
            rest_of(2)
            rest_of(3)
            third(2)
            rest_of(4)
            third(3)
            third(4)
            v.wait_ge(brow_in, 32)
            for g in range(4):
                v.wait_ge(pe_bank, V_AT + g + 1)
                nc.vector.tensor_tensor(keep["v"][:, 4 * g:4 * g + 4, :],
                                        ps[(V_AT + g) % 8][:].rearrange("p (t d) -> p t d", d=D),
                                        bv_row[:].unsqueeze(1).to_broadcast([P, 4, D]), ALU.add).then_inc(v_done, 1)


def attention(nc, a, scr, keep):
    ctx = ExitStack()
    with ctx:
        def sb(name, shape, dt=F32):
            return ctx.enter_context(nc.sbuf_tensor(name, shape, dt))

        def sem(name):
            return ctx.enter_context(nc.semaphore(name))

        ident, identb = keep["ident"], keep["identb"]
        tab = keep["tab"]
        qst, kst = ([keep[n][:, i] for i in range(4)] for n in ("qst", "kst"))
        rawq, rawk = keep["rawq"], keep["rawk"]
        vst = [sb(f"vst{i}", [P, NT, 32]) for i in range(2)]
        raw = [sb(f"raw{i}", [P, 2, NT, S]) for i in range(2)]
        fix = sb("fix", [P, NT, S])
        skew = [sb(f"skew{i}", [P, 2, NT, NEAR]) for i in range(2)]
        near = [sb(f"near{i}", [P, NT, NEAR]) for i in range(2)]
        probs = keep["probs"]
        st = sb("st", [P, NT, 3])
        mx = sb("mx", [P, NT])
        mparts = sb("mparts", [P, 2, NT], BF16)
        mrow = sb("mrow", [2 * NT, P], BF16)
        pvs = [sb(f"pvs{i}", [P, QH]) for i in range(2)]
        m_hat = sb("m_hat", [P, NT])
        csum = sb("csum", [P, NT, DK + 1])
        crec = sb("crec", [P, NT])

        nat = [ctx.enter_context(nc.psum_tensor(f"nat{i}", [P, T], F32)) for i in range(2)]
        tps = [ctx.enter_context(nc.psum_tensor(f"tps{i}", [P, QH], F32)) for i in range(2)]
        pv = ctx.enter_context(nc.psum_tensor("pv", [P, QH], F32))
        misc = ctx.enter_context(nc.psum_tensor("misc", [P, QH], F32))
        misc_b = misc[:].bitcast(BF16)

        zeroed = sem("zeroed")
        raw_in = keep["raw_in"]
        unit_in = [sem(f"unit_in{i}") for i in range(4)]
        v_zero, v_ones, v_set = sem("v_zero"), sem("v_ones"), sem("v_set")
        raw_done, raw_copied = sem("raw_done"), sem("raw_copied")
        fix_done, rel_done, fix_early, rel_early = (sem(n) for n in ("fix_done", "rel_done", "fix_early", "rel_early"))
        skew_out = [sem(f"skew_out{i}") for i in range(2)]
        skew_in = [sem(f"skew_in{i}") for i in range(2)]
        nat_done, near_done, far_done = sem("nat_done"), sem("near_done"), sem("far_done")
        m_step, m_done, mT_done, m_copied, m_rows = (sem(n) for n in ("m_step", "m_done", "mT_done", "m_copied", "m_rows"))
        xb_done = sem("xb_done")
        m_hat_done, sub_done = sem("m_hat_done"), sem("sub_done")
        t_done, exp_done = sem("t_done"), sem("exp_done")
        pv_done, pv_copied = sem("pv_done"), sem("pv_copied")
        finT_done, fin_step, fin_done = sem("finT_done"), sem("fin_step"), sem("fin_done")
        LOADS = 3 + 3 + 2 + 2
        RAW_LOADS = 6

        def near_cols(t):
            return max(0, (t - 1) * P), min(T, (t + 2) * P)

        def far_pieces(t):
            lo, hi = near_cols(t)
            return [(i + 1, c0, c1) for i, (c0, c1) in enumerate(((0, lo), (hi, T))) if c1 > c0]

        FAR = [sum(len(far_pieces(t)) for t in range(n)) for n in range(NT + 1)]

        def slots():
            return range(-SLOTS_BEFORE, UNITS + SLOTS_AFTER)

        def unit(u):
            return 0 <= u < UNITS

        def rel_count(u, kind):
            return 2 * (u - 1) + kind + 1

        def t_tiles(s, t):
            u, i = (s - 1, t - 3) if t >= 3 else (s - 2, t + 5)
            return (u, (2 * i, 2 * i + 1)) if unit(u) else (u, ())

        PV_AT = {5: (1, 0), 7: (1, 1), 1: (2, 2), 3: (2, 3)}
        FIN_AT = 4
        MT_AT = 1
        RAW_AT = {2: 0, 3: 1, 5: 2, 6: 3}
        EARLY = SLOTS_BEFORE
        SUB_AT = {0: (0, 1), 1: (2, 3), 2: (4, 5), 3: (6, 7)}

        block = ctx.enter_context(nc.Block())

        @block.sync
        def _(sp):
            sp.wait_ge(keep["parts_stored"][0], 16 * 6)
            for s in slots():
                u = s + 2
                if u == H:
                    sp.wait_ge(keep["parts_stored"][1], 16 * 6)
                if unit(u) and u > 0:
                    i = u % 2
                    if u >= 2:
                        sp.wait_ge(raw_done, 4 * (u - 1))
                    load_parts(sp, scr["qparts"], u, Q_ORDER, rawq[i], raw_in[i])
                    load_parts(sp, scr["kparts"], u, K_ORDER, rawk[i], raw_in[i])
                u = s + 1
                if u == 0:
                    sp.wait_ge(keep["far_stored"], 16)
                if unit(u):
                    i = u % 4
                    if u >= 4:
                        sp.wait_ge(t_done, 16 * (u - 3))
                    done = unit_in[i]
                    load_parts(sp, scr["qparts"], u, Q_ORDER, qst[i], done)
                    load_parts(sp, scr["kparts"], u, K_ORDER, kst[i], done)
                    for kind, dst in enumerate((qst[i][A_L:A_L + 3], qst[i][A_R:A_R + 3], kst[i][B_L:B_L + 3, 0],
                                                kst[i][B_R:B_R + 3, 1])):
                        row = ((u // H) * 4 + kind) * H + u % H
                        sp.dma_start(dst, bass.AP(scr["far"], row * 3 * T, [[T, 3], [1, T]])).then_inc(done, 16)
                u = s + 1
                if unit(u):
                    i = u % 2
                    ring = i * 2 * NT * P * 2 * S
                    if u >= 2:
                        sp.wait_ge(skew_in[i], 32 * (u // 2))
                    for kind in range(2):
                        if u == 0:
                            sp.wait_ge(rel_early, kind + 1)
                        else:
                            sp.wait_ge(rel_done, rel_count(u, kind))
                        dst = bass.AP(scr["ring"], ring + kind * NT * P * 2 * S, [[2 * S, P], [P * 2 * S, NT], [1, S]])
                        sp.dma_start(dst, raw[i][:, kind, :, :]).then_inc(skew_out[kind], 16)
                    if u >= 2:
                        sp.wait_ge(near_done, NT * (u - 1))
                        sp.wait_ge(nat_done, NT * (u - 1))
                    for kind in range(2):
                        sp.wait_ge(skew_out[kind], 16 * (u + 1))
                        src = bass.AP(scr["ring"], ring + kind * NT * P * 2 * S,
                                      [[2 * S - 1, P], [P * 2 * S, NT], [1, 2 * S]])
                        sp.dma_start(skew[i][:, kind, :, HALF:HALF + 2 * S], src).then_inc(skew_in[i], 16)

        @block.gpsimd
        def _(pool):
            for i in range(2):
                for c in (0, NEAR - HALF):
                    nc.gpsimd.memset(skew[i][:, :, :, c:c + HALF].rearrange("p a t c -> p (a t) c"), 0.0)\
                        .then_inc(zeroed, 1)
            for i in range(2):
                nc.gpsimd.memset(vst[i][:], 0.0).then_inc(v_zero, 1)
            pool.wait_ge(v_zero, 2)
            for i in range(2):
                nc.gpsimd.memset(vst[i][:, :, DK:DK + 1], 1.0).then_inc(v_ones, 1)

            def set_v(u):
                if u >= 2:
                    pool.wait_ge(pv_done, 4 * (u - 1))
                else:
                    pool.wait_ge(v_ones, 2)
                b, h = u // H, u % H
                nc.gpsimd.tensor_copy(vst[u % 2][:, :, 0:DK], keep["v"][:, b * NT:(b + 1) * NT, h * DK:(h + 1) * DK])\
                    .then_inc(v_set, 1)

            for s in slots():
                u = s + 2
                if not unit(u):
                    if unit(s):
                        set_v(s)
                    if s == UNITS:
                        nc.gpsimd.tensor_tensor(keep["xb"][:], keep["xb"][:],
                                                keep["bo_row"][:].unsqueeze(1).to_broadcast([P, B * NT, D]),
                                                ALU.add).then_inc(xb_done, 1)
                    continue
                r = raw[u % 2]
                for kind in range(2):
                    if kind == 1 and unit(s):
                        set_v(s)
                    if u == 0:
                        continue
                    pool.wait_ge(raw_copied, 4 * u + 2 * kind + 2)
                    if rel_count(u, kind) >= 2:
                        pool.wait_ge(rel_done, rel_count(u, kind) - 1)
                    mask, col = ((keep["cmask"], S - 1), (keep["pmask"], 0))[kind]
                    for t in range(NT):
                        last = nc.gpsimd.tensor_scalar(fix[:, t, :], mask[:], r[:, kind, t, col:col + 1], 0.0,
                                                       ALU.mult, ALU.add)
                    last.then_inc(fix_done, 1)
                    pool.wait_ge(fix_done, rel_count(u, kind))
                    nc.gpsimd.tensor_tensor(r[:, kind], r[:, kind], fix[:], ALU.subtract).then_inc(rel_done, 1)

        @block.tensor
        def _(pe):
            def natural(u, t):
                n = NT * u + t
                if n == 0:
                    pe.wait_ge(zeroed, 4)
                    pe.wait_ge(keep["rows_in"], 16 * 3)
                if t == 0:
                    pe.wait_ge(unit_in[u % 4], 16 * LOADS * (u // 4 + 1))
                    if u == 0:
                        for _ in range(WARM_UP):
                            nc.tensor.matmul(nat[0][:, 0:2 * S], identb[:], keep["cmask"][:].bitcast(BF16),
                                             start=True, stop=True)
                    pe.wait_ge(skew_in[u % 2], 32 * (u // 2 + 1))
                if n >= 2:
                    pe.wait_ge(near_done, n - 1)
                    pe.wait_ge(far_done, FAR[NT] * ((n - 2) // NT) + FAR[(n - 2) % NT + 1])
                o, q, k = nat[t % 2], qst[u % 4], kst[u % 4]
                pk = skew[u % 2][:, 1]
                edge = min(t * P + HALF, T)
                started = set()
                for side, c0, c1 in ((0, 0, edge), (1, edge, T)):
                    for b0 in (0, QH):
                        l, r = max(c0, b0), min(c1, b0 + QH)
                        if r > l:
                            nc.tensor.matmul(o[:, l:r], q[0:BASE_ROWS, t * P:(t + 1) * P], k[0:BASE_ROWS, side, l:r],
                                             start=b0 not in started, stop=False, skip_group_check=True)
                            started.add(b0)
                for kt, p1, x0 in ((t - 1, P, 2 * P), (t, P, P), (t + 1, HALF, 0)):
                    if 0 <= kt < NT:
                        c = kt * P
                        last = nc.tensor.matmul(o[:, c:c + p1], pk[0:p1, kt, x0:x0 + P], ident[0:p1, 0:p1],
                                                start=False, stop=True, is_transpose=True, skip_group_check=True)
                last.then_inc(nat_done, 1)

            def transposed(u, n):
                kt, half = n // 2, n % 2
                g = 16 * u + n
                if g >= 2:
                    pe.wait_ge(exp_done, g - 1)
                elif g == 0:
                    pe.wait_ge(raw_copied, 4 * EARLY)
                pe.wait_ge(sub_done, NT * u + min(NT, kt + 2))
                o, q, k = tps[n % 2], qst[u % 4], kst[u % 4]
                G = near[u % 2]
                h0, h1 = half * QH, (half + 1) * QH
                first, last = True, None
                n0, n1 = max(h0, (kt - 1) * P), min(h1, kt * P + P + HALF)
                for side, c0, c1 in ((1, h0, min(h1, (kt - 1) * P)), (0, max(h0, kt * P + P + HALF), h1)):
                    if c1 > c0:
                        last = nc.tensor.matmul(o[:, c0 - h0:c1 - h0], k[0:T_ROWS, side, kt * P:(kt + 1) * P],
                                                q[0:T_ROWS, c0:c1], start=first, stop=False, skip_group_check=True)
                        first = False
                if n1 > n0:
                    for qt, p1, x0 in ((kt - 1, P, 2 * P), (kt, P, P), (kt + 1, HALF, 0)):
                        c = qt * P
                        if h0 <= c < h1 and 0 <= qt < NT:
                            last = nc.tensor.matmul(o[:, c - h0:c - h0 + p1], G[0:p1, qt, x0:x0 + P],
                                                    ident[0:p1, 0:p1], start=first, stop=True,
                                                    is_transpose=True, skip_group_check=True)
                            first = False
                last.then_inc(t_done, 1)

            for s in slots():
                for t in range(NT):
                    if unit(s):
                        natural(s, t)
                    if t == MT_AT and unit(s - 1):
                        u = s - 1
                        pe.wait_ge(m_done, u + 1)
                        if unit(s + 1):
                            pe.wait_ge(raw_copied, 4 * (s + 2))
                        elif unit(s - 3):
                            pe.wait_ge(fin_done, s - 2)
                        nc.tensor.transpose(misc_b[0:2 * NT, 0:P], mparts[:].rearrange("p a t -> p (a t)"), identb[:])\
                            .then_inc(mT_done, 1)
                    u, tiles = t_tiles(s, t)
                    if tiles and tiles[0] == 0:
                        pe.wait_ge(m_rows, 16 * (u + 1))
                    for n in tiles:
                        transposed(u, n)
                    if t in PV_AT:
                        lag, g = PV_AT[t]
                        u = s - lag
                        if unit(u):
                            pe.wait_ge(exp_done, 16 * u + 4 * g + 4)
                            if g == 0:
                                pe.wait_ge(v_set, u + 1)
                            if g == 0 and u >= 1:
                                pe.wait_ge(pv_copied, u)
                            for j in range(4):
                                last = nc.tensor.matmul(pv[32 * j:32 * j + 32, :], vst[u % 2][:, 2 * g + j // 2, :],
                                                        probs[:, 4 * g + j, :], start=g == 0, stop=g == 3)
                            last.then_inc(pv_done, 1)
                    if t == FIN_AT and unit(s - 2):
                        u = s - 2
                        pe.wait_ge(pv_copied, u + 1)
                        if unit(s + 2):
                            pe.wait_ge(raw_copied, 4 * (s + 2) + 2)
                        elif unit(s - 1):
                            pe.wait_ge(m_copied, s)
                        else:
                            pe.wait_ge(fin_done, u)
                        for i in range(4):
                            last = nc.tensor.transpose(misc[:, i * P:(i + 1) * P], pvs[u % 2][:, i * P:(i + 1) * P], ident[:])
                        last.then_inc(finT_done, 1)
                    if t in RAW_AT and unit(s + 2):
                        u, r = s + 2, RAW_AT[t]
                        kind, half = r // 2, r % 2
                        if r == 0:
                            pe.wait_ge(raw_in[u % 2], 16 * RAW_LOADS * (u // 2 + 1))
                        bank = (misc, tps[0], tps[1], pv)[r] if u < EARLY else misc
                        if u < EARLY:
                            if u >= 1:
                                pe.wait_ge(raw_copied, 4 * (u - 1) + r + 1)
                        elif r == 0 and unit(s - 1):
                            pe.wait_ge(m_copied, s)
                        elif r == 2 and unit(s - 2):
                            pe.wait_ge(fin_done, s - 1)
                        else:
                            pe.wait_ge(raw_copied, 4 * u + r)
                        for i in range(4):
                            tt = 4 * half + i
                            lhs = (rawq, rawk)[kind][u % 2][:, tt * P:(tt + 1) * P]
                            last = nc.tensor.matmul(bank[:, i * P:(i + 1) * P], lhs, tab[:, kind, u % H, :],
                                                    start=True, stop=True)
                        last.then_inc(raw_done, 1)

        @block.scalar
        def _(act):
            for s in slots():
                for t in range(NT):
                    u, tiles = t_tiles(s, t)
                    for n in tiles:
                        g = 16 * u + n
                        act.wait_ge(t_done, g + 1)
                        if g == 0:
                            for b in range(B):
                                act.wait_ge(keep["parts_stored"][b], 16 * 6)
                            act.wait_ge(keep["far_stored"], 16)
                            act.wait_ge(keep["rows_in"], 16 * 3)
                        if u >= 1:
                            act.wait_ge(pv_done, 4 * (u - 1) + n // 4 + 1)
                        nc.scalar.activation(probs[:, n, :], tps[n % 2][:], ACT.Exp, scale=SCALE).then_inc(exp_done, 1)
                    if t == MT_AT and unit(s - 1):
                        u = s - 1
                        act.wait_ge(mT_done, u + 1)
                        if u >= 1:
                            act.wait_ge(m_rows, 16 * u)
                        nc.scalar.activation(mrow[:], misc_b[0:2 * NT, 0:P], ACT.Copy).then_inc(m_copied, 1)
                        act.wait_ge(m_copied, u + 1)
                        act.dma_start(qst[u % 4][M_ROW:T_ROWS, :].rearrange("r (t c) -> r t c", c=P), mrow[:])\
                            .then_inc(m_rows, 16)
                    if t == 3 and unit(s - 2):
                        u = s - 2
                        act.wait_ge(pv_done, 4 * u + 4)
                        if u >= 2:
                            act.wait_ge(finT_done, u - 1)
                        nc.scalar.activation(pvs[u % 2][:], pv[:], ACT.Copy).then_inc(pv_copied, 1)
                    if t in RAW_AT and unit(s + 2):
                        u, r = s + 2, RAW_AT[t]
                        kind, half = r // 2, r % 2
                        act.wait_ge(raw_done, 4 * u + r + 1)
                        if u >= 2:
                            act.wait_ge(skew_out[kind], 16 * (u - 1))
                        bank = (misc, tps[0], tps[1], pv)[r] if u < EARLY else misc
                        nc.scalar.activation(raw[u % 2][:, kind, 4 * half:4 * half + 4, :].rearrange("p t s -> p (t s)"),
                                             bank[:], ACT.Copy).then_inc(raw_copied, 1)

        @block.vector
        def _(v):
            nc.vector.memset(st[:], LOW).then_inc(m_step, 1)
            v.wait_ge(m_step, 1)
            steps = [1]
            for kind, (mask, col) in enumerate(((keep["cmask"], S - 1), (keep["pmask"], 0))):
                v.wait_ge(raw_copied, 2 * kind + 2)
                if kind == 1:
                    v.wait_ge(rel_early, 1)
                r, tmp = raw[0], near[1][:, :, 0:S]
                for t in range(NT):
                    last = nc.vector.tensor_scalar(tmp[:, t, :], mask[:], r[:, kind, t, col:col + 1], None, ALU.mult)
                last.then_inc(fix_early, 1)
                v.wait_ge(fix_early, kind + 1)
                nc.vector.tensor_tensor(r[:, kind], r[:, kind], tmp, ALU.subtract).then_inc(rel_early, 1)
            v.wait_ge(rel_early, 2)

            def m_wait(ins):
                steps[0] += 1
                ins.then_inc(m_step, 1)
                v.wait_ge(m_step, steps[0])

            def finish(u):
                v.wait_ge(finT_done, u + 1)
                nc.vector.tensor_reduce(csum[:].rearrange("p (h t) n -> p h t n", h=2),
                                        misc[:].rearrange("p (t r h n) -> p h t n r", t=4, r=2, h=2)[:, :, :, 0:DK + 1, :],
                                        AX_X, ALU.add).then_inc(fin_step, 1)
                v.wait_ge(fin_step, 2 * u + 1)
                nc.vector.reciprocal(crec[:], csum[:, :, DK]).then_inc(fin_step, 1)
                v.wait_ge(fin_step, 2 * u + 2)
                b, h = u // H, u % H
                nc.vector.tensor_tensor(keep["ctx"][:, b * NT:(b + 1) * NT, h * DK:(h + 1) * DK],
                                        csum[:, :, 0:DK], crec[:].unsqueeze(2).to_broadcast([P, NT, DK]),
                                        ALU.mult).then_inc(fin_done, 1)

            for s in slots():
                for t in range(NT):
                    if unit(s):
                        u = s
                        v.wait_ge(nat_done, NT * u + t + 1)
                        if t in (0, NT // 2) and u >= 2:
                            v.wait_ge(t_done, 16 * (u - 2) + (10 if t == 0 else 16))
                        if t == 0 and u == 0:
                            v.wait_ge(zeroed, 4)
                        if t == 0 and u >= 1:
                            v.wait_ge(m_step, steps[0])
                        lo, hi = near_cols(t)
                        x0 = lo - (t - 1) * P
                        x1 = x0 + hi - lo
                        nc.vector.tensor_tensor_reduce(out=near[u % 2][:, t, x0:x1], in0=nat[t % 2][:, lo:hi],
                                                       in1=skew[u % 2][:, 0, t, x0:x1], scale=1.0, scalar=LOW,
                                                       op0=ALU.add, op1=ALU.max,
                                                       accum_out=st[:, t, 0:1]).then_inc(near_done, 1)
                        for piece, c0, c1 in far_pieces(t):
                            nc.vector.reduce_max(st[:, t, piece:piece + 1], nat[t % 2][:, c0:c1], AX_X)\
                                .then_inc(far_done, 1)
                    if t == FIN_AT and unit(s - 2):
                        finish(s - 2)
                    if t in SUB_AT and unit(s - 1):
                        u = s - 1
                        if t == 0:
                            v.wait_ge(m_hat_done, u + 1)
                        for i in SUB_AT[t]:
                            lo, hi = near_cols(i)
                            g = near[u % 2][:, i, lo - (i - 1) * P:hi - (i - 1) * P]
                            nc.vector.tensor_scalar(g, g, m_hat[:, i:i + 1], None, ALU.add).then_inc(sub_done, 1)
                if unit(s):
                    v.wait_ge(near_done, NT * (s + 1))
                    v.wait_ge(far_done, FAR[NT] * (s + 1))
                    m_wait(nc.vector.tensor_reduce(mx[:], st[:], AX_X, ALU.max))
                    if s >= 1:
                        v.wait_ge(mT_done, s)
                        v.wait_ge(m_done, s)
                    m_wait(nc.vector.tensor_scalar(mparts[:, 0, :], mx[:], -1.0, None, ALU.mult))
                    nc.vector.scalar_tensor_tensor(out=mparts[:, 1, :], in0=mx[:], scalar=-1.0, in1=mparts[:, 0, :],
                                                   op0=ALU.mult, op1=ALU.subtract).then_inc(m_done, 1)
                    v.wait_ge(m_done, s + 1)
                    nc.vector.tensor_tensor(m_hat[:], mparts[:, 0, :], mparts[:, 1, :], ALU.add).then_inc(m_hat_done, 1)


def ffn(nc, a, keep, out):
    ctx = ExitStack()
    NTOK = B * NT
    GROUPS = NTOK // 4
    GATE = 5
    FIRST_DOWN = GATE + 8
    HS = FIRST_DOWN + 2
    with ctx:
        def sb(name, shape, dt=F32):
            return ctx.enter_context(nc.sbuf_tensor(name, shape, dt))

        def sem(name):
            return ctx.enter_context(nc.semaphore(name))

        ident = keep["ident"]
        w1 = sb("w1", [P, NE, HID])
        w3 = sb("w3", [P, NE, HID])
        w1_hi, w3_hi, w1_lo, w3_lo = (sb(n, [P, NE, HID], F32R) for n in ("w1_hi", "w3_hi", "w1_lo", "w3_lo"))
        x_hi, x_lo = (sb(n, [P, NTOK, P], F32R) for n in ("x_hi", "x_lo"))
        w2 = sb("w2", [P, NE, 2, D])
        b1 = sb("b1", [P, NE, 2])
        b3 = sb("b3", [P, NE, 2])
        wg = sb("wg", [P, NE])
        bg = sb("bg", [P, NE])
        wf = sb("wf", [P, D])
        bf = sb("bf", [P, D])
        b2rep = sb("b2rep", [P, D])
        tile_mask = sb("tile_mask", [P, NTOK])
        later = sb("later", [P, NE, NE])
        b2diag = sb("b2diag", [P, NTOK, D])
        xT = sb("xT2", [P, NTOK, P])
        y = sb("y", [P, NTOK, D])
        x1 = sb("x1", [P, NTOK, D])
        stats = sb("stats", [P, NTOK, 6])
        mv = sb("mv", [P, NTOK, 2])
        rstd = sb("rstd", [P, NTOK])
        logit = sb("logit", [P, NTOK, NE])
        gmax = sb("gmax", [P, NTOK])
        gate = sb("gate", [P, NTOK, NE])
        beats = sb("beats", [P, NTOK, NE, NE])
        ties = sb("ties", [P, NTOK, NE, NE])
        rank = sb("rank", [P, NTOK, NE])
        gw = sb("gw", [P, NTOK, NE])
        gwT = sb("gwT", [P, P])
        acc = keep["v"]
        h3b = [sb(f"h3b{i}", [P, QH]) for i in range(2)]
        hg = [sb(f"hg{i}", [P, QH]) for i in range(2)]
        hs = [keep["probs"][:, i] for i in range(HS)]
        epsc = sb("epsc", [P, 1])
        warm = sb("warm", [P, 1])
        ps = [ctx.enter_context(nc.psum_tensor(f"pf{i}", [P, QH], F32)) for i in range(8)]
        UP = 5
        DOWN, SIDE = (5, 6), 7

        w_first, w_rest, w_gate, b_up = sem("w_first"), sem("w_rest"), sem("w_gate"), sem("b_up")
        w2_in, b2_in, wf_in, mk = sem("w2_in"), sem("b2_in"), sem("wf_in"), sem("mk")
        ctxT, ctxT_c, proj, yadd = sem("ctxT"), sem("ctxT_c"), sem("proj"), sem("yadd")
        dv, rs, rt, rr, x1_done, x1_bf = (sem(n) for n in ("dv", "rs", "rt", "rr", "x1_done", "x1_bf"))
        w_hi_done, w_lo_done, x_lo_first, x_lo_rest = (sem(n) for n in ("w_hi_done", "w_lo_done", "x_lo_first", "x_lo_rest"))
        x1T, x1T_c, lg, lgc = sem("x1T"), sem("x1T_c"), sem("lg"), sem("lgc")
        glog, gexp, gwd, gwTd, gwTc, bd = (sem(n) for n in ("glog", "gexp", "gwd", "gwTd", "gwTc", "bd"))
        up, h3c, hgd, hsd, down, mixed = (sem(n) for n in ("up", "h3c", "hgd", "hsd", "down", "mixed"))
        mixT, mixT_c, fin, fy, rs2, rt2, rr2 = (sem(n) for n in ("mixT", "mixT_c", "fin", "fy", "rs2", "rt2", "rr2"))
        od_first, od_last, stored = sem("od_first"), sem("od_last"), sem("stored")
        block = ctx.enter_context(nc.Block())

        units = [(g, e, c) for g in range(GROUPS) for e in range(NE) for c in range(2)]
        PER_GROUP = 2 * NE
        LAST = len(units) - 1
        entries = []
        for g in range(GROUPS):
            for e in (0, 1, 2, 3, 4, NE, 5, 6, 7):
                n = PER_GROUP * g + (12 if e == NE else 2 * e + 3)
                entries.append((g, e, max(n, FIRST_DOWN + len(entries))))
        ENTRY = {(g, e): k for k, (g, e, _) in enumerate(entries)}
        NEXT_X1 = {0: 1, 2: 2, 3: 3}
        MIXT_AT, FINAL_AT, OUT_AT = PER_GROUP + 7, PER_GROUP + 9, PER_GROUP + 10
        ROOTS_AT = LAST - 4

        @block.sync
        def _(sp):
            w1v, w3v = (a["L0_ffn_" + n].rearrange("e d h -> d e h") for n in ("W1", "W3"))
            sp.dma_start(w3[:, 0:2], w3v[:, 0:2]).then_inc(w_first, 16)
            sp.dma_start(w1[:, 0:2], w1v[:, 0:2]).then_inc(w_first, 16)
            with nc.allow_non_contiguous_dma(reason="bias columns"):
                sp.dma_start(b3[:], a["L0_ffn_b3"].rearrange("e (c p) -> p e c", p=P)).then_inc(b_up, 16)
                sp.dma_start(b1[:], a["L0_ffn_b1"].rearrange("e (c p) -> p e c", p=P)).then_inc(b_up, 16)
            sp.dma_start(wg[:], a["L0_ffn_Wg"]).then_inc(w_gate, 16)
            sp.dma_start(bg[:], a["L0_ffn_bg"].partition_broadcast(P)).then_inc(w_gate, 16)
            sp.dma_start(w3[:, 2:NE], w3v[:, 2:NE]).then_inc(w_rest, 16)
            sp.dma_start(w1[:, 2:NE], w1v[:, 2:NE]).then_inc(w_rest, 16)
            sp.dma_start(w2[:], a["L0_ffn_W2"].rearrange("e (c p) o -> p e c o", p=P)).then_inc(w2_in, 16)
            for i in range(NTOK):
                sp.dma_start(b2rep[i * NE:(i + 1) * NE, :], a["L0_ffn_b2"]).then_inc(b2_in, 16)
            sp.dma_start(wf[:], a["L0_ffn_Wf"]).then_inc(wf_in, 16)
            sp.dma_start(bf[:], a["L0_ffn_bf"].partition_broadcast(P)).then_inc(wf_in, 16)
            ov = out.rearrange("b (t p) d -> p (b t) d", p=P)
            for g in range(GROUPS):
                if g < GROUPS - 1:
                    sp.wait_ge(od_first, 4 * g + 4)
                else:
                    sp.wait_ge(od_last, 4)
                sp.dma_start(ov[:, 4 * g:4 * g + 4, :], y[:, 4 * g:4 * g + 4, :]).then_inc(stored, 16)
            sp.wait_ge(stored, 16 * GROUPS)

        @block.gpsimd
        def _(pool):
            nc.gpsimd.memset(epsc[:], EPS).then_inc(mk, 1)
            head_mask(nc, pool, tile_mask, mk, 1)
            nc.gpsimd.memset(later[:], 1.0).then_inc(mk, 1)
            pool.wait_ge(mk, 5)
            nc.gpsimd.affine_select(out=later[:], in_=later[:], compare_op=ALU.is_ge, fill=0.0, base=-1,
                                    pattern=[[-1, NE], [1, NE]], channel_multiplier=0).then_inc(mk, 1)
            def low(c):
                pool.wait_ge(w_hi_done, 2 * c + 2)
                for lo, hi, w in ((w3_lo, w3_hi, w3), (w1_lo, w1_hi, w1)):
                    nc.gpsimd.tensor_tensor(lo[:, 2 * c:2 * c + 2], w[:, 2 * c:2 * c + 2], hi[:, 2 * c:2 * c + 2],
                                            ALU.subtract).then_inc(w_lo_done, 1)

            pool.wait_ge(w_first, 32)
            low(0)
            pool.wait_ge(w_rest, 32)
            for c in (1, 2, 3):
                low(c)
            for g in range(1, GROUPS):
                pool.wait_ge(x1T_c, g + 1)
                nc.gpsimd.tensor_tensor(x_lo[:, 4 * g:4 * g + 4, :], xT[:, 4 * g:4 * g + 4, :],
                                        x_hi[:, 4 * g:4 * g + 4, :], ALU.subtract).then_inc(x_lo_rest, 1)
            pool.wait_ge(b2_in, 16 * NTOK)
            for i in range(NTOK):
                nc.gpsimd.tensor_scalar(b2diag[:, i, :], b2rep[:], tile_mask[:, i:i + 1], 0.0, ALU.mult, ALU.add)\
                    .then_inc(bd, 1)
            pool.wait_ge(wf_in, 32)
            pool.wait_ge(x1_done, 4 * GROUPS)
            pool.wait_ge(x1T, GROUPS)
            nc.gpsimd.tensor_tensor(x1[:], x1[:], bf[:].unsqueeze(1).to_broadcast([P, NTOK, D]), ALU.add)\
                .then_inc(x1_bf, 1)
            for g in range(GROUPS - 1):
                pool.wait_ge(rr2, g + 1)
                for i in range(4 * g, 4 * g + 4):
                    nc.gpsimd.tensor_scalar(y[:, i, :], y[:, i, :], mv[:, i, 0:1], rstd[:, i:i + 1],
                                            ALU.subtract, ALU.mult).then_inc(od_first, 1)

        @block.tensor
        def _(pe):
            def transposes(g, src, bank, done):
                for i in range(4):
                    last = nc.tensor.transpose(ps[bank][:, i * P:(i + 1) * P], src[:, 4 * g + i, :], ident[:])
                last.then_inc(done, 1)

            def project(g):
                pe.wait_ge(ctxT_c, g + 1)
                for i in range(4):
                    last = nc.tensor.matmul(ps[4 + g][:, i * P:(i + 1) * P], xT[:, 4 * g + i, :], keep["woT"][:],
                                            start=True, stop=True)
                last.then_inc(proj, 1)

            def down_entry(k):
                g, e, _ = entries[k]
                if k >= 2:
                    pe.wait_ge(mixed, 4 * (k - 1))
                o = ps[DOWN[k % 2]]
                if e == NE:
                    last = nc.tensor.matmul(o[:], gwT[:], b2diag[:, 4 * g:4 * g + 4, :], start=True, stop=True)
                else:
                    m = PER_GROUP * g + 2 * e
                    pe.wait_ge(hsd, m + 2)
                    for i in range(4):
                        for c in range(2):
                            last = nc.tensor.matmul(o[:, i * P:(i + 1) * P], hs[(m + c) % HS][:, i * P:(i + 1) * P],
                                                    w2[:, e, c, :], start=c == 0, stop=c == 1)
                last.then_inc(down, 1)

            def mixed_back(g, bank):
                pe.wait_ge(mixed, 4 * (ENTRY[g, NE - 1] + 1))
                transposes(g, acc, bank, mixT)

            def final(g, bank):
                pe.wait_ge(mixT_c, g + 1)
                for i in range(4):
                    last = nc.tensor.matmul(ps[bank][:, i * P:(i + 1) * P], xT[:, 4 * g + i, :], wf[:],
                                            start=True, stop=True)
                last.then_inc(fin, 1)

            transposes(0, keep["ctx"], 0, ctxT)
            transposes(1, keep["ctx"], 1, ctxT)
            project(0)
            transposes(2, keep["ctx"], 2, ctxT)
            project(1)
            transposes(3, keep["ctx"], 3, ctxT)
            project(2)
            project(3)
            pe.wait_ge(x1_done, 4)
            transposes(0, x1, 3, x1T)
            pe.wait_ge(x1T_c, 1)
            k = 0
            for n, (g, e, c) in enumerate(units):
                if g == 0 and e % 2 == 0 and c == 0:
                    pe.wait_ge(w_hi_done, e + 2)
                    pe.wait_ge(w_lo_done, e + 2)
                if n % PER_GROUP == 0 and 0 < g:
                    pe.wait_ge(x1T_c, g + 1)
                    pe.wait_ge(x_lo_rest, g)
                x_h, x_l = x_hi[:, 4 * g:4 * g + 4, :], x_lo[:, 4 * g:4 * g + 4, :]
                for j, w_h, w_l in ((2 * n, w3_hi, w3_lo), (2 * n + 1, w1_hi, w1_lo)):
                    if j >= UP:
                        if (j - UP) % 2 == 0:
                            pe.wait_ge(h3c, (j - UP) // 2 + 1)
                        else:
                            pe.wait_ge(hgd, (j - UP) // 2 + 1)
                    o, cols = ps[j % UP], slice(c * P, (c + 1) * P)
                    nc.tensor.matmul(o[:], w_h[:, e, cols], x_h, start=True, stop=False)
                    nc.tensor.matmul(o[:], w_l[:, e, cols], x_h, start=False, stop=False)
                    if n == 0:
                        pe.wait_ge(x_lo_first, 1)
                    nc.tensor.matmul(o[:], w_h[:, e, cols], x_l, start=False, stop=True).then_inc(up, 1)
                if n in NEXT_X1:
                    m = NEXT_X1[n]
                    pe.wait_ge(x1_done, 4 * m + 4)
                    if m == 1:
                        pe.wait_ge(yadd, 4)
                    else:
                        pe.wait_ge(x1T_c, m)
                    transposes(m, x1, SIDE, x1T)
                if n == GATE - 1:
                    pe.wait_ge(w_gate, 32)
                    pe.wait_ge(x1T_c, GROUPS)
                    for i in range(NTOK):
                        last = nc.tensor.matmul(ps[SIDE][:, i * NE:(i + 1) * NE], xT[:, i, :], wg[:], start=True, stop=True)
                    last.then_inc(lg, 1)
                    pe.wait_ge(w2_in, 16)
                if n == FIRST_DOWN:
                    pe.wait_ge(gwd, 1)
                    nc.tensor.transpose(ps[SIDE][:, 0:P], gw[:].rearrange("p t e -> p (t e)"), ident[:]).then_inc(gwTd, 1)
                if n == entries[ENTRY[0, NE]][2]:
                    pe.wait_ge(gwTc, 1)
                    pe.wait_ge(bd, NTOK)
                while k < len(entries) and entries[k][2] == n:
                    down_entry(k)
                    k += 1
                if n > MIXT_AT - 1 and n % PER_GROUP == MIXT_AT % PER_GROUP:
                    mg = n // PER_GROUP - 1
                    if mg >= 1:
                        pe.wait_ge(fy, mg)
                    else:
                        pe.wait_ge(wf_in, 32)
                    mixed_back(mg, SIDE)
                if n > FINAL_AT - 1 and n % PER_GROUP == FINAL_AT % PER_GROUP:
                    final(n // PER_GROUP - 1, SIDE)
            down_entry(len(entries) - 1)
            mixed_back(GROUPS - 1, 0)
            final(GROUPS - 1, 1)

        @block.scalar
        def _(act):
            def copy_group(g, bank, done):
                nc.scalar.activation(xT[:, 4 * g:4 * g + 4, :].rearrange("p t d -> p (t d)"), ps[bank][:], ACT.Copy)\
                    .then_inc(done, 1)

            def copy_x1(g, bank):
                act.wait_ge(x1T, g + 1)
                nc.scalar.activation(x_hi[:, 4 * g:4 * g + 4, :].rearrange("p t d -> p (t d)"), ps[bank][:], ACT.Copy)
                copy_group(g, bank, x1T_c)

            def high(c):
                if c == 0:
                    act.wait_ge(w_first, 32)
                elif c == 1:
                    act.wait_ge(w_rest, 32)
                for hi, w in ((w3_hi, w3), (w1_hi, w1)):
                    nc.scalar.activation(hi[:, 2 * c:2 * c + 2], w[:, 2 * c:2 * c + 2], ACT.Copy).then_inc(w_hi_done, 1)

            def root(g, ready, done):
                act.wait_ge(ready, g + 1)
                nc.scalar.activation(rstd[:, 4 * g:4 * g + 4], mv[:, 4 * g:4 * g + 4, 1], ACT.Sqrt, bias=epsc[:])\
                    .then_inc(done, 1)

            def silu(m):
                act.wait_ge(hgd, m + 1)
                if m >= HS:
                    g, e, _ = units[m - HS]
                    act.wait_ge(down, ENTRY[g, e] + 1)
                nc.scalar.activation(hs[m % HS][:], hg[m % 2][:], ACT.Silu).then_inc(hsd, 1)

            act.wait_ge(mk, 1)
            nc.scalar.activation(warm[:], epsc[:], ACT.Sqrt)
            for g in range(GROUPS):
                act.wait_ge(ctxT, g + 1)
                copy_group(g, g, ctxT_c)
            high(0)
            root(0, rs, rt)
            root(1, rs, rt)
            act.wait_ge(proj, 1)
            copy_x1(0, 3)
            root(2, rs, rt)
            root(3, rs, rt)
            act.wait_ge(proj, GROUPS)
            act.wait_ge(b_up, 32)
            for n, (g, e, c) in enumerate(units):
                act.wait_ge(up, 2 * n + 1)
                if n >= 2:
                    act.wait_ge(hgd, n - 1)
                nc.scalar.activation(h3b[n % 2][:], ps[2 * n % UP][:], ACT.Identity, bias=b3[:, e, c:c + 1])\
                    .then_inc(h3c, 1)
                if n in NEXT_X1:
                    copy_x1(NEXT_X1[n], SIDE)
                if n in (0, 1, 2):
                    high(n + 1)
                if n >= 1:
                    silu(n - 1)
                if n == GATE + 1:
                    act.wait_ge(glog, 1)
                    nc.scalar.activation(gate[:], logit[:], ACT.Exp).then_inc(gexp, 1)
                if n == FIRST_DOWN:
                    act.wait_ge(gwTd, 1)
                    nc.scalar.activation(gwT[:], ps[SIDE][:, 0:P], ACT.Copy).then_inc(gwTc, 1)
                if n > MIXT_AT - 1 and n % PER_GROUP == MIXT_AT % PER_GROUP:
                    mg = n // PER_GROUP - 1
                    act.wait_ge(mixT, mg + 1)
                    copy_group(mg, SIDE, mixT_c)
                if n == ROOTS_AT:
                    for g in range(GROUPS - 1):
                        root(g, rs2, rt2)
            silu(LAST)
            nc.scalar.activation(warm[:], epsc[:], ACT.Sqrt)
            act.wait_ge(mixT, GROUPS)
            copy_group(GROUPS - 1, 0, mixT_c)
            root(GROUPS - 1, rs2, rt2)

        @block.vector
        def _(v):
            count = [0]

            def step(ins):
                count[0] += 1
                ins.then_inc(dv, 1)
                v.wait_ge(dv, count[0])

            def norm_stats(g, done):
                for i in range(4 * g, 4 * g + 4):
                    last = nc.vector.bn_stats(stats[:, i, :], y[:, i, :])
                step(last)
                for i in range(4 * g, 4 * g + 4):
                    last = nc.vector.bn_aggr(mv[:, i, :], stats[:, i, :])
                last.then_inc(done, 1)

            def one_over(g, roots, done):
                v.wait_ge(roots, g + 1)
                nc.vector.reciprocal(rstd[:, 4 * g:4 * g + 4], rstd[:, 4 * g:4 * g + 4]).then_inc(done, 1)

            def residual(g):
                v.wait_ge(proj, g + 1)
                nc.vector.tensor_tensor(y[:, 4 * g:4 * g + 4, :].rearrange("p t d -> p (t d)"), ps[4 + g][:],
                                        keep["xb"][:, 4 * g:4 * g + 4, :].rearrange("p t d -> p (t d)"),
                                        ALU.add).then_inc(yadd, 1)
                v.wait_ge(yadd, g + 1)
                norm_stats(g, rs)

            def mix(k):
                g, e, _ = entries[k]
                v.wait_ge(down, k + 1)
                if e > 0:
                    v.wait_ge(mixed, 4 * k)
                o = ps[DOWN[k % 2]]
                if e == NE:
                    whole = acc[:, 4 * g:4 * g + 4, :].rearrange("p t d -> p (t d)")
                    nc.vector.tensor_tensor(whole, o[:], whole, ALU.add).then_inc(mixed, 4)
                    return
                for i in range(4):
                    tt = 4 * g + i
                    if e == 0:
                        nc.vector.tensor_scalar(acc[:, tt, :], o[:, i * P:(i + 1) * P], gw[:, tt, e:e + 1], None,
                                                ALU.mult).then_inc(mixed, 1)
                    else:
                        nc.vector.scalar_tensor_tensor(out=acc[:, tt, :], in0=o[:, i * P:(i + 1) * P],
                                                       scalar=gw[:, tt, e:e + 1], in1=acc[:, tt, :],
                                                       op0=ALU.mult, op1=ALU.add).then_inc(mixed, 1)

            def output_stats(g, bank):
                v.wait_ge(fin, g + 1)
                if g == 0:
                    v.wait_ge(x1_bf, 1)
                nc.vector.tensor_tensor(y[:, 4 * g:4 * g + 4, :].rearrange("p t d -> p (t d)"), ps[bank][:],
                                        x1[:, 4 * g:4 * g + 4, :].rearrange("p t d -> p (t d)"), ALU.add).then_inc(fy, 1)
                v.wait_ge(fy, g + 1)
                norm_stats(g, rs2)

            def first_norm(g):
                v.wait_ge(rr, g + 1)
                for i in range(4 * g, 4 * g + 4):
                    nc.vector.tensor_scalar(x1[:, i, :], y[:, i, :], mv[:, i, 0:1], rstd[:, i:i + 1],
                                            ALU.subtract, ALU.mult).then_inc(x1_done, 1)

            residual(0)
            residual(1)
            one_over(0, rt, rr)
            first_norm(0)
            one_over(1, rt, rr)
            first_norm(1)
            v.wait_ge(x1T_c, 1)
            nc.vector.tensor_tensor(x_lo[:, 0:4, :], xT[:, 0:4, :], x_hi[:, 0:4, :], ALU.subtract).then_inc(x_lo_first, 1)
            residual(2)
            one_over(2, rt, rr)
            residual(3)
            one_over(3, rt, rr)
            fl = lambda x: x[:].rearrange("p t e f -> p t (e f)")
            k = 0
            for n, (g, e, c) in enumerate(units):
                v.wait_ge(h3c, n + 1)
                v.wait_ge(up, 2 * n + 2)
                if n >= 2:
                    v.wait_ge(hsd, n - 1)
                nc.vector.scalar_tensor_tensor(out=hg[n % 2][:], in0=ps[(2 * n + 1) % UP][:], scalar=b1[:, e, c:c + 1],
                                               in1=h3b[n % 2][:], op0=ALU.add, op1=ALU.mult).then_inc(hgd, 1)
                if n in (0, 1):
                    first_norm(2 + n)
                if n == GATE:
                    v.wait_ge(lg, 1)
                    nc.vector.tensor_tensor(logit[:], ps[SIDE][:, 0:NTOK * NE].rearrange("p (t e) -> p t e", e=NE),
                                            bg[:].unsqueeze(1).to_broadcast([P, NTOK, NE]), ALU.add).then_inc(lgc, 1)
                    v.wait_ge(lgc, 1)
                    step(nc.vector.tensor_reduce(gmax[:], logit[:], AX_X, ALU.max))
                    nc.vector.tensor_tensor(logit[:], logit[:], gmax[:].unsqueeze(2).to_broadcast([P, NTOK, NE]),
                                            ALU.subtract).then_inc(glog, 1)
                if n == GATE + 1:
                    v.wait_ge(gexp, 1)
                    step(nc.vector.tensor_reduce(gmax[:], gate[:], AX_X, ALU.add))
                    step(nc.vector.reciprocal(gmax[:], gmax[:]))
                    step(nc.vector.tensor_tensor(gate[:], gate[:], gmax[:].unsqueeze(2).to_broadcast([P, NTOK, NE]),
                                                 ALU.mult))
                    v.wait_ge(mk, 6)
                    mine = gate[:].unsqueeze(3).to_broadcast([P, NTOK, NE, NE])
                    other = gate[:].unsqueeze(2).to_broadcast([P, NTOK, NE, NE])
                    nc.vector.tensor_tensor(beats[:], other, mine, ALU.is_gt)
                if n == GATE + 2:
                    step(nc.vector.tensor_tensor(ties[:], other, mine, ALU.is_equal))
                    lat = later[:].rearrange("p e f -> p (e f)").unsqueeze(1).to_broadcast([P, NTOK, NE * NE])
                    step(nc.vector.tensor_tensor(fl(ties), fl(ties), lat, ALU.mult))
                if n == GATE + 3:
                    step(nc.vector.tensor_tensor(fl(beats), fl(beats), fl(ties), ALU.add))
                if n == GATE + 4:
                    step(nc.vector.tensor_reduce(rank[:], beats[:], AX_X, ALU.add))
                    step(nc.vector.tensor_scalar(rank[:], rank[:], 1.5, None, ALU.is_lt))
                    nc.vector.tensor_tensor(gw[:], gate[:], rank[:], ALU.mult).then_inc(gwd, 1)
                    v.wait_ge(gwd, 1)
                while k < len(entries) and entries[k][2] + 1 == n:
                    mix(k)
                    k += 1
                if n > OUT_AT - 1 and n % PER_GROUP == OUT_AT % PER_GROUP:
                    output_stats(n // PER_GROUP - 1, SIDE)
                if n == ROOTS_AT + 1:
                    for og in range(GROUPS - 1):
                        one_over(og, rt2, rr2)
            for rest in range(k, len(entries)):
                mix(rest)
            output_stats(GROUPS - 1, 1)
            one_over(GROUPS - 1, rt2, rr2)
            v.wait_ge(rr2, GROUPS)
            for i in range(4 * GROUPS - 4, 4 * GROUPS):
                nc.vector.tensor_scalar(y[:, i, :], y[:, i, :], mv[:, i, 0:1], rstd[:, i:i + 1],
                                        ALU.subtract, ALU.mult).then_inc(od_last, 1)


NAMES = ["L0_attn_x", "L0_attn_Wq", "L0_attn_bq", "L0_attn_Wk", "L0_attn_bk", "L0_attn_Wv", "L0_attn_bv",
         "L0_attn_Wo", "L0_attn_bo", "L0_attn_Wpk", "L0_attn_bpk", "L0_attn_Wpq", "L0_attn_bpq", "L0_attn_rel_emb",
         "L0_ffn_W1", "L0_ffn_b1", "L0_ffn_W3", "L0_ffn_b3", "L0_ffn_W2", "L0_ffn_b2", "L0_ffn_Wg", "L0_ffn_bg",
         "L0_ffn_Wf", "L0_ffn_bf"]


def build(nc, a, out):
    scr = {
        "qparts": nc.dram_tensor("qparts", [UNITS, 3, DK, T], BF16, kind="Internal"),
        "kparts": nc.dram_tensor("kparts", [UNITS, 3, DK, T], BF16, kind="Internal"),
        "far": nc.dram_tensor("far_rows", [P, 3, T], BF16, kind="Internal"),
        "tab": nc.dram_tensor("pos_parts", [3, P, 2 * S], BF16, kind="Internal"),
        "ring": nc.dram_tensor("skew_ring", [2, 2, NT * P, 2 * S], F32, kind="Internal"),
    }
    ctx = ExitStack()
    with ctx:
        keep = {}
        for name, shape, dt in (("ident", [P, P], F32), ("identb", [P, P], BF16), ("cmask", [P, S], F32),
                                ("pmask", [P, S], F32), ("woT", [P, P], F32), ("bo_row", [P, D], F32),
                                ("xb", [P, B * NT, D], F32),
                                ("v", [P, B * NT, D], F32),
                                ("ctx", [P, B * NT, D], F32)):
            keep[name] = ctx.enter_context(nc.sbuf_tensor(name, shape, dt))
        keep["probs"] = ctx.enter_context(nc.sbuf_tensor("probs", [P, 16, QH], F32))
        stacks = ExitStack()
        with stacks:
            keep["tab"] = stacks.enter_context(nc.sbuf_tensor("tab", [ROWS, 2, H, S], BF16))
            keep["qst"] = stacks.enter_context(nc.sbuf_tensor("qst", [T_ROWS, 4, T], BF16))
            keep["kst"] = stacks.enter_context(nc.sbuf_tensor("kst", [T_ROWS, 4, 2, T], BF16))
            for name in ("rawq", "rawk"):
                keep[name] = [stacks.enter_context(nc.sbuf_tensor(f"{name}{i}", [ROWS, T], BF16)) for i in range(2)]
            keep["parts_stored"] = [stacks.enter_context(nc.semaphore(f"parts_stored{b}")) for b in range(B)]
            keep["far_stored"] = stacks.enter_context(nc.semaphore("far_stored"))
            keep["rows_in"] = stacks.enter_context(nc.semaphore("rows_in"))
            keep["raw_in"] = [stacks.enter_context(nc.semaphore(f"raw_in{i}")) for i in range(2)]
            prologue(nc, a, scr, keep)
            attention(nc, a, scr, keep)
        ffn(nc, a, keep, out)


def kernel(**inputs):
    import numpy as np
    import concourse.bacc as bacc
    from concourse.bass_utils import run_bass_kernel_spmd

    nc = bacc.Bacc("TRN2", target_bir_lowering=False, num_devices=1)
    arrays, args = {}, {}
    for name in NAMES:
        x = np.ascontiguousarray(inputs[name])
        arrays[f"in_{name}"] = x
        args[name] = nc.dram_tensor(f"in_{name}", x.shape, mybir.dt.from_np(x.dtype), kind="ExternalInput").ap()
    out = nc.dram_tensor("out_0_dram", (B, T, D), F32, kind="ExternalOutput").ap()
    build(nc, args, out)
    return run_bass_kernel_spmd(nc, [arrays], core_ids=[0]).results[0]["out_0_dram"]
```
